# Optimizing a Trainium2 kernel written in Bass

```python
import numpy as np
import jax
import jax.numpy as jnp

def _softmax(x, axis=-1):
    return jax.nn.softmax(x, axis=axis)

def _gelu(x):
    return jax.nn.gelu(x, approximate=True)

def _silu(x):
    return jax.nn.silu(x)

def _sigmoid(x):
    return jax.nn.sigmoid(x)

def _layernorm(x, axis=-1, eps=1e-05):
    m = jnp.mean(x, axis=axis, keepdims=True)
    v = jnp.var(x, axis=axis, keepdims=True)
    return (x - m) / jnp.sqrt(v + eps)

def _scatter_add(tgt, idx, src, axis=0):
    return tgt.at[idx].add(src)

def _segment_sum(src, seg, n):
    return jax.ops.segment_sum(src, seg, n)
kernel_name = 'mk_prb_d1_jaxref_r4_6976b7'

def setup_inputs(seed: int=0):
    np.random.seed(seed)
    _w = jnp.asarray

    def _L0_attn_setup():
        import jax, jax.numpy as jnp
        import numpy as np
        from jax import lax
        B, T, D = (2, 256, 256)
        H, DK, DV, K = (8, 128, 64, 4)
        EPS = 1e-05

        def short_conv(x, w):
            Kc = w.shape[-1]
            xp = jnp.pad(x, ((0, 0), (Kc - 1, 0), (0, 0))).transpose(0, 2, 1)
            y = lax.conv_general_dilated(xp, w[:, None, :], (1,), 'VALID', feature_group_count=w.shape[0])
            return jax.nn.silu(y.transpose(0, 2, 1))

        def l2norm(x):
            return x * lax.rsqrt(jnp.sum(x * x, axis=-1, keepdims=True) + 1e-06)

        def gated_delta_rule(q, k, v, g, beta):
            scale = q.shape[-1] ** (-0.5)
            q = l2norm(q) * scale
            k = l2norm(k)
            qT, kT, vT = (a.transpose(1, 0, 2, 3) for a in (q, k, v))
            gT, bT = (g.transpose(1, 0, 2), beta.transpose(1, 0, 2))
            S0 = jnp.zeros((q.shape[0], q.shape[2], q.shape[3], v.shape[3]), q.dtype)

            def step(S, inp):
                q_t, k_t, v_t, g_t, b_t = inp
                S = S * jnp.exp(g_t)[..., None, None]
                u = (v_t - jnp.einsum('bhk,bhkv->bhv', k_t, S)) * b_t[..., None]
                S = S + jnp.einsum('bhk,bhv->bhkv', k_t, u)
                o_t = jnp.einsum('bhk,bhkv->bhv', q_t, S)
                return (S, o_t)
            _, oT = lax.scan(step, S0, (qT, kT, vT, gT, bT))
            return oT.transpose(1, 0, 2, 3)
        key = jax.random.key(seed)
        ks = jax.random.split(key, 16)
        s = 0.02
        dt = jax.random.uniform(ks[10], (H,), minval=0.001, maxval=0.1)
        return {'x': jax.random.normal(ks[0], (B, T, D), jnp.float32), 'Wq': jax.random.normal(ks[1], (D, H * DK), jnp.float32) * s, 'Wk': jax.random.normal(ks[2], (D, H * DK), jnp.float32) * s, 'Wv': jax.random.normal(ks[3], (D, H * DV), jnp.float32) * s, 'conv_q': jax.random.normal(ks[4], (H * DK, K), jnp.float32) * 0.2, 'conv_k': jax.random.normal(ks[5], (H * DK, K), jnp.float32) * 0.2, 'conv_v': jax.random.normal(ks[6], (H * DV, K), jnp.float32) * 0.2, 'Wb': jax.random.normal(ks[7], (D, H), jnp.float32) * s, 'Wa': jax.random.normal(ks[8], (D, H), jnp.float32) * s, 'A_log': jnp.log(jax.random.uniform(ks[9], (H,), minval=1.0, maxval=16.0)), 'dt_bias': jnp.log(jnp.expm1(dt)), 'Wg': jax.random.normal(ks[11], (D, H * DV), jnp.float32) * s, 'norm_w': jnp.ones((DV,), jnp.float32), 'Wo': jax.random.normal(ks[12], (H * DV, D), jnp.float32) * s}
    _L0_attn_in = _L0_attn_setup()

    def _L0_ffn_setup():
        import jax, jax.numpy as jnp
        import numpy as np
        E = 8
        D = 256
        H = 512
        TOP_K = 2
        key = jax.random.key(seed)
        k_x, k_g, k_w1, k_w2 = jax.random.split(key, 4)
        B, S = (4, 512)
        inp = {'input': jax.random.normal(k_x, (B, S, D), dtype=jnp.float32), 'Wg': jax.random.normal(k_g, (D, E), dtype=jnp.float32) * 0.02, 'W1': jax.random.normal(k_w1, (E, D, H), dtype=jnp.float32) * 0.02, 'b1': jnp.zeros((E, H), dtype=jnp.float32), 'W2': jax.random.normal(k_w2, (E, H, D), dtype=jnp.float32) * 0.02, 'b2': jnp.zeros((E, D), dtype=jnp.float32)}
        return inp
    _L0_ffn_in = _L0_ffn_setup()
    _d = {'L0_attn_x': _L0_attn_in['x'], 'L0_attn_Wq': _L0_attn_in['Wq'], 'L0_attn_Wk': _L0_attn_in['Wk'], 'L0_attn_Wv': _L0_attn_in['Wv'], 'L0_attn_conv_q': _L0_attn_in['conv_q'], 'L0_attn_conv_k': _L0_attn_in['conv_k'], 'L0_attn_conv_v': _L0_attn_in['conv_v'], 'L0_attn_Wb': _L0_attn_in['Wb'], 'L0_attn_Wa': _L0_attn_in['Wa'], 'L0_attn_A_log': _L0_attn_in['A_log'], 'L0_attn_dt_bias': _L0_attn_in['dt_bias'], 'L0_attn_Wg': _L0_attn_in['Wg'], 'L0_attn_norm_w': _L0_attn_in['norm_w'], 'L0_attn_Wo': _L0_attn_in['Wo'], 'L0_ffn_Wg': _L0_ffn_in['Wg'], 'L0_ffn_W1': _L0_ffn_in['W1'], 'L0_ffn_b1': _L0_ffn_in['b1'], 'L0_ffn_W2': _L0_ffn_in['W2'], 'L0_ffn_b2': _L0_ffn_in['b2']}
    _x0 = _d['L0_attn_x']
    _d['L0_attn_x'] = jax.random.normal(jax.random.fold_in(jax.random.key(seed), 1), (4, 2048, 256), dtype=_x0.dtype)
    del _x0
    return _d

def reference(L0_attn_x, L0_attn_Wq, L0_attn_Wk, L0_attn_Wv, L0_attn_conv_q, L0_attn_conv_k, L0_attn_conv_v, L0_attn_Wb, L0_attn_Wa, L0_attn_A_log, L0_attn_dt_bias, L0_attn_Wg, L0_attn_norm_w, L0_attn_Wo, L0_ffn_Wg, L0_ffn_W1, L0_ffn_b1, L0_ffn_W2, L0_ffn_b2):

    def _L0_attn_ref(x, Wq, Wk, Wv, conv_q, conv_k, conv_v, Wb, Wa, A_log, dt_bias, Wg, norm_w, Wo):
        import jax, jax.numpy as jnp
        import numpy as np
        from jax import lax
        B, T, D = (2, 256, 256)
        H, DK, DV, K = (8, 128, 64, 4)
        EPS = 1e-05

        def short_conv(x, w):
            Kc = w.shape[-1]
            xp = jnp.pad(x, ((0, 0), (Kc - 1, 0), (0, 0))).transpose(0, 2, 1)
            y = lax.conv_general_dilated(xp, w[:, None, :], (1,), 'VALID', feature_group_count=w.shape[0])
            return jax.nn.silu(y.transpose(0, 2, 1))

        def l2norm(x):
            return x * lax.rsqrt(jnp.sum(x * x, axis=-1, keepdims=True) + 1e-06)

        def gated_delta_rule(q, k, v, g, beta):
            scale = q.shape[-1] ** (-0.5)
            q = l2norm(q) * scale
            k = l2norm(k)
            qT, kT, vT = (a.transpose(1, 0, 2, 3) for a in (q, k, v))
            gT, bT = (g.transpose(1, 0, 2), beta.transpose(1, 0, 2))
            S0 = jnp.zeros((q.shape[0], q.shape[2], q.shape[3], v.shape[3]), q.dtype)

            def step(S, inp):
                q_t, k_t, v_t, g_t, b_t = inp
                S = S * jnp.exp(g_t)[..., None, None]
                u = (v_t - jnp.einsum('bhk,bhkv->bhv', k_t, S)) * b_t[..., None]
                S = S + jnp.einsum('bhk,bhv->bhkv', k_t, u)
                o_t = jnp.einsum('bhk,bhkv->bhv', q_t, S)
                return (S, o_t)
            _, oT = lax.scan(step, S0, (qT, kT, vT, gT, bT))
            return oT.transpose(1, 0, 2, 3)
        Bx, Tx = (x.shape[0], x.shape[1])
        q = short_conv(x @ Wq, conv_q).reshape(Bx, Tx, H, DK)
        k = short_conv(x @ Wk, conv_k).reshape(Bx, Tx, H, DK)
        v = short_conv(x @ Wv, conv_v).reshape(Bx, Tx, H, DV)
        beta = jax.nn.sigmoid(x @ Wb)
        g = -jnp.exp(A_log) * jax.nn.softplus(x @ Wa + dt_bias)
        o = gated_delta_rule(q, k, v, g, beta)
        gv = (x @ Wg).reshape(Bx, Tx, H, DV)
        o = o * lax.rsqrt(jnp.mean(o * o, axis=-1, keepdims=True) + EPS) * norm_w
        o = o * jax.nn.silu(gv)
        return o.reshape(Bx, Tx, H * DV) @ Wo

    def _L0_ffn_ref(input, Wg, W1, b1, W2, b2):
        import jax, jax.numpy as jnp
        import numpy as np
        E = 8
        D = 256
        H = 512
        TOP_K = 2
        logits = jnp.einsum('bsd,de->bse', input, Wg)
        probs = jax.nn.softmax(logits, axis=-1)
        top_vals, top_idx = jax.lax.top_k(probs, TOP_K)
        top_vals = top_vals / jnp.sum(top_vals, axis=-1, keepdims=True)
        onehot = jax.nn.one_hot(top_idx, E, dtype=input.dtype)
        mask = jnp.sum(onehot, axis=2)
        scores = jnp.sum(onehot * top_vals[..., None], axis=2)
        xm = input[None] * jnp.moveaxis(mask, -1, 0)[..., None]
        h = jnp.einsum('ebsd,edh->ebsh', xm, W1) + b1[:, None, None, :]
        h = jax.nn.relu(h)
        y = jnp.einsum('ebsh,ehd->ebsd', h, W2) + b2[:, None, None, :]
        out = jnp.sum(y * jnp.moveaxis(scores, -1, 0)[..., None], axis=0)
        return out
    x = L0_attn_x
    xn = _layernorm(x, axis=-1)
    x = x + _L0_attn_ref(xn, L0_attn_Wq, L0_attn_Wk, L0_attn_Wv, L0_attn_conv_q, L0_attn_conv_k, L0_attn_conv_v, L0_attn_Wb, L0_attn_Wa, L0_attn_A_log, L0_attn_dt_bias, L0_attn_Wg, L0_attn_norm_w, L0_attn_Wo) + _L0_ffn_ref(xn, L0_ffn_Wg, L0_ffn_W1, L0_ffn_b1, L0_ffn_W2, L0_ffn_b2)
    return x

_drawn_inputs = setup_inputs


def setup_inputs(seed=0):
    import zlib

    import numpy as np

    out = dict(_drawn_inputs(seed))
    spreads = {'L0_attn_norm_w': (1.0, 0.6), 'L0_ffn_b1': (0.0, 1.811), 'L0_ffn_b2': (0.0, 0.544)}
    factors = {'L0_attn_Wq': 6.285,
     'L0_attn_Wk': 6.271,
     'L0_attn_Wv': 6.305,
     'L0_attn_conv_q': 6.303,
     'L0_attn_conv_k': 6.231,
     'L0_attn_conv_v': 6.118,
     'L0_attn_Wb': 8.0,
     'L0_attn_Wa': 8.0,
     'L0_attn_A_log': 8.0,
     'L0_attn_dt_bias': 8.0,
     'L0_attn_Wg': 6.328,
     'L0_attn_Wo': 6.283,
     'L0_ffn_W1': 4.164}
    for name, (base, spread) in spreads.items():
        noise = np.random.default_rng([zlib.crc32(name.encode()), seed]).standard_normal(out[name].shape)
        drawn = base * np.exp(spread * noise) if base else spread * noise
        out[name] = jnp.asarray(drawn.astype(out[name].dtype))
    for name, factor in factors.items():
        out[name] = (out[name] * factor).astype(out[name].dtype)
    return out
```

```python
from contextlib import ExitStack

import concourse.bass as bass
from concourse import mybir

ALU = mybir.AluOpType
ACT = mybir.ActivationFunctionType
F32 = mybir.dt.float32
BF16 = mybir.dt.bfloat16
I32 = mybir.dt.int32
AX_X = mybir.AxisListType.X

P = 128
GROUP = 4
GT = GROUP * P
D = 256
DC = D // P
E = 8
HID = 512
HC = HID // P
H = 8
DK = 128
DV = 64
TAPS = 4
QKV = 2 * H + H * DV // P
VC = H * DV // P
SMALL = E + 2 * H
NEG = -30000.0
LN_EPS = 1e-5
L2_EPS = 1e-6
RMS_EPS = 1e-5
NSTAT = 5


def bc(ap, axis, n):
    ap = ap.unsqueeze(axis)
    shape = list(ap.shape)
    shape[axis] = n
    return ap.to_broadcast(shape)


def col(t, i):
    return t[:, bass.ds(i, 1)]


def build(nc, x, Wq, Wk, Wv, cq, ck, cv, Wb, Wa, A_log, dt_bias, Wg, norm_w, Wo, Wr, W1, b1, W2, b2, out):
    B, T, _ = x.shape
    N = B * T
    NT = N // P
    NG = N // GT
    MT = 2 * NT + E
    xf = x.rearrange("b t d -> (b t) d")
    of = out.rearrange("b t d -> (b t) d")
    xn_d = nc.dram_tensor("xn_rows", [N, D], F32, kind="Internal").ap()
    xnT_d = nc.dram_tensor("xn_cols", [P, DC, N], F32, kind="Internal").ap()
    xg_d = nc.dram_tensor("expert_in", [MT * P, D], F32, kind="Internal").ap()
    yg_d = nc.dram_tensor("expert_out", [MT * P, D], F32, kind="Internal").ap()
    dims = (B, T, N, NT, NG, MT)
    with ExitStack() as ctx:
        def sb(name, shape, dt=F32):
            return ctx.enter_context(nc.sbuf_tensor(name, shape, dt))

        keep = {
            "ident": sb("ident", [P, P]), "tri_le": sb("tri_le", [P, P]), "tri_gt": sb("tri_gt", [P, P]),
            "ones": sb("ones", [P, P]),
            "stat": sb("stat", [P, NT, NSTAT, H]),
            "slot": sb("slot", [P, NT, 2], I32),
            "wtop": sb("wtop", [P, NT, 2]),
            "tile_expert": sb("tile_expert", [1, MT], I32),
        }
        norm_and_route(nc, keep, dims, xf, Wr, Wb, Wa, A_log, dt_bias, xn_d, xnT_d, xg_d)
        experts(nc, keep, dims, W1, b1, W2, b2, xn_d, xg_d, yg_d)
        attention(nc, keep, dims, xf, Wq, Wk, Wv, cq, ck, cv, Wg, norm_w, Wo, xnT_d, yg_d, of)


def norm_and_route(nc, keep, dims, xf, Wr, Wb, Wa, A_log, dt_bias, xn_d, xnT_d, xg_d):
    B, T, N, NT, NG, MT = dims
    ident, tri_le, tri_gt, ones = keep["ident"], keep["tri_le"], keep["tri_gt"], keep["ones"]
    stat, slot, wtop, tile_expert = keep["stat"], keep["slot"], keep["wtop"], keep["tile_expert"]
    ZR = 8
    with ExitStack() as ctx:
        def sb(name, shape, dt=F32):
            return ctx.enter_context(nc.sbuf_tensor("route_" + name, shape, dt))

        def sem(name):
            return ctx.enter_context(nc.semaphore("route_" + name))

        zero = sb("zero", [P, ZR * D])
        w_small = sb("w_small", [P, DC, SMALL])
        alog = sb("alog", [P, H]); dtb = sb("dtb", [P, H]); expa = sb("expa", [P, H])
        tri_lt = sb("tri_lt", [P, P])
        x_in = sb("x_in", [P, 2, GROUP, D])
        xn = sb("xn", [P, 2, GROUP, D])
        xnT = sb("xnT", [P, 2, DC, GT])
        bnst = sb("bnst", [P, 2, GROUP, 6]); mv = sb("mv", [P, 2, GROUP, 2])
        var_eps = sb("var_eps", [P, 2, GROUP]); rstd = sb("rstd", [P, 2, GROUP])
        minus_half = sb("minus_half", [P, GROUP])
        lg = sb("lg", [P, NT, SMALL])
        psT = ctx.enter_context(nc.psum_tensor("route_psT", [P, 2, DC, GT], F32))
        psL = ctx.enter_context(nc.psum_tensor("route_psL", [P, 2, 512], F32))
        psR = ctx.enter_context(nc.psum_tensor("route_psR", [P, 2, 512], F32))
        big = [sb(f"route{i}", [P, NT, E]) for i in range(8)]
        r1 = [sb(f"row{i}", [P, NT]) for i in range(6)]
        e8 = [sb(f"per_expert{i}", [P, E]) for i in range(6)]
        e8i = sb("per_expert_int", [P, E], I32)
        rank_w = sb("rank_w", [P, E])
        jt = sb("jt", [1, MT]); jcmp = sb("jcmp", [1, MT, E]); jsum = sb("jsum", [1, MT])

        consts, params, xn_made = sem("consts"), sem("params"), sem("xn_made")
        x_loaded = [sem(f"x_loaded{par}") for par in range(2)]
        bn_done, aggr_done, ve_done, rstd_done = (sem(n) for n in ("bn_done", "aggr_done", "ve_done", "rstd_done"))
        tr_done, xnT_done, lg_mm, lg_done = sem("tr_done"), sem("xnT_done"), sem("lg_mm"), sem("lg_done")
        rows_stored = [sem(f"rows_stored{par}") for par in range(2)]
        cols_stored = [sem(f"cols_stored{par}") for par in range(2)]
        zeroed, passed = sem("zeroed"), sem("passed")
        step, a_step, mm_step, p_step = sem("route_step"), sem("route_exp"), sem("route_mm"), sem("route_iota")
        block = ctx.enter_context(nc.Block())
        xt_v = xf.rearrange("(g a p) d -> g p a d", a=GROUP, p=P)
        xn_v = xn_d.rearrange("(g a p) d -> g p a d", a=GROUP, p=P)
        NCONST = 12
        counts = {}

        @block.sync
        def _(sp):
            sp.dma_start(w_small[:, :, 0:E], Wr.rearrange("(c p) e -> p c e", p=P)).then_inc(params, 16)
            sp.dma_start(w_small[:, :, E:E + H], Wb.rearrange("(c p) e -> p c e", p=P)).then_inc(params, 16)
            sp.dma_start(w_small[:, :, E + H:SMALL], Wa.rearrange("(c p) e -> p c e", p=P)).then_inc(params, 16)
            sp.dma_start(alog[:, :], A_log.rearrange("(a h) -> a h", a=1).to_broadcast([P, H])).then_inc(params, 16)
            sp.dma_start(dtb[:, :], dt_bias.rearrange("(a h) -> a h", a=1).to_broadcast([P, H])).then_inc(params, 16)
            with sp.Fori(0, NG // 2) as i:
                for par in range(2):
                    g = 2 * i + par
                    sp.wait_ge(xn_made, 4 * g + 4)
                    sp.dma_start(x_in[:, par], xt_v[bass.ds(g, 1)].rearrange("o p a d -> (o p) a d")).then_inc(x_loaded[par], 16)

        @block.gpsimd
        def _(pool):
            pool.memset(zero[:, :], 0.0).then_inc(consts, 1)
            pool.memset(ident[:, :], 0.0).then_inc(consts, 1)
            pool.memset(ones[:, :], 1.0).then_inc(consts, 1)
            pool.memset(minus_half[:, :], -0.5).then_inc(consts, 1)
            pool.wait_ge(consts, 4)
            pool.affine_select(out=ident[:, :], in_=ident[:, :], compare_op=ALU.not_equal, fill=1.0, base=0,
                               pattern=[[-1, P]], channel_multiplier=1).then_inc(consts, 1)
            pool.affine_select(out=tri_le[:, :], in_=ones[:, :], compare_op=ALU.is_ge, fill=0.0, base=0,
                               pattern=[[1, P]], channel_multiplier=-1).then_inc(consts, 1)
            pool.affine_select(out=tri_lt[:, :], in_=ones[:, :], compare_op=ALU.is_gt, fill=0.0, base=0,
                               pattern=[[1, P]], channel_multiplier=-1).then_inc(consts, 1)
            pool.affine_select(out=tri_gt[:, :], in_=ones[:, :], compare_op=ALU.is_gt, fill=0.0, base=0,
                               pattern=[[-1, P]], channel_multiplier=1).then_inc(consts, 1)
            pool.iota(e8i[:, :], pattern=[[-1, E]], base=E, channel_multiplier=0).then_inc(consts, 1)
            pool.wait_ge(consts, 9)
            pool.tensor_copy(rank_w[:, :], e8i[:, :]).then_inc(consts, 1)
            pool.iota(jcmp[0:1, :, 0].bitcast(I32), pattern=[[1, MT]], base=0, channel_multiplier=0).then_inc(consts, 1)
            pool.wait_ge(consts, 11)
            pool.tensor_copy(jt[0:1, :], jcmp[0:1, :, 0].bitcast(I32)).then_inc(consts, 1)
            for r in range(MT // ZR):
                pool.dma_start(xg_d[r * ZR * P:(r + 1) * ZR * P, :].rearrange("(p r) d -> p (r d)", p=P), zero[:, :]).then_inc(zeroed, 16)
            with pool.Fori(0, NG // 2) as i:
                for par in range(2):
                    pool.wait_ge(ve_done, 2 * i + par + 1)
                    pool.tensor_tensor(rstd[:, par], var_eps[:, par], minus_half[:, :], op=ALU.pow).then_inc(rstd_done, 1)
            pool.wait_ge(zeroed, 16 * (MT // ZR))

        @block.vector
        def _(dve):
            dve.sem_inc(xn_made, 2 * GROUP)
            dve.sem_inc(lg_done, 2)
            dve.sem_inc(xnT_done, 4)
            with dve.Fori(0, NG // 2) as i:
                for par in range(2):
                    g = 2 * i + par
                    dve.wait_ge(x_loaded[par], 16 * i + 16)
                    for a in range(GROUP):
                        nc.vector.bn_stats(bnst[:, par, a], x_in[:, par, a]).then_inc(bn_done, 1)
                    for a in range(GROUP):
                        dve.wait_ge(bn_done, 4 * g + a + 1)
                        dve.sem_inc(passed, 1)
                        nc.vector.bn_aggr(mv[:, par, a], bnst[:, par, a]).then_inc(aggr_done, 1)
                    dve.wait_ge(aggr_done, 4 * g + 4)
                    nc.vector.tensor_scalar(var_eps[:, par], mv[:, par, :, 1], LN_EPS, None, ALU.add).then_inc(ve_done, 1)
                    dve.wait_ge(rstd_done, g + 1)
                    dve.wait_ge(rows_stored[par], 16 * i + 16)
                    dve.wait_ge(tr_done, g + 1)
                    for a in range(GROUP):
                        nc.vector.tensor_scalar(xn[:, par, a], x_in[:, par, a], mv[:, par, a, 0:1], rstd[:, par, a:a + 1],
                                                ALU.subtract, ALU.mult).then_inc(xn_made, 1)
                    dve.wait_ge(tr_done, g + 3)
                    dve.wait_ge(cols_stored[par], 16 * i + 16)
                    nc.vector.tensor_copy(xnT[:, par, 1], psT[:, par, 1]).then_inc(xnT_done, 1)
                    dve.wait_ge(lg_mm, g + 1)
                    nc.vector.tensor_scalar(lg[:, bass.ds(4 * g, GROUP), :], psL[:, par, 0:GROUP * SMALL].rearrange("p (a s) -> p a s", a=GROUP),
                                            1.0, None, ALU.mult).then_inc(lg_done, 1)
            n = [0]

            def link(ins):
                n[0] += 1
                ins.then_inc(step, 1)
                dve.wait_ge(step, n[0])

            V = nc.vector
            dve.wait_ge(lg_done, NG + 2)
            L = lg[:, :, 0:E]
            oh1, cand, oh2, l2, mask, ex, cnt, pos = big
            m1, m2, pick, esum, w1s, dd = r1
            rw = bc(rank_w[:, :], 1, NT)

            def onehot(dst, src, top):
                link(V.tensor_reduce(top[:, :], src, op=ALU.max, axis=AX_X))
                link(V.tensor_tensor(cand[:, :, :], src, bc(top[:, :], 2, E), op=ALU.is_equal))
                link(V.tensor_tensor(cand[:, :, :], cand[:, :, :], rw, op=ALU.mult))
                link(V.tensor_reduce(pick[:, :], cand[:, :, :], op=ALU.max, axis=AX_X))
                link(V.tensor_tensor(dst[:, :, :], cand[:, :, :], bc(pick[:, :], 2, E), op=ALU.is_equal))

            onehot(oh1, L, m1)
            link(V.scalar_tensor_tensor(out=l2[:, :, :], in0=oh1[:, :, :], scalar=-3.0e38, in1=L, op0=ALU.mult, op1=ALU.add))
            onehot(oh2, l2[:, :, :], m2)
            link(V.tensor_tensor(dd[:, :], m2[:, :], m1[:, :], op=ALU.subtract))
            link(V.tensor_tensor(mask[:, :, :], oh1[:, :, :], oh2[:, :, :], op=ALU.add))
            mask_at = n[0]
            dve.wait_ge(a_step, 1)
            link(V.tensor_scalar(esum[:, :], w1s[:, :], 1.0, None, ALU.add))
            link(V.reciprocal(pick[:, :], esum[:, :]))
            link(V.tensor_copy(wtop[:, :, 0], pick[:, :]))
            link(V.tensor_tensor(wtop[:, :, 1], pick[:, :], w1s[:, :], op=ALU.mult))
            dve.wait_ge(mm_step, 1)
            link(V.tensor_copy(cnt[:, :, :], psR[:, 1, 0:NT * E].rearrange("p (t e) -> p t e", e=E)))
            link(V.memset(l2[:, :, :], 0.0))
            for e in range(E):
                link(V.tensor_tensor_scan(out=ex[:, :, e], data0=cnt[:, :, e], data1=l2[:, :, e], initial=0.0,
                                          op0=ALU.add, op1=ALU.add))
            tot, tiles_f, end, base, zer8, tmp8 = e8
            link(V.tensor_scalar(tot[:, :], ex[:, NT - 1, :], float(P - 1), None, ALU.add))
            link(V.tensor_copy(e8i[:, :], tot[:, :]))
            link(V.tensor_scalar(e8i[:, :], e8i[:, :], 7, None, ALU.arith_shift_right))
            link(V.tensor_copy(tiles_f[:, :], e8i[:, :]))
            link(V.memset(zer8[:, :], 0.0))
            link(V.tensor_tensor_scan(out=end[:, :], data0=tiles_f[:, :], data1=zer8[:, :], initial=0.0, op0=ALU.add, op1=ALU.add))
            link(V.tensor_tensor(base[:, :], end[:, :], tiles_f[:, :], op=ALU.subtract))
            link(V.tensor_scalar(base[:, :], base[:, :], float(P), None, ALU.mult))
            link(V.tensor_tensor(ex[:, :, :], ex[:, :, :], cnt[:, :, :], op=ALU.subtract))
            link(V.tensor_tensor(pos[:, :, :], ex[:, :, :], psR[:, 0, 0:NT * E].rearrange("p (t e) -> p t e", e=E), op=ALU.add))
            link(V.tensor_tensor(pos[:, :, :], pos[:, :, :], bc(base[:, :], 1, NT), op=ALU.add))
            for k, oh in enumerate((oh1, oh2)):
                link(V.tensor_tensor(cand[:, :, :], pos[:, :, :], oh[:, :, :], op=ALU.mult))
                link(V.tensor_reduce(m1[:, :], cand[:, :, :], op=ALU.add, axis=AX_X))
                link(V.tensor_copy(slot[:, :, k], m1[:, :]))
            link(V.tensor_tensor(jcmp[0:1, :, :], bc(jt[0:1, :], 2, E), bc(end[0:1, :], 1, MT), op=ALU.is_ge))
            link(V.tensor_reduce(jsum[0:1, :], jcmp[0:1, :, :], op=ALU.add, axis=AX_X))
            link(V.tensor_scalar(jsum[0:1, :], jsum[0:1, :], float(E - 1), None, ALU.min))
            link(V.tensor_copy(tile_expert[0:1, :], jsum[0:1, :]))
            a_in, u, s, s2, acc, ab = (t for t in (oh1, cand, oh2, l2, mask, ex))
            link(V.tensor_tensor(a_in[:, :, :], lg[:, :, E + H:SMALL], bc(dtb[:, :], 1, NT), op=ALU.add))
            link(V.tensor_scalar(ab[:, :, :], a_in[:, :, :], -1.0, None, ALU.mult))
            link(V.tensor_tensor(ab[:, :, :], a_in[:, :, :], ab[:, :, :], op=ALU.min))
            ab_at = n[0]
            dve.wait_ge(a_step, 4)
            link(V.tensor_scalar(s[:, :, :], u[:, :, :], 2.0, None, ALU.add))
            link(V.reciprocal(s[:, :, :], s[:, :, :]))
            link(V.tensor_tensor(s[:, :, :], s[:, :, :], u[:, :, :], op=ALU.mult))
            link(V.tensor_tensor(s2[:, :, :], s[:, :, :], s[:, :, :], op=ALU.mult))
            link(V.tensor_scalar(acc[:, :, :], s2[:, :, :], 1.0 / 17, 1.0 / 15, ALU.mult, ALU.add))
            for k in (13, 11, 9, 7, 5, 3, 1):
                link(V.tensor_tensor(acc[:, :, :], acc[:, :, :], s2[:, :, :], op=ALU.mult))
                link(V.tensor_scalar(acc[:, :, :], acc[:, :, :], 1.0 / k, None, ALU.add))
            link(V.tensor_tensor(acc[:, :, :], acc[:, :, :], s[:, :, :], op=ALU.mult))
            link(V.tensor_scalar(a_in[:, :, :], a_in[:, :, :], 0.0, None, ALU.max))
            link(V.scalar_tensor_tensor(out=acc[:, :, :], in0=acc[:, :, :], scalar=2.0, in1=a_in[:, :, :], op0=ALU.mult, op1=ALU.add))
            link(V.scalar_tensor_tensor(out=stat[:, :, 1, :], in0=acc[:, :, :], scalar=-1.0, in1=bc(expa[:, :], 1, NT), op0=ALU.mult, op1=ALU.mult))
            g_at = n[0]
            link(V.tensor_scalar(pos[:, :, :], pos[:, :, :], 1.0, None, ALU.add))
            link(V.reciprocal(pos[:, :, :], pos[:, :, :]))
            link(V.tensor_copy(stat[:, :, 0, :], pos[:, :, :]))
            counts["mask"], counts["ab"], counts["g"] = mask_at, ab_at, g_at
            counts["end"] = n[0]

        @block.scalar
        def _(act):
            act.wait_ge(params, 80)
            with act.Fori(0, NG // 2) as i:
                for par in range(2):
                    g = 2 * i + par
                    act.wait_ge(xn_made, 4 * g + 12)
                    act.dma_start(xn_v[bass.ds(g, 1)].rearrange("o p a d -> (o p) a d"), xn[:, par]).then_inc(rows_stored[par], 16)
                    act.wait_ge(tr_done, g + 3)
                    act.wait_ge(cols_stored[par], 16 * i + 16)
                    nc.scalar.activation(xnT[:, par, 0], psT[:, par, 0], ACT.Copy).then_inc(xnT_done, 1)
                    act.wait_ge(xnT_done, 2 * g + 6)
                    act.dma_start(xnT_d[:, :, bass.ds(g * GT, GT)], xnT[:, par]).then_inc(cols_stored[par], 16)
            m2_m1, w1s = r1[5], r1[4]
            act.wait_ge(step, counts["mask"])
            nc.scalar.activation(w1s[:, :], m2_m1[:, :], ACT.Exp).then_inc(a_step, 1)
            nc.scalar.activation(expa[:, :], alog[:, :], ACT.Exp).then_inc(a_step, 1)
            act.wait_ge(step, counts["ab"])
            nc.scalar.activation(big[1][:, :, :], big[5][:, :, :], ACT.Exp).then_inc(a_step, 1)
            nc.scalar.activation(big[7][:, :, :], lg[:, :, E:E + H], ACT.Exp, scale=-1.0).then_inc(a_step, 1)
            for k in range(3):
                act.wait_ge(mm_step, 2 + k)
                src = (psR[:, 0], psR[:, 1], psL[:, 0])[k]
                nc.scalar.activation(stat[:, :, 2 + k, :], src[:, 0:NT * H].rearrange("p (t h) -> p t h", h=H), ACT.Exp).then_inc(a_step, 1)
            for par in range(2):
                act.wait_ge(rows_stored[par], 8 * NG + 16)
            for par in range(2):
                act.wait_ge(cols_stored[par], 8 * NG + 16)

        @block.tensor
        def _(pe):
            pe.sem_inc(tr_done, 2)
            for par in range(2):
                pe.sem_inc(rows_stored[par], 16)
            for par in range(2):
                pe.sem_inc(cols_stored[par], 16)
            pe.wait_ge(params, 80)
            pe.wait_ge(consts, NCONST)
            with pe.Fori(0, NG // 2) as i:
                for par in range(2):
                    g = 2 * i + par
                    pe.wait_ge(xn_made, 4 * g + 12)
                    pe.wait_ge(xnT_done, 2 * g + 2)
                    for c in range(DC):
                        for a in range(GROUP):
                            last = nc.tensor.transpose(psT[:, par, c, a * P:(a + 1) * P], xn[:, par, a, c * P:(c + 1) * P], ident[:, :])
                    last.then_inc(tr_done, 1)
                    pe.wait_ge(xnT_done, 2 * g + 6)
                    pe.wait_ge(lg_done, g + 1)
                    for a in range(GROUP):
                        for c in range(DC):
                            last = nc.tensor.matmul(psL[:, par, a * SMALL:(a + 1) * SMALL], xnT[:, par, c, a * P:(a + 1) * P],
                                                    w_small[:, c, :], start=(c == 0), stop=(c == DC - 1))
                    last.then_inc(lg_mm, 1)
            pe.wait_ge(step, counts["mask"])
            mk = big[4][:, :, :].rearrange("p t e -> p (t e)")
            nc.tensor.matmul(psR[:, 0, 0:NT * E], tri_lt[:, :], mk, start=True, stop=True)
            nc.tensor.matmul(psR[:, 1, 0:NT * E], ones[:, :], mk, start=True, stop=True).then_inc(mm_step, 1)
            pe.wait_ge(step, counts["g"])
            for k, (dst, tri) in enumerate(((psR[:, 0], tri_le), (psR[:, 1], tri_gt), (psL[:, 0], ones))):
                nc.tensor.matmul(dst[:, 0:NT * H], tri[:, :], stat[:, :, 1, :], start=True, stop=True).then_inc(mm_step, 1)


def experts(nc, keep, dims, W1, b1, W2, b2, xn_d, xg_d, yg_d):
    B, T, N, NT, NG, MT = dims
    ident, slot, tile_expert = keep["ident"], keep["slot"], keep["tile_expert"]
    with ExitStack() as ctx:
        def sb(name, shape, dt=F32):
            return ctx.enter_context(nc.sbuf_tensor("moe_" + name, shape, dt))

        def pair(name):
            return [ctx.enter_context(nc.psum_tensor(f"moe_{name}{i}", [P, 512], F32)) for i in range(2)]

        def sem(name):
            return ctx.enter_context(nc.semaphore("moe_" + name))

        w1 = sb("w1", [P, E, DC, HID]); w2 = sb("w2", [P, E, HC, D])
        b1b = sb("b1b", [P, E, HID]); b2b = sb("b2b", [P, E, D])
        rows = sb("rows", [P, 2, GROUP, D]); idx = sb("idx", [P, 2, GROUP, 2], I32)
        xt = sb("xt", [P, 2, D]); xT = sb("xT", [P, 2, DC, P])
        h = sb("h", [P, 2, HID]); hT = sb("hT", [P, 2, HC, P]); y = sb("y", [P, 2, D])
        psX, psH, psHT, psY = pair("psX"), pair("psH"), pair("psHT"), pair("psY")

        weights = [sem(f"weights{i}") for i in range(4)]
        rows_loaded = [sem(f"rows_loaded{i}") for i in range(2)]
        scattered = [sem(f"scattered{i}") for i in range(2)]
        idx_copied, passed = sem("idx_copied"), sem("passed")
        x_loaded = [sem(f"tile_loaded{i}") for i in range(2)]
        y_stored = [sem(f"y_stored{i}") for i in range(2)]
        xtr, xT_done, h_mm, h_done, htr, hT_done, y_mm, y_done = (
            sem(n) for n in ("xtr", "xT_done", "h_mm", "h_done", "htr", "hT_done", "y_mm", "y_done"))
        block = ctx.enter_context(nc.Block())
        rows_v = xn_d.rearrange("(g a p) d -> g p a d", a=GROUP, p=P)
        xg_v = xg_d.rearrange("(t p) d -> t p d", p=P)
        yg_v = yg_d.rearrange("(t p) d -> t p d", p=P)

        def before(q, par):
            return (q, 0) if par else (q - 1, 1)

        def after(q, par):
            return (q + 1, 0) if par else (q, 1)

        def steps(eng, step):
            step(None, (0, 0), None)
            step((0, 0), (0, 1), None)
            step((0, 1), (1, 0), (0, 0))
            step((1, 0), (1, 1), (0, 1))
            with eng.Fori(1, MT // 2 - 1) as i:
                for tile in ((i, 1), (i + 1, 0)):
                    step(tile, after(*tile), before(*tile))
            last = (MT // 2 - 1, 1)
            step(last, None, before(*last))
            step(None, None, last)

        @block.sync
        def _(sp):
            sp.dma_start(w1[:, :, :, :], W1.rearrange("e (c p) n -> p e c n", p=P)).then_inc(weights[0], 16)
            for par in range(2):
                sp.dma_start(rows[:, par], rows_v[par]).then_inc(rows_loaded[par], 16)
            with sp.Fori(1, NG // 2) as i:
                for par in range(2):
                    sp.wait_ge(scattered[par], 2 * GROUP * 16 * i)
                    sp.dma_start(rows[:, par], rows_v[bass.ds(2 * i + par, 1)].rearrange("o p a d -> (o p) a d")).then_inc(rows_loaded[par], 16)
            for par in range(2):
                sp.wait_ge(scattered[par], 2 * GROUP * 16 * (NG // 2))
            with sp.Fori(0, MT // 2) as i:
                for par in range(2):
                    sp.wait_ge(xtr, 2 * i + par + 1)
                    sp.dma_start(xt[:, par], xg_v[bass.ds(2 * i + par, 1)].rearrange("o p d -> (o p) d")).then_inc(x_loaded[par], 16)

        @block.gpsimd
        def _(pool):
            pool.sem_inc(idx_copied, 1)

            def scatter(i):
                for par in range(2):
                    g = 2 * i + par
                    if not (isinstance(i, int) and i == 0):
                        pool.wait_ge(scattered[par], 2 * GROUP * 16 * i)
                    pool.tensor_copy(idx[:, par], slot[:, bass.ds(GROUP * g, GROUP), :]).then_inc(idx_copied, 1)
                    pool.wait_ge(rows_loaded[par], 16 * i + 16)
                    pool.wait_ge(idx_copied, g + 2)
                    pool.sem_inc(passed, 1)
                    for a in range(GROUP):
                        for k in range(2):
                            pool.indirect_dma_start(xg_d[:, :], bass.IndirectOffsetOnAxis(ap=idx[:, par, a, k:k + 1], axis=0),
                                                    rows[:, par, a], None).then_inc(scattered[par], 16)

            scatter(0)
            with pool.Fori(1, NG // 2) as i:
                scatter(i)
            with pool.Fori(0, MT // 2) as i:
                for par in range(2):
                    t = 2 * i + par
                    pool.wait_ge(y_done, t + 3)
                    pool.sem_inc(passed, 1)
                    pool.dma_start(yg_v[bass.ds(t, 1)].rearrange("o p d -> (o p) d"), y[:, par]).then_inc(y_stored[par], 16)
            for par in range(2):
                pool.wait_ge(y_stored[par], 8 * MT)

        @block.scalar
        def _(act):
            act.sem_inc(xT_done, 2)
            act.sem_inc(hT_done, 2)
            act.dma_start(w2[:, :, :, :], W2.rearrange("e (c p) n -> p e c n", p=P)).then_inc(weights[1], 16)
            act.dma_start(b1b[:, :, :], b1.rearrange("(o e) n -> o e n", o=1).to_broadcast([P, E, HID])).then_inc(weights[2], 16)
            act.dma_start(b2b[:, :, :], b2.rearrange("(o e) n -> o e n", o=1).to_broadcast([P, E, D])).then_inc(weights[3], 16)

            def step(cur, nxt, prev):
                if prev:
                    q, par = prev
                    t = 2 * q + par
                    act.wait_ge(htr, t + 3)
                    act.wait_ge(y_mm, t + 1)
                    nc.scalar.activation(hT[:, par], psHT[par][:, :].rearrange("p (c n) -> p c n", c=HC), ACT.Relu).then_inc(hT_done, 1)
                if nxt:
                    q, par = nxt
                    t = 2 * q + par
                    act.wait_ge(xtr, t + 3)
                    act.wait_ge(h_mm, t + 1)
                    nc.scalar.activation(xT[:, par], psX[par][:, 0:D].rearrange("p (c n) -> p c n", c=DC), ACT.Copy).then_inc(xT_done, 1)

            steps(act, step)

        @block.vector
        def _(dve):
            dve.sem_inc(h_done, 2)
            dve.sem_inc(y_done, 2)
            for w in weights[2:]:
                dve.wait_ge(w, 16)

            def step(cur, nxt, prev):
                if cur:
                    q, par = cur
                    t = 2 * q + par
                    e = dve.value_load(tile_expert[0:1, t:t + 1] if isinstance(t, int) else tile_expert[0:1, bass.ds(t, 1)], min_val=0, max_val=E - 1)
                    dve.wait_ge(h_mm, t + 3)
                    dve.wait_ge(htr, t + 1)
                    nc.vector.tensor_tensor(h[:, par], psH[par][:, :], b1b[:, bass.ds(e, 1), :].rearrange("p o n -> p (o n)"), op=ALU.add).then_inc(h_done, 1)
                if prev:
                    q, par = prev
                    t = 2 * q + par
                    e = dve.value_load(tile_expert[0:1, t:t + 1] if isinstance(t, int) else tile_expert[0:1, bass.ds(t, 1)], min_val=0, max_val=E - 1)
                    dve.wait_ge(y_mm, t + 3)
                    if not isinstance(q, int) or q > 0:
                        dve.wait_ge(y_stored[par], 16 * q)
                    nc.vector.tensor_tensor(y[:, par], psY[par][:, 0:D], b2b[:, bass.ds(e, 1), :].rearrange("p o n -> p (o n)"), op=ALU.add).then_inc(y_done, 1)

            steps(dve, step)

        @block.tensor
        def _(pe):
            for s in (xtr, h_mm, htr, y_mm):
                pe.sem_inc(s, 2)
            for w in weights[0:2]:
                pe.wait_ge(w, 16)

            def expert(t):
                return pe.value_load(tile_expert[0:1, t:t + 1] if isinstance(t, int) else tile_expert[0:1, bass.ds(t, 1)], min_val=0, max_val=E - 1)

            def step(cur, nxt, prev):
                if nxt:
                    q, par = nxt
                    t = 2 * q + par
                    pe.wait_ge(x_loaded[par], 16 * q + 16)
                    pe.wait_ge(xT_done, t + 1)
                    for c in range(DC):
                        last = nc.tensor.transpose(psX[par][:, c * P:(c + 1) * P], xt[:, par, c * P:(c + 1) * P], ident[:, :])
                    last.then_inc(xtr, 1)
                if prev:
                    q, par = prev
                    t = 2 * q + par
                    pe.wait_ge(h_done, t + 3)
                    pe.wait_ge(hT_done, t + 1)
                    for c in range(HC):
                        last = nc.tensor.transpose(psHT[par][:, c * P:(c + 1) * P], h[:, par, c * P:(c + 1) * P], ident[:, :])
                    last.then_inc(htr, 1)
                if cur:
                    q, par = cur
                    t = 2 * q + par
                    e = expert(t)
                    pe.wait_ge(xT_done, t + 3)
                    pe.wait_ge(h_done, t + 1)
                    for c in range(DC):
                        last = nc.tensor.matmul(psH[par][:, :], xT[:, par, c], w1[:, bass.ds(e, 1), c].rearrange("p o n -> p (o n)"),
                                                start=(c == 0), stop=(c == DC - 1))
                    last.then_inc(h_mm, 1)
                if prev:
                    q, par = prev
                    t = 2 * q + par
                    e = expert(t)
                    pe.wait_ge(hT_done, t + 3)
                    pe.wait_ge(y_done, t + 1)
                    for c in range(HC):
                        last = nc.tensor.matmul(psY[par][:, 0:D], hT[:, par, c], w2[:, bass.ds(e, 1), c].rearrange("p o n -> p (o n)"),
                                                start=(c == 0), stop=(c == HC - 1))
                    last.then_inc(y_mm, 1)

            steps(pe, step)


def scan_order():
    order = [(step, 0) for step in ("tokens", "p32", "y32", "p64", "y64")]
    for c in range(GROUP):
        nxt = [(step, c + 1) for step in ("p32", "y32", "p64", "tokens", "y64")] if c + 1 < GROUP else [None] * 5
        order += [("read", c), nxt[0], ("solve", c), nxt[1], ("apply", c), nxt[2], nxt[3], ("norm", c), nxt[4], ("out", c)]
    return [x for x in order if x]


CREDIT = 4


def attention(nc, keep, dims, xf, Wq, Wk, Wv, cq, ck, cv, Wg, norm_w, Wo, xnT_d, yg_d, of):
    B, T, N, NT, NG, MT = dims
    ident, tri_le, tri_gt, ones = keep["ident"], keep["tri_le"], keep["tri_gt"], keep["ones"]
    U = GROUP * H
    NB = P // 32
    PAIRS = QKV // 2
    QKP = 2 * H // 2
    HV = H * DV
    PER_BATCH = T // GT
    assert U == 32
    with ExitStack() as ctx:
        def sb(name, shape, dt=F32):
            return ctx.enter_context(nc.sbuf_tensor("att_" + name, shape, dt))

        wqkv = sb("wqkv", [P, DC, QKV * P]); wg = sb("wg", [P, DC, HV]); wo = sb("wo", [P, VC, D])
        cw = sb("cw", [P, QKV, TAPS]); nw = sb("nw", [P, DV])
        identb = sb("identb", [P, P], BF16); negb = sb("negb", [P, GROUP, P], BF16)
        half = sb("half", [P, GROUP, H]); mhalf = sb("mhalf", [P, GROUP, H]); goes_on = sb("goes_on", [P, NG])
        xt = sb("xt", [P, DC, GT])
        qk = sb("qk", [P, H, 2, GT]); vc = sb("vc", [P, VC, GT]); sq = sb("sq", [P, 2, 2, GT])
        tails = sb("tails", [P, QKV, 3]); tk = sb("tk", [P, QKV, 3]); corr = sb("corr", [P, QKV, 3]); ctmp = sb("ctmp", [P, QKV, 3])
        gate = sb("gate", [P, GROUP, HV])
        mst = sb("mst", [P, GROUP, NSTAT, H]); wt = sb("wt", [P, GROUP, 2]); sidx = sb("sidx", [P, GROUP, 2], I32)
        nkq = sb("nkq", [P, GROUP, 2, H]); rn = sb("rn", [P, GROUP, H]); eps = sb("eps", [P, GROUP, H])
        knorm = sb("knorm", [P, GROUP, H]); qscale = sb("qscale", [P, GROUP, H])
        qg = sb("qg", [P, H, P]); dec = sb("dec", [P, 2, GROUP, P])
        Y = sb("Y", [P, U, P]); AT = sb("AT", [P, U, P]); X = sb("X", [P, U, 64])
        vr = sb("vr", [P, GROUP, HV]); ktok = sb("ktok", [P, 2, H, P])
        Pb = sb("Pb", [P, H, 64])
        S = sb("S", [P, HV]); Sd = sb("Sd", [P, HV])
        ks = sb("ks", [P, HV]); R = sb("R", [P, HV]); W1s = sb("Wp", [P, HV]); W2s = sb("Wpp", [P, HV])
        t2 = sb("t2", [P, HV]); O = sb("O", [P, HV]); O3 = sb("O3", [P, HV])
        lane_n, lane_x = (sq[:, i].rearrange("p h (i j) -> p (h i) j", j=32) for i in range(2))
        lane_t, osq, O2, acc1, acc2 = R[:, 0:256], t2, O, ks[:, 0:D], ks[:, D:2 * D]
        ss = sb("ss", [P, H]); f1 = sb("f1", [P, H]); f2 = sb("f2", [P, H]); f3 = sb("f3", [P, H]); f4 = sb("f4", [P, H]); fo = sb("fo", [P, H])
        oT = sb("oT", [P, VC, P]); yb = sb("yb", [P, GROUP, 2, D]); xr = sb("xr", [P, GROUP, D])
        ob = sb("ob", [P, 2, D])

        pA = ctx.enter_context(nc.psum_tensor("att_psA", [P, 2, 512], F32))
        pB = [ctx.enter_context(nc.psum_tensor(f"att_psB{i}", [P, 512], F32)) for i in range(2)]
        pC = [ctx.enter_context(nc.psum_tensor(f"att_psC{i}", [P, 512], F32)) for i in range(2)]
        pD = ctx.enter_context(nc.psum_tensor("att_psD", [P, 512], F32))
        pE = ctx.enter_context(nc.psum_tensor("att_psE", [P, 512], F32))

        names = {
            "tensor": "proj_ready gate_ready norms_mm dexp_ready kkq_ready vtr_ready ktok_ready p32_ready y32_ready "
                      "p64_ready y64_ready ks_ready s_read w_ready aw_ready sup_ready otr_ready wo_ready",
            "scalar": "tap3_done silu_done gate_done dec_done ktok_done p32_done y32_done p64_done y64_done oT_done",
            "vector": "tap taps_done tails_done nkq_done rn_done eps_done kkq_used vr_done elim inv_done p32_done_v "
                      "y32_done_v ks_scaled r_done w1_done w2_done t2_done o_sum s_kept s_done ss_done o2_done o3_done "
                      "acc1_done acc2_done fin_done",
            "gpsimd": "mst_done wt_done sidx_done tk_done corr_step corr_done qg_ready sq_ready gatew_done knorm_done "
                      "qscale_done sd_done osq_done f_step f5_done f_done",
        }
        s = {n: ctx.enter_context(nc.semaphore("att_" + n)) for group in names.values() for n in group.split()}
        params, consts = ctx.enter_context(nc.semaphore("att_params")), ctx.enter_context(nc.semaphore("att_consts"))
        xt_loaded, xr_loaded, y_loaded = (ctx.enter_context(nc.semaphore("att_" + n)) for n in ("xt_loaded", "xr_loaded", "y_loaded"))
        out_stored = [ctx.enter_context(nc.semaphore(f"att_out_stored{i}")) for i in range(2)]
        block = ctx.enter_context(nc.Block())
        passed = ctx.enter_context(nc.semaphore("att_passed"))
        NPARAM, NCONST = 9, 10

        def credits(eng, which):
            for n in names[which].split():
                eng.sem_inc(s[n], CREDIT)

        def wait(eng, name, count):
            eng.wait_ge(s[name], count + CREDIT)

        def apart(eng):
            eng.sem_inc(passed, 1)

        def conv_dst(k):
            if k < H // 2:
                return qk[:, 2 * k:2 * k + 2, 0, :]
            if k < H:
                return qk[:, 2 * k - H:2 * k - H + 2, 1, :]
            return vc[:, 2 * (k - H):2 * (k - H) + 2, :]

        def heads(ap):
            return ap.rearrange("p (h v) -> p h v", h=H)

        xt_v = xnT_d
        xr_v = xf.rearrange("(g a p) d -> g p a d", a=GROUP, p=P)
        of_v = of.rearrange("(t p) d -> t p d", p=P)

        @block.sync
        def _(sp):
            hq = H * DK
            sp.dma_start(wqkv[:, :, 0:hq], Wq.rearrange("(c p) n -> p c n", p=P)).then_inc(params, 16)
            sp.dma_start(wqkv[:, :, hq:2 * hq], Wk.rearrange("(c p) n -> p c n", p=P)).then_inc(params, 16)
            sp.dma_start(wqkv[:, :, 2 * hq:], Wv.rearrange("(c p) n -> p c n", p=P)).then_inc(params, 16)
            sp.dma_start(cw[:, 0:H, :], cq.rearrange("(c p) k -> p c k", p=P)).then_inc(params, 16)
            sp.dma_start(cw[:, H:2 * H, :], ck.rearrange("(c p) k -> p c k", p=P)).then_inc(params, 16)
            sp.dma_start(cw[:, 2 * H:QKV, :], cv.rearrange("(c p) k -> p c k", p=P)).then_inc(params, 16)
            sp.dma_start(wg[:, :, :], Wg.rearrange("(c p) n -> p c n", p=P)).then_inc(params, 16)
            sp.dma_start(wo[:, :, :], Wo.rearrange("(c p) n -> p c n", p=P)).then_inc(params, 16)
            sp.dma_start(nw[:, :], norm_w.rearrange("(a n) -> a n", a=1).to_broadcast([P, DV])).then_inc(params, 16)
            with sp.Fori(0, NG) as m:
                wait(sp, "proj_ready", PAIRS * m)
                wait(sp, "gate_ready", GROUP * m)
                sp.dma_start(xt[:, :, :], xt_v[:, :, bass.ds(m * GT, GT)]).then_inc(xt_loaded, 16)
                wait(sp, "fin_done", GROUP * m)
                sp.dma_start(xr[:, :, :], xr_v[bass.ds(m, 1)].rearrange("o p a d -> (o p) a d")).then_inc(xr_loaded, 16)

        @block.tensor
        def _(pe):
            credits(pe, "tensor")
            pe.wait_ge(params, 16 * NPARAM)
            pe.wait_ge(consts, NCONST)
            MM, TR = nc.tensor.matmul, nc.tensor.transpose

            def project(m, k):
                wait(pe, "taps_done", PAIRS * m + k)
                if k == 0:
                    pe.wait_ge(xt_loaded, 16 * m + 16)
                    wait(pe, "ktok_done", 2 * GROUP * m)
                    wait(pe, "oT_done", GROUP * m)
                for h in range(2):
                    for c in range(DC):
                        last = MM(pA[:, h, :], wqkv[:, c, (2 * k + h) * P:(2 * k + h + 1) * P], xt[:, c, :], start=(c == 0), stop=(c == DC - 1))
                last.then_inc(s["proj_ready"], 1)

            def project_gate(m, c):
                wait(pe, "o_sum", GROUP * m)
                wait(pe, "gate_done", GROUP * m + c)
                for d in range(DC):
                    last = MM(pD[:, :], xt[:, d, c * P:(c + 1) * P], wg[:, d, :], start=(d == 0), stop=(d == DC - 1))
                last.then_inc(s["gate_ready"], 1)

            def norms(m, k):
                wait(pe, "sq_ready", QKP * m + k + 1)
                wait(pe, "fin_done", GROUP * m)
                for h in range(2):
                    for c in range(GROUP):
                        at = c * 2 * H + 2 * k + h
                        last = MM(pE[:, at:at + 1], sq[:, k % 2, h, c * P:(c + 1) * P], ones[:, 0:1], start=True, stop=True)
                last.then_inc(s["norms_mm"], 1)

            def products(m, c):
                n = GROUP * m + c
                for g in range(2):
                    wait(pe, "qg_ready", n + 1)
                    wait(pe, "dec_done", 2 * n + g - 1)
                    wait(pe, "y64_done", GROUP * m)
                    MM(pB[g][:, :], tri_gt[:, :], qg[:, 4 * g:4 * g + 4, :], start=True, stop=False)
                    MM(pB[g][:, :], identb[:, :], negb[:, :, :], start=False, stop=True).then_inc(s["dexp_ready"], 1)
                if c == 0:
                    wait(pe, "silu_done", PAIRS * m + PAIRS)
                    wait(pe, "t2_done", GROUP * m)
                    wait(pe, "w1_done", GROUP * m)
                    wait(pe, "gate_done", GROUP * m + GROUP)
                for g in range(4):
                    wait(pe, "kkq_used", 4 * n + g - 1)
                    for h in range(2):
                        last = MM(pC[g % 2][:, 256 * h:256 * h + 256].rearrange("p (a n) -> p a n", a=2), qk[:, 2 * g + h, 1, c * P:(c + 1) * P],
                                  qk[:, 2 * g + h, :, c * P:(c + 1) * P], start=True, stop=True)
                    last.then_inc(s["kkq_ready"], 1)
                wait(pe, "vr_done", n)
                for j in range(VC):
                    last = TR(pD[:, j * P:(j + 1) * P], vc[:, j, c * P:(c + 1) * P], ident[:, :])
                last.then_inc(s["vtr_ready"], 1)

            def tokens(m, c):
                n = GROUP * m + c
                wait(pe, "taps_done", PAIRS * m + PAIRS)
                wait(pe, "ktok_done", 2 * n)
                wait(pe, "oT_done", n - 1)
                for g in range(2):
                    for h in range(4):
                        last = TR(pA[:, g, h * P:(h + 1) * P], qk[:, 4 * g + h, 1, c * P:(c + 1) * P], ident[:, :])
                    last.then_inc(s["ktok_ready"], 1)

            def p32(m, c):
                n = GROUP * m + c
                wait(pe, "inv_done", m + 1)
                wait(pe, "dec_done", 2 * GROUP * m + 2 * GROUP)
                wait(pe, "y64_done", n)
                apart(pe)
                for q in range(2):
                    a, b = 64 * q, 64 * q + 32
                    for h in range(H):
                        u = c * H + h
                        last = MM(pB[q][b:b + 32, 32 * h:32 * h + 32], Y[a:a + 32, u, b:b + 32], X[a:a + 32, u, 0:32], start=True, stop=True)
                last.then_inc(s["p32_ready"], 1)

            def y32(m, c):
                n = GROUP * m + c
                wait(pe, "p32_done", n + 1)
                wait(pe, "p32_done_v", n + 1)
                apart(pe)
                for q in range(2):
                    a, b = 64 * q, 64 * q + 32
                    for h in range(H):
                        u = c * H + h
                        last = MM(pB[q][a:a + 32, 256 + 32 * h:288 + 32 * h], Pb[b:b + 32, h, 0:32], Y[b:b + 32, u, b:b + 32], start=True, stop=True)
                for h in range(H):
                    last = MM(pB[0][32:64, 256 + 32 * h:288 + 32 * h], Y[32:64, c * H + h, 32:64], Pb[32:64, h, 0:32], start=True, stop=True)
                last.then_inc(s["y32_ready"], 1)

            def p64(m, c):
                n = GROUP * m + c
                wait(pe, "y32_done", n + 1)
                wait(pe, "y32_done_v", n + 1)
                apart(pe)
                for h in range(H):
                    last = MM(pB[0][64:128, 64 * h:64 * h + 64], Y[0:64, c * H + h, 64:128], X[0:64, c * H + h, :], start=True, stop=True)
                last.then_inc(s["p64_ready"], 1)

            def y64(m, c):
                n = GROUP * m + c
                wait(pe, "p64_done", n + 1)
                apart(pe)
                for h in range(H):
                    last = MM(pB[1][0:64, 64 * h:64 * h + 64], Pb[64:128, h, :], Y[64:128, c * H + h, 64:128], start=True, stop=True)
                last.then_inc(s["y64_ready"], 1)

            def read(m, c):
                n = GROUP * m + c
                if c == 0:
                    wait(pe, "kkq_used", 4 * GROUP * (m + 1))
                    wait(pe, "s_kept", m + 1)
                wait(pe, "s_done", n)
                wait(pe, "w1_done", n)
                wait(pe, "t2_done", n)
                for dst, which, sem in ((pC[0], 1, "ks_ready"), (pC[1], 0, "s_read")):
                    for h in range(H):
                        last = MM(dst[:, DV * h:DV * h + DV], qk[:, h, which, c * P:(c + 1) * P], S[:, DV * h:DV * h + DV], start=True, stop=True)
                    last.then_inc(s[sem], 1)

            def solve(m, c):
                n = GROUP * m + c
                wait(pe, "r_done", n + 1)
                wait(pe, "y64_done", n + 1)
                for h in range(H):
                    last = MM(pC[0][:, DV * h:DV * h + DV], Y[:, c * H + h, :], R[:, DV * h:DV * h + DV], start=True, stop=True)
                last.then_inc(s["w_ready"], 1)

            def apply(m, c):
                n = GROUP * m + c
                wait(pe, "w2_done", n + 1)
                wait(pe, "ktok_done", 2 * n + 2)
                wait(pe, "nkq_done", m + 1)
                wait(pe, "fin_done", n)
                for h in range(H):
                    last = MM(pE[:, DV * h:DV * h + DV], ktok[:, c % 2, h, :], W2s[:, DV * h:DV * h + DV], start=True, stop=True)
                last.then_inc(s["sup_ready"], 1)
                wait(pe, "vr_done", GROUP * (m + 1))
                wait(pe, "o_sum", n)
                for h in range(H):
                    last = MM(pD[:, DV * h:DV * h + DV], AT[:, c * H + h, :], W1s[:, DV * h:DV * h + DV], start=True, stop=True)
                last.then_inc(s["aw_ready"], 1)

            def out(m, c):
                n = GROUP * m + c
                wait(pe, "o3_done", n + 1)
                wait(pe, "ktok_done", 2 * n + (4 if c + 1 < GROUP else 2))
                for j in range(VC):
                    last = TR(pA[:, 0, j * P:(j + 1) * P], O3[:, j * P:(j + 1) * P], ident[:, :])
                last.then_inc(s["otr_ready"], 1)
                wait(pe, "oT_done", n + 1)
                wait(pe, "s_done", n + 1)
                for j in range(VC):
                    last = MM(pE[:, 0:D], oT[:, j, :], wo[:, j, :], start=(j == 0), stop=(j == VC - 1))
                last.then_inc(s["wo_ready"], 1)

            steps = {"tokens": tokens, "p32": p32, "y32": y32, "p64": p64, "y64": y64, "read": read, "solve": solve, "apply": apply, "out": out}
            with pe.Fori(0, NG) as m:
                for k in range(PAIRS):
                    project(m, k)
                    if k >= 2:
                        if k % 2 == 0:
                            project_gate(m, k // 2 - 1)
                        norms(m, k - 2)
                for c in range(GROUP):
                    products(m, c)
                for step, c in scan_order():
                    if step in steps:
                        steps[step](m, c)

        @block.scalar
        def _(act):
            credits(act, "scalar")
            for q in out_stored:
                act.sem_inc(q, 16)
            act.wait_ge(params, 16 * NPARAM)
            A = nc.scalar.activation

            def tap3(m, k):
                wait(act, "proj_ready", PAIRS * m + k + 1)
                if k == 0:
                    wait(act, "s_read", GROUP * m)
                    wait(act, "ktok_ready", 2 * GROUP * m)
                    wait(act, "vtr_ready", GROUP * m)
                dst = conv_dst(k)
                for h in range(2):
                    last = A(dst[:, h, :], pA[:, h, :], ACT.Copy, scale=cw[:, 2 * k + h, TAPS - 1:TAPS])
                last.then_inc(s["tap3_done"], 1)

            def silu(m, k):
                wait(act, "taps_done", PAIRS * m + k + 1)
                A(conv_dst(k), conv_dst(k), ACT.Silu).then_inc(s["silu_done"], 1)

            def silu_gate(m, c):
                wait(act, "gate_ready", GROUP * m + c + 1)
                wait(act, "o3_done", GROUP * m)
                A(gate[:, c, :], pD[:, :], ACT.Silu).then_inc(s["gate_done"], 1)

            def decays(m, c):
                n = GROUP * m + c
                for g in range(2):
                    wait(act, "dexp_ready", 2 * n + g + 1)
                    wait(act, "kkq_used", 4 * n + 2 * g - 2)
                    A(dec[:, g], pB[g][:, :].rearrange("p (h n) -> p h n", h=GROUP), ACT.Exp).then_inc(s["dec_done"], 1)

            def tokens(m, c):
                n = GROUP * m + c
                wait(act, "sup_ready", n - 1)
                for g in range(2):
                    wait(act, "ktok_ready", 2 * n + g + 1)
                    A(ktok[:, c % 2, 4 * g:4 * g + 4, :], pA[:, g, :].rearrange("p (h n) -> p h n", h=4), ACT.Copy).then_inc(s["ktok_done"], 1)

            def p32(m, c):
                n = GROUP * m + c
                wait(act, "p32_ready", n + 1)
                wait(act, "y64_ready", n)
                A(Pb[32:64, :, 0:32], pB[0][32:64, 0:256].rearrange("p (h n) -> p h n", h=H), ACT.Copy).then_inc(s["p32_done"], 1)

            def y32(m, c):
                n = GROUP * m + c
                wait(act, "y32_ready", n + 1)
                A(Y[0:32, c * H:(c + 1) * H, 32:64], pB[0][0:32, 256:512].rearrange("p (h n) -> p h n", h=H), ACT.Copy, scale=-1.0)
                A(X[32:64, c * H:(c + 1) * H, 0:32], pB[0][32:64, 256:512].rearrange("p (h n) -> p h n", h=H), ACT.Copy, scale=-1.0).then_inc(s["y32_done"], 1)

            def p64(m, c):
                n = GROUP * m + c
                wait(act, "p64_ready", n + 1)
                A(Pb[64:128, :, :], pB[0][64:128, :].rearrange("p (h n) -> p h n", h=H), ACT.Copy).then_inc(s["p64_done"], 1)

            def y64(m, c):
                n = GROUP * m + c
                wait(act, "y64_ready", n + 1)
                A(Y[0:64, c * H:(c + 1) * H, 64:128], pB[1][0:64, :].rearrange("p (h n) -> p h n", h=H), ACT.Copy, scale=-1.0).then_inc(s["y64_done"], 1)

            def out(m, c):
                n = GROUP * m + c
                wait(act, "otr_ready", n + 1)
                wait(act, "wo_ready", n)
                A(oT[:, :, :], pA[:, 0, :].rearrange("p (j n) -> p j n", j=VC), ACT.Copy).then_inc(s["oT_done"], 1)
                wait(act, "fin_done", n + 1)
                act.dma_start(of_v[bass.ds(n, 1)].rearrange("o p d -> (o p) d"), ob[:, c % 2]).then_inc(out_stored[c % 2], 16)

            steps = {"tokens": tokens, "p32": p32, "y32": y32, "p64": p64, "y64": y64, "out": out}
            with act.Fori(0, NG) as m:
                for k in range(PAIRS):
                    tap3(m, k)
                    if k:
                        silu(m, k - 1)
                    if k >= 3 and k % 2:
                        silu_gate(m, (k - 3) // 2)
                silu(m, PAIRS - 1)
                for c in range(GROUP):
                    decays(m, c)
                for step, c in scan_order():
                    if step in steps:
                        steps[step](m, c)
            for q in out_stored:
                act.wait_ge(q, 16 * 2 * NG + 16)

        @block.vector
        def _(dve):
            credits(dve, "vector")
            dve.wait_ge(params, 16 * NPARAM)
            dve.wait_ge(consts, NCONST)
            V = nc.vector

            def taps(m, k):
                i = PAIRS * m + k
                wait(dve, "tap3_done", i + 1)
                dst = conv_dst(k)
                for d in range(1, TAPS):
                    for h in range(2):
                        if d > 1:
                            wait(dve, "tap", 6 * i + 2 * (d - 2) + h + 1)
                        V.scalar_tensor_tensor(out=dst[:, h, d:GT], in0=pA[:, h, 0:GT - d], scalar=cw[:, 2 * k + h, TAPS - 1 - d:TAPS - d],
                                               in1=dst[:, h, d:GT], op0=ALU.mult, op1=ALU.add).then_inc(s["tap"], 1)
                wait(dve, "corr_done", m + 1)
                V.tensor_copy(tails[:, 2 * k:2 * k + 2, :], pA[:, :, GT - 3:GT]).then_inc(s["tails_done"], 1)
                wait(dve, "tap", 6 * i + 6)
                V.tensor_tensor(dst[:, :, 0:3], dst[:, :, 0:3], corr[:, 2 * k:2 * k + 2, :], op=ALU.add).then_inc(s["taps_done"], 1)

            def stats(m):
                wait(dve, "norms_mm", QKP * m + QKP)
                wait(dve, "qscale_done", m)
                V.tensor_scalar(nkq[:, :, :, :], pE[:, 0:GROUP * 2 * H].rearrange("p (c a h) -> p c a h", c=GROUP, a=2), L2_EPS, None, ALU.add).then_inc(s["nkq_done"], 1)
                wait(dve, "nkq_done", m + 1)
                V.reciprocal(rn[:, :, :], nkq[:, :, 1, :]).then_inc(s["rn_done"], 1)
                wait(dve, "rn_done", m + 1)
                wait(dve, "mst_done", m + 1)
                V.tensor_tensor(eps[:, :, :], rn[:, :, :], mst[:, :, 0, :], op=ALU.mult).then_inc(s["eps_done"], 1)
                wait(dve, "eps_done", m + 1)
                wait(dve, "s_done", GROUP * m)
                V.tensor_scalar(S[:, :], S[:, :], goes_on[:, bass.ds(m, 1)], None, ALU.mult).then_inc(s["s_kept"], 1)

            def products(m, c):
                n = GROUP * m + c
                if c == 0:
                    wait(dve, "w_ready", GROUP * m)
                    wait(dve, "aw_ready", GROUP * m)
                    wait(dve, "knorm_done", m + 1)
                for g in range(4):
                    wait(dve, "kkq_ready", 4 * n + g + 1)
                    wait(dve, "dec_done", 2 * n + g // 2 + 1)
                    pk = pC[g % 2][:, :].rearrange("p (h a n) -> p h a n", h=2, a=2)
                    for h in range(2):
                        V.scalar_tensor_tensor(out=Y[:, c * H + 2 * g + h, :], in0=pk[:, h, 1, :], scalar=eps[:, c, 2 * g + h:2 * g + h + 1],
                                               in1=dec[:, g // 2, 2 * (g % 2) + h, :], op0=ALU.mult, op1=ALU.mult)
                    u = c * H + 2 * g
                    V.tensor_tensor(AT[:, u:u + 2, :], pk[:, :, 0, :], dec[:, g // 2, 2 * (g % 2):2 * (g % 2) + 2, :], op=ALU.mult).then_inc(s["kkq_used"], 1)
                wait(dve, "vtr_ready", n + 1)
                V.tensor_tensor(heads(vr[:, c, :]), heads(pD[:, :]), bc(knorm[:, c, :], 2, DV), op=ALU.mult).then_inc(s["vr_done"], 1)

            def invert(m):
                step = [0]
                per = 7 + 2 * 30

                def link(ins, hold=True):
                    step[0] += 1
                    ins.then_inc(s["elim"], 1)
                    if hold:
                        wait(dve, "elim", per * m + step[0])

                wait(dve, "kkq_used", 4 * GROUP * (m + 1))
                for a in range(NB):
                    r = slice(32 * a, 32 * a + 32)
                    link(V.transpose(lane_n[r, :, :], Y[r, :, r].rearrange("p u i -> p i u")), hold=(a == NB - 1))
                link(V.tensor_scalar(lane_x[:, :, :], lane_n[:, :, :], -1.0, None, ALU.mult))
                link(V.memset(lane_x[:, :, :].rearrange("p i j -> p (i j)")[:, 0:1024:33], 1.0))
                for j in range(1, 31):
                    tmp = lane_t[:, 0:(31 - j) * j].rearrange("p (i j) -> p i j", j=j)
                    link(V.tensor_tensor(tmp, lane_n[:, j + 1:32, j:j + 1].to_broadcast([P, 31 - j, j]),
                                         lane_x[:, j:j + 1, 0:j].to_broadcast([P, 31 - j, j]), op=ALU.mult))
                    link(V.tensor_tensor(lane_x[:, j + 1:32, 0:j], lane_x[:, j + 1:32, 0:j], tmp, op=ALU.subtract))
                for a in range(NB):
                    r = slice(32 * a, 32 * a + 32)
                    V.transpose(Y[r, :, r].rearrange("p u i -> p i u"), lane_x[r, :, :])
                for a in range(3):
                    r = slice(32 * a, 32 * a + 32)
                    k = 32 if a == 1 else 0
                    last = V.transpose(X[r, :, k:k + 32].rearrange("p u j -> p j u"), lane_x[r, :, :].rearrange("p i j -> p j i"))
                last.then_inc(s["elim"], 1)
                wait(dve, "elim", per * m + per)
                assert step[0] + 1 == per
                V.memset(X[0:32, :, 32:64], 0.0).then_inc(s["inv_done"], 1)

            def p32(m, c):
                n = GROUP * m + c
                wait(dve, "p32_ready", n + 1)
                V.tensor_copy(Pb[96:128, :, 0:32], pB[1][96:128, 0:256].rearrange("p (h n) -> p h n", h=H)).then_inc(s["p32_done_v"], 1)

            def y32(m, c):
                n = GROUP * m + c
                wait(dve, "y32_ready", n + 1)
                V.tensor_scalar(Y[64:96, c * H:(c + 1) * H, 96:128], pB[1][64:96, 256:512].rearrange("p (h n) -> p h n", h=H), -1.0, None, ALU.mult).then_inc(s["y32_done_v"], 1)

            def read(m, c):
                n = GROUP * m + c
                wait(dve, "ks_ready", n + 1)
                wait(dve, "fin_done", n)
                V.tensor_tensor(heads(ks[:, :]), heads(pC[0][:, :]), bc(mst[:, c, 2, :], 2, DV), op=ALU.mult).then_inc(s["ks_scaled"], 1)
                wait(dve, "ks_scaled", n + 1)
                wait(dve, "w_ready", n)
                V.tensor_tensor(R[:, :], vr[:, c, :], ks[:, :], op=ALU.subtract).then_inc(s["r_done"], 1)
                wait(dve, "s_read", n + 1)
                V.tensor_tensor(heads(t2[:, :]), heads(pC[1][:, :]), bc(mst[:, c, 2, :], 2, DV), op=ALU.mult).then_inc(s["t2_done"], 1)

            def solve(m, c):
                n = GROUP * m + c
                wait(dve, "w_ready", n + 1)
                wait(dve, "aw_ready", n)
                V.tensor_tensor(heads(W1s[:, :]), heads(pC[0][:, :]), bc(eps[:, c, :], 2, DV), op=ALU.mult).then_inc(s["w1_done"], 1)
                wait(dve, "w1_done", n + 1)
                V.tensor_tensor(heads(W2s[:, :]), heads(W1s[:, :]), bc(mst[:, c, 3, :], 2, DV), op=ALU.mult).then_inc(s["w2_done"], 1)

            def apply(m, c):
                n = GROUP * m + c
                wait(dve, "sup_ready", n + 1)
                wait(dve, "sd_done", n + 1)
                V.tensor_tensor(S[:, :], pE[:, :], Sd[:, :], op=ALU.add).then_inc(s["s_done"], 1)
                wait(dve, "aw_ready", n + 1)
                wait(dve, "t2_done", n + 1)
                V.tensor_tensor(O[:, :], pD[:, :], t2[:, :], op=ALU.add).then_inc(s["o_sum"], 1)

            def norm(m, c):
                n = GROUP * m + c
                wait(dve, "osq_done", n + 1)
                V.tensor_reduce(ss[:, :], heads(osq[:, :]), op=ALU.add, axis=AX_X).then_inc(s["ss_done"], 1)
                wait(dve, "f_done", n + 1)
                V.tensor_tensor(heads(O2[:, :]), heads(O[:, :]), bc(fo[:, :], 2, DV), op=ALU.mult).then_inc(s["o2_done"], 1)
                wait(dve, "o2_done", n + 1)
                wait(dve, "gatew_done", GROUP * m + c + 1)
                wait(dve, "otr_ready", n)
                V.tensor_tensor(O3[:, :], O2[:, :], gate[:, c, :], op=ALU.mult).then_inc(s["o3_done"], 1)

            def out(m, c):
                n = GROUP * m + c
                if c == 0:
                    dve.wait_ge(y_loaded, 2 * GROUP * 16 * (m + 1))
                    dve.wait_ge(xr_loaded, 16 * (m + 1))
                    wait(dve, "wt_done", m + 1)
                V.scalar_tensor_tensor(out=acc1[:, :], in0=yb[:, c, 0, :], scalar=wt[:, c, 0:1], in1=xr[:, c, :], op0=ALU.mult, op1=ALU.add).then_inc(s["acc1_done"], 1)
                wait(dve, "acc1_done", n + 1)
                V.scalar_tensor_tensor(out=acc2[:, :], in0=yb[:, c, 1, :], scalar=wt[:, c, 1:2], in1=acc1[:, :], op0=ALU.mult, op1=ALU.add).then_inc(s["acc2_done"], 1)
                wait(dve, "acc2_done", n + 1)
                wait(dve, "wo_ready", n + 1)
                dve.wait_ge(out_stored[c % 2], 16 * (2 * m + c // 2) + 16)
                V.tensor_tensor(ob[:, c % 2], pE[:, 0:D], acc2[:, :], op=ALU.add).then_inc(s["fin_done"], 1)

            steps = {"p32": p32, "y32": y32, "read": read, "solve": solve, "apply": apply, "norm": norm, "out": out}
            with dve.Fori(0, NG) as m:
                for k in range(PAIRS):
                    taps(m, k)
                stats(m)
                for c in range(GROUP):
                    products(m, c)
                invert(m)
                for step, c in scan_order():
                    if step in steps:
                        steps[step](m, c)

        @block.gpsimd
        def _(pool):
            credits(pool, "gpsimd")
            G = pool
            G.memset(identb[:, :], 0.0).then_inc(consts, 1)
            G.memset(negb[:, :, :], 0.0).then_inc(consts, 1)
            G.memset(half[:, :, :], 0.5).then_inc(consts, 1)
            G.memset(mhalf[:, :, :], -0.5).then_inc(consts, 1)
            G.memset(goes_on[:, :], 1.0).then_inc(consts, 1)
            G.memset(tails[:, :, :], 0.0).then_inc(consts, 1)
            G.memset(S[:, :], 0.0).then_inc(consts, 1)
            G.wait_ge(consts, 7)
            G.memset(goes_on[:, 0:NG:PER_BATCH], 0.0).then_inc(consts, 1)
            G.affine_select(out=identb[:, :], in_=identb[:, :], compare_op=ALU.not_equal, fill=1.0, base=0,
                            pattern=[[-1, P]], channel_multiplier=1).then_inc(consts, 1)
            G.affine_select(out=negb[:, :, :], in_=negb[:, :, :], compare_op=ALU.is_ge, fill=NEG, base=0,
                            pattern=[[0, GROUP], [1, P]], channel_multiplier=-1).then_inc(consts, 1)
            G.wait_ge(consts, NCONST)
            G.wait_ge(params, 16 * NPARAM)

            def begin(m):
                wait(G, "o3_done", GROUP * m)
                wait(G, "w2_done", GROUP * m)
                wait(G, "fin_done", GROUP * m)
                G.tensor_copy(mst[:, :, :, :], keep["stat"][:, bass.ds(GROUP * m, GROUP), :, :]).then_inc(s["mst_done"], 1)
                G.tensor_copy(wt[:, :, :], keep["wtop"][:, bass.ds(GROUP * m, GROUP), :]).then_inc(s["wt_done"], 1)
                G.tensor_copy(sidx[:, :, :], keep["slot"][:, bass.ds(GROUP * m, GROUP), :]).then_inc(s["sidx_done"], 1)
                wait(G, "tails_done", PAIRS * m)
                wait(G, "taps_done", PAIRS * m)
                G.tensor_tensor(tk[:, :, :], tails[:, :, :], bc(goes_on[:, bass.ds(m, 1)], 1, QKV).to_broadcast([P, QKV, 3]), op=ALU.mult).then_inc(s["tk_done"], 1)
                wait(G, "tk_done", m + 1)
                G.tensor_tensor(corr[:, :, 0:3], tk[:, :, 0:3], cw[:, :, 0:1].to_broadcast([P, QKV, 3]), op=ALU.mult).then_inc(s["corr_step"], 1)
                for d in (1, 2):
                    w = 3 - d
                    G.tensor_tensor(ctmp[:, :, 0:w], tk[:, :, d:3], cw[:, :, d:d + 1].to_broadcast([P, QKV, w]), op=ALU.mult).then_inc(s["corr_step"], 1)
                    wait(G, "corr_step", 4 * m + 2 * d)
                    last = G.tensor_tensor(corr[:, :, 0:w], corr[:, :, 0:w], ctmp[:, :, 0:w], op=ALU.add)
                    if d == 1:
                        last.then_inc(s["corr_step"], 1)
                        wait(G, "corr_step", 4 * m + 3)
                last.then_inc(s["corr_done"], 1)

            def gather(m):
                wait(G, "sidx_done", m + 1)
                apart(G)
                for c in range(GROUP):
                    for k in range(2):
                        G.indirect_dma_start(yb[:, c, k, :], None, yg_d[:, :], bass.IndirectOffsetOnAxis(ap=sidx[:, c, k:k + 1], axis=0)).then_inc(y_loaded, 16)

            def squares(m, k):
                wait(G, "silu_done", PAIRS * m + k + 1)
                wait(G, "norms_mm", QKP * m + k - 1)
                wait(G, "inv_done", m)
                G.tensor_tensor(sq[:, k % 2], conv_dst(k), conv_dst(k), op=ALU.mult).then_inc(s["sq_ready"], 1)

            def weigh_gate(m, c):
                wait(G, "gate_done", GROUP * m + c + 1)
                G.tensor_tensor(heads(gate[:, c, :]), heads(gate[:, c, :]), bc(nw[:, :], 1, H), op=ALU.mult).then_inc(s["gatew_done"], 1)

            def decay_sums(m, c):
                n = GROUP * m + c
                wait(G, "mst_done", m + 1)
                wait(G, "dexp_ready", 2 * n)
                G.tensor_tensor(qg[:, :, :], bc(tri_le[:, :], 1, H), bc(mst[:, c, 1, :], 2, P), op=ALU.mult).then_inc(s["qg_ready"], 1)

            def powers(m):
                wait(G, "nkq_done", m + 1)
                G.tensor_tensor(knorm[:, :, :], nkq[:, :, 1, :], half[:, :, :], op=ALU.pow).then_inc(s["knorm_done"], 1)
                G.tensor_tensor(qscale[:, :, :], nkq[:, :, 0, :], mhalf[:, :, :], op=ALU.pow).then_inc(s["qscale_done"], 1)

            def read(m, c):
                n = GROUP * m + c
                if c == 0:
                    wait(G, "s_kept", m + 1)
                wait(G, "s_done", n)
                G.tensor_tensor(heads(Sd[:, :]), heads(S[:, :]), bc(mst[:, c, 4, :], 2, DV), op=ALU.mult).then_inc(s["sd_done"], 1)

            def norm(m, c):
                n = GROUP * m + c
                wait(G, "o_sum", n + 1)
                wait(G, "ss_done", n)
                G.tensor_tensor(osq[:, :], O[:, :], O[:, :], op=ALU.mult).then_inc(s["osq_done"], 1)
                wait(G, "ss_done", n + 1)
                wait(G, "qscale_done", m + 1)
                G.tensor_tensor(f1[:, :], ss[:, :], qscale[:, c, :], op=ALU.mult).then_inc(s["f_step"], 1)
                wait(G, "f_step", 4 * n + 1)
                G.tensor_tensor(f2[:, :], f1[:, :], qscale[:, c, :], op=ALU.mult).then_inc(s["f_step"], 1)
                wait(G, "f_step", 4 * n + 2)
                apart(G)
                G.tensor_scalar(f3[:, :], f2[:, :], 1.0 / (DK * DV), RMS_EPS, ALU.mult, ALU.add).then_inc(s["f_step"], 1)
                wait(G, "f_step", 4 * n + 3)
                G.tensor_tensor(f4[:, :], f3[:, :], mhalf[:, 0, :], op=ALU.pow).then_inc(s["f_step"], 1)
                wait(G, "f_step", 4 * n + 4)
                wait(G, "o2_done", n)
                apart(G)
                G.tensor_tensor(f1[:, :], f4[:, :], qscale[:, c, :], op=ALU.mult).then_inc(s["f5_done"], 1)
                wait(G, "f5_done", n + 1)
                apart(G)
                G.tensor_scalar(fo[:, :], f1[:, :], DK ** -0.5, None, ALU.mult).then_inc(s["f_done"], 1)

            steps = {"read": read, "norm": norm}
            with G.Fori(0, NG) as m:
                begin(m)
                for k in range(QKP):
                    squares(m, k)
                    if k % 2:
                        weigh_gate(m, k // 2)
                gather(m)
                powers(m)
                for c in range(GROUP):
                    decay_sums(m, c)
                for step, c in scan_order():
                    if step in steps:
                        steps[step](m, c)


_INS = ["L0_attn_x", "L0_attn_Wq", "L0_attn_Wk", "L0_attn_Wv", "L0_attn_conv_q", "L0_attn_conv_k", "L0_attn_conv_v",
        "L0_attn_Wb", "L0_attn_Wa", "L0_attn_A_log", "L0_attn_dt_bias", "L0_attn_Wg", "L0_attn_norm_w", "L0_attn_Wo",
        "L0_ffn_Wg", "L0_ffn_W1", "L0_ffn_b1", "L0_ffn_W2", "L0_ffn_b2"]


def kernel(**inputs):
    import numpy as _np
    import concourse.bacc as _bacc
    from concourse import mybir as _mybir
    from concourse.bass_utils import run_bass_kernel_spmd as _run

    nc = _bacc.Bacc("TRN2", target_bir_lowering=False, num_devices=1)
    arrays, args = {}, []
    for name in _INS:
        a = _np.ascontiguousarray(inputs[name])
        arrays[f"in_{name}_dram"] = a
        args.append(nc.dram_tensor(f"in_{name}_dram", a.shape, _mybir.dt.from_np(a.dtype), kind="ExternalInput").ap())
    out = nc.dram_tensor("out_dram", inputs["L0_attn_x"].shape, _mybir.dt.float32, kind="ExternalOutput").ap()
    build(nc, *args, out)
    r = _run(nc, [arrays], core_ids=[0])
    return r.results[0]["out_dram"]
```

```python
from contextlib import ExitStack

import concourse.bass as bass
from concourse import mybir

ALU = mybir.AluOpType
ACT = mybir.ActivationFunctionType
F32 = mybir.dt.float32
BF16 = mybir.dt.bfloat16
I32 = mybir.dt.int32
AX_X = mybir.AxisListType.X

P = 128
GROUP = 4
GT = GROUP * P
D = 256
DC = D // P
E = 8
HID = 512
HC = HID // P
H = 8
DK = 128
DV = 64
TAPS = 4
QKV = 2 * H + H * DV // P
VC = H * DV // P
SMALL = E + 2 * H
NEG = -30000.0
LN_EPS = 1e-5
L2_EPS = 1e-6
RMS_EPS = 1e-5
NSTAT = 5


def bc(ap, axis, n):
    ap = ap.unsqueeze(axis)
    shape = list(ap.shape)
    shape[axis] = n
    return ap.to_broadcast(shape)


def col(t, i):
    return t[:, bass.ds(i, 1)]


def build(nc, x, Wq, Wk, Wv, cq, ck, cv, Wb, Wa, A_log, dt_bias, Wg, norm_w, Wo, Wr, W1, b1, W2, b2, out):
    B, T, _ = x.shape
    N = B * T
    NT = N // P
    NG = N // GT
    MT = 2 * NT + E
    xf = x.rearrange("b t d -> (b t) d")
    of = out.rearrange("b t d -> (b t) d")
    xn_d = nc.dram_tensor("xn_rows", [N, D], F32, kind="Internal").ap()
    xnT_d = nc.dram_tensor("xn_cols", [P, DC, N], F32, kind="Internal").ap()
    xg_d = nc.dram_tensor("expert_in", [MT * P, D], F32, kind="Internal").ap()
    yg_d = nc.dram_tensor("expert_out", [MT * P, D], F32, kind="Internal").ap()
    dims = (B, T, N, NT, NG, MT)
    with ExitStack() as ctx:
        def sb(name, shape, dt=F32):
            return ctx.enter_context(nc.sbuf_tensor(name, shape, dt))

        keep = {
            "ident": sb("ident", [P, P]), "tri_le": sb("tri_le", [P, P]), "tri_gt": sb("tri_gt", [P, P]),
            "ones": sb("ones", [P, P]),
            "stat": sb("stat", [P, NT, NSTAT, H]),
            "slot": sb("slot", [P, NT, 2], I32),
            "wtop": sb("wtop", [P, NT, 2]),
            "tile_expert": sb("tile_expert", [1, MT], I32),
        }
        norm_and_route(nc, keep, dims, xf, Wr, Wb, Wa, A_log, dt_bias, xn_d, xnT_d, xg_d)
        experts(nc, keep, dims, W1, b1, W2, b2, xn_d, xg_d, yg_d)
        attention(nc, keep, dims, xf, Wq, Wk, Wv, cq, ck, cv, Wg, norm_w, Wo, xnT_d, yg_d, of)


def norm_and_route(nc, keep, dims, xf, Wr, Wb, Wa, A_log, dt_bias, xn_d, xnT_d, xg_d):
    B, T, N, NT, NG, MT = dims
    ident, tri_le, tri_gt, ones = keep["ident"], keep["tri_le"], keep["tri_gt"], keep["ones"]
    stat, slot, wtop, tile_expert = keep["stat"], keep["slot"], keep["wtop"], keep["tile_expert"]
    ZR = 8
    with ExitStack() as ctx:
        def sb(name, shape, dt=F32):
            return ctx.enter_context(nc.sbuf_tensor("route_" + name, shape, dt))

        def sem(name):
            return ctx.enter_context(nc.semaphore("route_" + name))

        zero = sb("zero", [P, ZR * D])
        w_small = sb("w_small", [P, DC, SMALL])
        alog = sb("alog", [P, H]); dtb = sb("dtb", [P, H]); expa = sb("expa", [P, H])
        tri_lt = sb("tri_lt", [P, P])
        x_in = sb("x_in", [P, 2, GROUP, D])
        xn = sb("xn", [P, 2, GROUP, D])
        xnT = sb("xnT", [P, 2, DC, GT])
        bnst = sb("bnst", [P, 2, GROUP, 6]); mv = sb("mv", [P, 2, GROUP, 2])
        var_eps = sb("var_eps", [P, 2, GROUP]); rstd = sb("rstd", [P, 2, GROUP])
        minus_half = sb("minus_half", [P, GROUP])
        lg = sb("lg", [P, NT, SMALL])
        psT = ctx.enter_context(nc.psum_tensor("route_psT", [P, 2, DC, GT], F32))
        psL = ctx.enter_context(nc.psum_tensor("route_psL", [P, 2, 512], F32))
        psR = ctx.enter_context(nc.psum_tensor("route_psR", [P, 2, 512], F32))
        big = [sb(f"route{i}", [P, NT, E]) for i in range(8)]
        r1 = [sb(f"row{i}", [P, NT]) for i in range(6)]
        e8 = [sb(f"per_expert{i}", [P, E]) for i in range(6)]
        e8i = sb("per_expert_int", [P, E], I32)
        rank_w = sb("rank_w", [P, E])
        jt = sb("jt", [1, MT]); jcmp = sb("jcmp", [1, MT, E]); jsum = sb("jsum", [1, MT])

        consts, params, xn_made = sem("consts"), sem("params"), sem("xn_made")
        x_loaded = [sem(f"x_loaded{par}") for par in range(2)]
        bn_done, aggr_done, ve_done, rstd_done = (sem(n) for n in ("bn_done", "aggr_done", "ve_done", "rstd_done"))
        tr_done, xnT_done, lg_mm, lg_done = sem("tr_done"), sem("xnT_done"), sem("lg_mm"), sem("lg_done")
        rows_stored = [sem(f"rows_stored{par}") for par in range(2)]
        cols_stored = [sem(f"cols_stored{par}") for par in range(2)]
        zeroed, passed = sem("zeroed"), sem("passed")
        step, a_step, mm_step, p_step = sem("route_step"), sem("route_exp"), sem("route_mm"), sem("route_iota")
        block = ctx.enter_context(nc.Block())
        xt_v = xf.rearrange("(g a p) d -> g p a d", a=GROUP, p=P)
        xn_v = xn_d.rearrange("(g a p) d -> g p a d", a=GROUP, p=P)
        NCONST = 12
        counts = {}

        @block.sync
        def _(sp):
            sp.dma_start(w_small[:, :, 0:E], Wr.rearrange("(c p) e -> p c e", p=P)).then_inc(params, 16)
            sp.dma_start(w_small[:, :, E:E + H], Wb.rearrange("(c p) e -> p c e", p=P)).then_inc(params, 16)
            sp.dma_start(w_small[:, :, E + H:SMALL], Wa.rearrange("(c p) e -> p c e", p=P)).then_inc(params, 16)
            sp.dma_start(alog[:, :], A_log.rearrange("(a h) -> a h", a=1).to_broadcast([P, H])).then_inc(params, 16)
            sp.dma_start(dtb[:, :], dt_bias.rearrange("(a h) -> a h", a=1).to_broadcast([P, H])).then_inc(params, 16)
            with sp.Fori(0, NG // 2) as i:
                for par in range(2):
                    g = 2 * i + par
                    sp.wait_ge(xn_made, 4 * g + 4)
                    sp.dma_start(x_in[:, par], xt_v[bass.ds(g, 1)].rearrange("o p a d -> (o p) a d")).then_inc(x_loaded[par], 16)

        @block.gpsimd
        def _(pool):
            pool.memset(zero[:, :], 0.0).then_inc(consts, 1)
            pool.memset(ident[:, :], 0.0).then_inc(consts, 1)
            pool.memset(ones[:, :], 1.0).then_inc(consts, 1)
            pool.memset(minus_half[:, :], -0.5).then_inc(consts, 1)
            pool.wait_ge(consts, 4)
            pool.affine_select(out=ident[:, :], in_=ident[:, :], compare_op=ALU.not_equal, fill=1.0, base=0,
                               pattern=[[-1, P]], channel_multiplier=1).then_inc(consts, 1)
            pool.affine_select(out=tri_le[:, :], in_=ones[:, :], compare_op=ALU.is_ge, fill=0.0, base=0,
                               pattern=[[1, P]], channel_multiplier=-1).then_inc(consts, 1)
            pool.affine_select(out=tri_lt[:, :], in_=ones[:, :], compare_op=ALU.is_gt, fill=0.0, base=0,
                               pattern=[[1, P]], channel_multiplier=-1).then_inc(consts, 1)
            pool.affine_select(out=tri_gt[:, :], in_=ones[:, :], compare_op=ALU.is_gt, fill=0.0, base=0,
                               pattern=[[-1, P]], channel_multiplier=1).then_inc(consts, 1)
            pool.iota(e8i[:, :], pattern=[[-1, E]], base=E, channel_multiplier=0).then_inc(consts, 1)
            pool.wait_ge(consts, 9)
            pool.tensor_copy(rank_w[:, :], e8i[:, :]).then_inc(consts, 1)
            pool.iota(jcmp[0:1, :, 0].bitcast(I32), pattern=[[1, MT]], base=0, channel_multiplier=0).then_inc(consts, 1)
            pool.wait_ge(consts, 11)
            pool.tensor_copy(jt[0:1, :], jcmp[0:1, :, 0].bitcast(I32)).then_inc(consts, 1)
            for r in range(MT // ZR):
                pool.dma_start(xg_d[r * ZR * P:(r + 1) * ZR * P, :].rearrange("(p r) d -> p (r d)", p=P), zero[:, :]).then_inc(zeroed, 16)
            with pool.Fori(0, NG // 2) as i:
                for par in range(2):
                    pool.wait_ge(ve_done, 2 * i + par + 1)
                    pool.tensor_tensor(rstd[:, par], var_eps[:, par], minus_half[:, :], op=ALU.pow).then_inc(rstd_done, 1)
            pool.wait_ge(zeroed, 16 * (MT // ZR))

        @block.vector
        def _(dve):
            dve.sem_inc(xn_made, 2 * GROUP)
            dve.sem_inc(lg_done, 2)
            dve.sem_inc(xnT_done, 4)
            with dve.Fori(0, NG // 2) as i:
                for par in range(2):
                    g = 2 * i + par
                    dve.wait_ge(x_loaded[par], 16 * i + 16)
                    for a in range(GROUP):
                        nc.vector.bn_stats(bnst[:, par, a], x_in[:, par, a]).then_inc(bn_done, 1)
                    for a in range(GROUP):
                        dve.wait_ge(bn_done, 4 * g + a + 1)
                        dve.sem_inc(passed, 1)
                        nc.vector.bn_aggr(mv[:, par, a], bnst[:, par, a]).then_inc(aggr_done, 1)
                    dve.wait_ge(aggr_done, 4 * g + 4)
                    nc.vector.tensor_scalar(var_eps[:, par], mv[:, par, :, 1], LN_EPS, None, ALU.add).then_inc(ve_done, 1)
                    dve.wait_ge(rstd_done, g + 1)
                    dve.wait_ge(rows_stored[par], 16 * i + 16)
                    dve.wait_ge(tr_done, g + 1)
                    for a in range(GROUP):
                        nc.vector.tensor_scalar(xn[:, par, a], x_in[:, par, a], mv[:, par, a, 0:1], rstd[:, par, a:a + 1],
                                                ALU.subtract, ALU.mult).then_inc(xn_made, 1)
                    dve.wait_ge(tr_done, g + 3)
                    dve.wait_ge(cols_stored[par], 16 * i + 16)
                    nc.vector.tensor_copy(xnT[:, par, 1], psT[:, par, 1]).then_inc(xnT_done, 1)
                    dve.wait_ge(lg_mm, g + 1)
                    nc.vector.tensor_scalar(lg[:, bass.ds(4 * g, GROUP), :], psL[:, par, 0:GROUP * SMALL].rearrange("p (a s) -> p a s", a=GROUP),
                                            1.0, None, ALU.mult).then_inc(lg_done, 1)
            n = [0]

            def link(ins):
                n[0] += 1
                ins.then_inc(step, 1)
                dve.wait_ge(step, n[0])

            V = nc.vector
            dve.wait_ge(lg_done, NG + 2)
            L = lg[:, :, 0:E]
            oh1, cand, oh2, l2, mask, ex, cnt, pos = big
            m1, m2, pick, esum, w1s, dd = r1
            rw = bc(rank_w[:, :], 1, NT)

            def onehot(dst, src, top):
                link(V.tensor_reduce(top[:, :], src, op=ALU.max, axis=AX_X))
                link(V.tensor_tensor(cand[:, :, :], src, bc(top[:, :], 2, E), op=ALU.is_equal))
                link(V.tensor_tensor(cand[:, :, :], cand[:, :, :], rw, op=ALU.mult))
                link(V.tensor_reduce(pick[:, :], cand[:, :, :], op=ALU.max, axis=AX_X))
                link(V.tensor_tensor(dst[:, :, :], cand[:, :, :], bc(pick[:, :], 2, E), op=ALU.is_equal))

            onehot(oh1, L, m1)
            link(V.scalar_tensor_tensor(out=l2[:, :, :], in0=oh1[:, :, :], scalar=-3.0e38, in1=L, op0=ALU.mult, op1=ALU.add))
            onehot(oh2, l2[:, :, :], m2)
            link(V.tensor_tensor(dd[:, :], m2[:, :], m1[:, :], op=ALU.subtract))
            link(V.tensor_tensor(mask[:, :, :], oh1[:, :, :], oh2[:, :, :], op=ALU.add))
            mask_at = n[0]
            dve.wait_ge(a_step, 1)
            link(V.tensor_scalar(esum[:, :], w1s[:, :], 1.0, None, ALU.add))
            link(V.reciprocal(pick[:, :], esum[:, :]))
            link(V.tensor_copy(wtop[:, :, 0], pick[:, :]))
            link(V.tensor_tensor(wtop[:, :, 1], pick[:, :], w1s[:, :], op=ALU.mult))
            dve.wait_ge(mm_step, 1)
            link(V.tensor_copy(cnt[:, :, :], psR[:, 1, 0:NT * E].rearrange("p (t e) -> p t e", e=E)))
            link(V.memset(l2[:, :, :], 0.0))
            for e in range(E):
                link(V.tensor_tensor_scan(out=ex[:, :, e], data0=cnt[:, :, e], data1=l2[:, :, e], initial=0.0,
                                          op0=ALU.add, op1=ALU.add))
            tot, tiles_f, end, base, zer8, tmp8 = e8
            link(V.tensor_scalar(tot[:, :], ex[:, NT - 1, :], float(P - 1), None, ALU.add))
            link(V.tensor_copy(e8i[:, :], tot[:, :]))
            link(V.tensor_scalar(e8i[:, :], e8i[:, :], 7, None, ALU.arith_shift_right))
            link(V.tensor_copy(tiles_f[:, :], e8i[:, :]))
            link(V.memset(zer8[:, :], 0.0))
            link(V.tensor_tensor_scan(out=end[:, :], data0=tiles_f[:, :], data1=zer8[:, :], initial=0.0, op0=ALU.add, op1=ALU.add))
            link(V.tensor_tensor(base[:, :], end[:, :], tiles_f[:, :], op=ALU.subtract))
            link(V.tensor_scalar(base[:, :], base[:, :], float(P), None, ALU.mult))
            link(V.tensor_tensor(ex[:, :, :], ex[:, :, :], cnt[:, :, :], op=ALU.subtract))
            link(V.tensor_tensor(pos[:, :, :], ex[:, :, :], psR[:, 0, 0:NT * E].rearrange("p (t e) -> p t e", e=E), op=ALU.add))
            link(V.tensor_tensor(pos[:, :, :], pos[:, :, :], bc(base[:, :], 1, NT), op=ALU.add))
            for k, oh in enumerate((oh1, oh2)):
                link(V.tensor_tensor(cand[:, :, :], pos[:, :, :], oh[:, :, :], op=ALU.mult))
                link(V.tensor_reduce(m1[:, :], cand[:, :, :], op=ALU.add, axis=AX_X))
                link(V.tensor_copy(slot[:, :, k], m1[:, :]))
            link(V.tensor_tensor(jcmp[0:1, :, :], bc(jt[0:1, :], 2, E), bc(end[0:1, :], 1, MT), op=ALU.is_ge))
            link(V.tensor_reduce(jsum[0:1, :], jcmp[0:1, :, :], op=ALU.add, axis=AX_X))
            link(V.tensor_scalar(jsum[0:1, :], jsum[0:1, :], float(E - 1), None, ALU.min))
            link(V.tensor_copy(tile_expert[0:1, :], jsum[0:1, :]))
            a_in, u, s, s2, acc, ab = (t for t in (oh1, cand, oh2, l2, mask, ex))
            link(V.tensor_tensor(a_in[:, :, :], lg[:, :, E + H:SMALL], bc(dtb[:, :], 1, NT), op=ALU.add))
            link(V.tensor_scalar(ab[:, :, :], a_in[:, :, :], -1.0, None, ALU.mult))
            link(V.tensor_tensor(ab[:, :, :], a_in[:, :, :], ab[:, :, :], op=ALU.min))
            ab_at = n[0]
            dve.wait_ge(a_step, 4)
            link(V.tensor_scalar(s[:, :, :], u[:, :, :], 2.0, None, ALU.add))
            link(V.reciprocal(s[:, :, :], s[:, :, :]))
            link(V.tensor_tensor(s[:, :, :], s[:, :, :], u[:, :, :], op=ALU.mult))
            link(V.tensor_tensor(s2[:, :, :], s[:, :, :], s[:, :, :], op=ALU.mult))
            link(V.tensor_scalar(acc[:, :, :], s2[:, :, :], 1.0 / 17, 1.0 / 15, ALU.mult, ALU.add))
            for k in (13, 11, 9, 7, 5, 3, 1):
                link(V.tensor_tensor(acc[:, :, :], acc[:, :, :], s2[:, :, :], op=ALU.mult))
                link(V.tensor_scalar(acc[:, :, :], acc[:, :, :], 1.0 / k, None, ALU.add))
            link(V.tensor_tensor(acc[:, :, :], acc[:, :, :], s[:, :, :], op=ALU.mult))
            link(V.tensor_scalar(a_in[:, :, :], a_in[:, :, :], 0.0, None, ALU.max))
            link(V.scalar_tensor_tensor(out=acc[:, :, :], in0=acc[:, :, :], scalar=2.0, in1=a_in[:, :, :], op0=ALU.mult, op1=ALU.add))
            link(V.scalar_tensor_tensor(out=stat[:, :, 1, :], in0=acc[:, :, :], scalar=-1.0, in1=bc(expa[:, :], 1, NT), op0=ALU.mult, op1=ALU.mult))
            g_at = n[0]
            link(V.tensor_scalar(pos[:, :, :], pos[:, :, :], 1.0, None, ALU.add))
            link(V.reciprocal(pos[:, :, :], pos[:, :, :]))
            link(V.tensor_copy(stat[:, :, 0, :], pos[:, :, :]))
            counts["mask"], counts["ab"], counts["g"] = mask_at, ab_at, g_at
            counts["end"] = n[0]

        @block.scalar
        def _(act):
            act.wait_ge(params, 80)
            with act.Fori(0, NG // 2) as i:
                for par in range(2):
                    g = 2 * i + par
                    act.wait_ge(xn_made, 4 * g + 12)
                    act.dma_start(xn_v[bass.ds(g, 1)].rearrange("o p a d -> (o p) a d"), xn[:, par]).then_inc(rows_stored[par], 16)
                    act.wait_ge(tr_done, g + 3)
                    act.wait_ge(cols_stored[par], 16 * i + 16)
                    nc.scalar.activation(xnT[:, par, 0], psT[:, par, 0], ACT.Copy).then_inc(xnT_done, 1)
                    act.wait_ge(xnT_done, 2 * g + 6)
                    act.dma_start(xnT_d[:, :, bass.ds(g * GT, GT)], xnT[:, par]).then_inc(cols_stored[par], 16)
            m2_m1, w1s = r1[5], r1[4]
            act.wait_ge(step, counts["mask"])
            nc.scalar.activation(w1s[:, :], m2_m1[:, :], ACT.Exp).then_inc(a_step, 1)
            nc.scalar.activation(expa[:, :], alog[:, :], ACT.Exp).then_inc(a_step, 1)
            act.wait_ge(step, counts["ab"])
            nc.scalar.activation(big[1][:, :, :], big[5][:, :, :], ACT.Exp).then_inc(a_step, 1)
            nc.scalar.activation(big[7][:, :, :], lg[:, :, E:E + H], ACT.Exp, scale=-1.0).then_inc(a_step, 1)
            for k in range(3):
                act.wait_ge(mm_step, 2 + k)
                src = (psR[:, 0], psR[:, 1], psL[:, 0])[k]
                nc.scalar.activation(stat[:, :, 2 + k, :], src[:, 0:NT * H].rearrange("p (t h) -> p t h", h=H), ACT.Exp).then_inc(a_step, 1)
            for par in range(2):
                act.wait_ge(rows_stored[par], 8 * NG + 16)
            for par in range(2):
                act.wait_ge(cols_stored[par], 8 * NG + 16)

        @block.tensor
        def _(pe):
            pe.sem_inc(tr_done, 2)
            for par in range(2):
                pe.sem_inc(rows_stored[par], 16)
            for par in range(2):
                pe.sem_inc(cols_stored[par], 16)
            pe.wait_ge(params, 80)
            pe.wait_ge(consts, NCONST)
            with pe.Fori(0, NG // 2) as i:
                for par in range(2):
                    g = 2 * i + par
                    pe.wait_ge(xn_made, 4 * g + 12)
                    pe.wait_ge(xnT_done, 2 * g + 2)
                    for c in range(DC):
                        for a in range(GROUP):
                            last = nc.tensor.transpose(psT[:, par, c, a * P:(a + 1) * P], xn[:, par, a, c * P:(c + 1) * P], ident[:, :])
                    last.then_inc(tr_done, 1)
                    pe.wait_ge(xnT_done, 2 * g + 6)
                    pe.wait_ge(lg_done, g + 1)
                    for a in range(GROUP):
                        for c in range(DC):
                            last = nc.tensor.matmul(psL[:, par, a * SMALL:(a + 1) * SMALL], xnT[:, par, c, a * P:(a + 1) * P],
                                                    w_small[:, c, :], start=(c == 0), stop=(c == DC - 1))
                    last.then_inc(lg_mm, 1)
            pe.wait_ge(step, counts["mask"])
            mk = big[4][:, :, :].rearrange("p t e -> p (t e)")
            nc.tensor.matmul(psR[:, 0, 0:NT * E], tri_lt[:, :], mk, start=True, stop=True)
            nc.tensor.matmul(psR[:, 1, 0:NT * E], ones[:, :], mk, start=True, stop=True).then_inc(mm_step, 1)
            pe.wait_ge(step, counts["g"])
            for k, (dst, tri) in enumerate(((psR[:, 0], tri_le), (psR[:, 1], tri_gt), (psL[:, 0], ones))):
                nc.tensor.matmul(dst[:, 0:NT * H], tri[:, :], stat[:, :, 1, :], start=True, stop=True).then_inc(mm_step, 1)


def experts(nc, keep, dims, W1, b1, W2, b2, xn_d, xg_d, yg_d):
    B, T, N, NT, NG, MT = dims
    ident, slot, tile_expert = keep["ident"], keep["slot"], keep["tile_expert"]
    with ExitStack() as ctx:
        def sb(name, shape, dt=F32):
            return ctx.enter_context(nc.sbuf_tensor("moe_" + name, shape, dt))

        def pair(name):
            return [ctx.enter_context(nc.psum_tensor(f"moe_{name}{i}", [P, 512], F32)) for i in range(2)]

        def sem(name):
            return ctx.enter_context(nc.semaphore("moe_" + name))

        w1 = sb("w1", [P, E, DC, HID]); w2 = sb("w2", [P, E, HC, D])
        b1b = sb("b1b", [P, E, HID]); b2b = sb("b2b", [P, E, D])
        rows = sb("rows", [P, 2, GROUP, D]); idx = sb("idx", [P, 2, GROUP, 2], I32)
        xt = sb("xt", [P, 2, D]); xT = sb("xT", [P, 2, DC, P])
        h = sb("h", [P, 2, HID]); hT = sb("hT", [P, 2, HC, P]); y = sb("y", [P, 2, D])
        psX, psH, psHT, psY = pair("psX"), pair("psH"), pair("psHT"), pair("psY")

        weights = [sem(f"weights{i}") for i in range(4)]
        rows_loaded = [sem(f"rows_loaded{i}") for i in range(2)]
        scattered = [sem(f"scattered{i}") for i in range(2)]
        idx_copied, passed = sem("idx_copied"), sem("passed")
        x_loaded = [sem(f"tile_loaded{i}") for i in range(2)]
        y_stored = [sem(f"y_stored{i}") for i in range(2)]
        xtr, xT_done, h_mm, h_done, htr, hT_done, y_mm, y_done = (
            sem(n) for n in ("xtr", "xT_done", "h_mm", "h_done", "htr", "hT_done", "y_mm", "y_done"))
        block = ctx.enter_context(nc.Block())
        rows_v = xn_d.rearrange("(g a p) d -> g p a d", a=GROUP, p=P)
        xg_v = xg_d.rearrange("(t p) d -> t p d", p=P)
        yg_v = yg_d.rearrange("(t p) d -> t p d", p=P)

        def before(q, par):
            return (q, 0) if par else (q - 1, 1)

        def after(q, par):
            return (q + 1, 0) if par else (q, 1)

        def steps(eng, step):
            step(None, (0, 0), None)
            step((0, 0), (0, 1), None)
            step((0, 1), (1, 0), (0, 0))
            step((1, 0), (1, 1), (0, 1))
            with eng.Fori(1, MT // 2 - 1) as i:
                for tile in ((i, 1), (i + 1, 0)):
                    step(tile, after(*tile), before(*tile))
            last = (MT // 2 - 1, 1)
            step(last, None, before(*last))
            step(None, None, last)

        @block.sync
        def _(sp):
            sp.dma_start(w1[:, :, :, :], W1.rearrange("e (c p) n -> p e c n", p=P)).then_inc(weights[0], 16)
            for par in range(2):
                sp.dma_start(rows[:, par], rows_v[par]).then_inc(rows_loaded[par], 16)
            with sp.Fori(1, NG // 2) as i:
                for par in range(2):
                    sp.wait_ge(scattered[par], 2 * GROUP * 16 * i)
                    sp.dma_start(rows[:, par], rows_v[bass.ds(2 * i + par, 1)].rearrange("o p a d -> (o p) a d")).then_inc(rows_loaded[par], 16)
            for par in range(2):
                sp.wait_ge(scattered[par], 2 * GROUP * 16 * (NG // 2))
            with sp.Fori(0, MT // 2) as i:
                for par in range(2):
                    sp.wait_ge(xtr, 2 * i + par + 1)
                    sp.dma_start(xt[:, par], xg_v[bass.ds(2 * i + par, 1)].rearrange("o p d -> (o p) d")).then_inc(x_loaded[par], 16)

        @block.gpsimd
        def _(pool):
            pool.sem_inc(idx_copied, 1)

            def scatter(i):
                for par in range(2):
                    g = 2 * i + par
                    if not (isinstance(i, int) and i == 0):
                        pool.wait_ge(scattered[par], 2 * GROUP * 16 * i)
                    pool.tensor_copy(idx[:, par], slot[:, bass.ds(GROUP * g, GROUP), :]).then_inc(idx_copied, 1)
                    pool.wait_ge(rows_loaded[par], 16 * i + 16)
                    pool.wait_ge(idx_copied, g + 2)
                    pool.sem_inc(passed, 1)
                    for a in range(GROUP):
                        for k in range(2):
                            pool.indirect_dma_start(xg_d[:, :], bass.IndirectOffsetOnAxis(ap=idx[:, par, a, k:k + 1], axis=0),
                                                    rows[:, par, a], None).then_inc(scattered[par], 16)

            scatter(0)
            with pool.Fori(1, NG // 2) as i:
                scatter(i)
            with pool.Fori(0, MT // 2) as i:
                for par in range(2):
                    t = 2 * i + par
                    pool.wait_ge(y_done, t + 3)
                    pool.sem_inc(passed, 1)
                    pool.dma_start(yg_v[bass.ds(t, 1)].rearrange("o p d -> (o p) d"), y[:, par]).then_inc(y_stored[par], 16)
            for par in range(2):
                pool.wait_ge(y_stored[par], 8 * MT)

        @block.scalar
        def _(act):
            act.sem_inc(xT_done, 2)
            act.sem_inc(hT_done, 2)
            act.dma_start(w2[:, :, :, :], W2.rearrange("e (c p) n -> p e c n", p=P)).then_inc(weights[1], 16)
            act.dma_start(b1b[:, :, :], b1.rearrange("(o e) n -> o e n", o=1).to_broadcast([P, E, HID])).then_inc(weights[2], 16)
            act.dma_start(b2b[:, :, :], b2.rearrange("(o e) n -> o e n", o=1).to_broadcast([P, E, D])).then_inc(weights[3], 16)

            def step(cur, nxt, prev):
                if prev:
                    q, par = prev
                    t = 2 * q + par
                    act.wait_ge(htr, t + 3)
                    act.wait_ge(y_mm, t + 1)
                    nc.scalar.activation(hT[:, par], psHT[par][:, :].rearrange("p (c n) -> p c n", c=HC), ACT.Relu).then_inc(hT_done, 1)
                if nxt:
                    q, par = nxt
                    t = 2 * q + par
                    act.wait_ge(xtr, t + 3)
                    act.wait_ge(h_mm, t + 1)
                    nc.scalar.activation(xT[:, par], psX[par][:, 0:D].rearrange("p (c n) -> p c n", c=DC), ACT.Copy).then_inc(xT_done, 1)

            steps(act, step)

        @block.vector
        def _(dve):
            dve.sem_inc(h_done, 2)
            dve.sem_inc(y_done, 2)
            for w in weights[2:]:
                dve.wait_ge(w, 16)

            def step(cur, nxt, prev):
                if cur:
                    q, par = cur
                    t = 2 * q + par
                    e = dve.value_load(tile_expert[0:1, t:t + 1] if isinstance(t, int) else tile_expert[0:1, bass.ds(t, 1)], min_val=0, max_val=E - 1)
                    dve.wait_ge(h_mm, t + 3)
                    dve.wait_ge(htr, t + 1)
                    nc.vector.tensor_tensor(h[:, par], psH[par][:, :], b1b[:, bass.ds(e, 1), :].rearrange("p o n -> p (o n)"), op=ALU.add).then_inc(h_done, 1)
                if prev:
                    q, par = prev
                    t = 2 * q + par
                    e = dve.value_load(tile_expert[0:1, t:t + 1] if isinstance(t, int) else tile_expert[0:1, bass.ds(t, 1)], min_val=0, max_val=E - 1)
                    dve.wait_ge(y_mm, t + 3)
                    if not isinstance(q, int) or q > 0:
                        dve.wait_ge(y_stored[par], 16 * q)
                    nc.vector.tensor_tensor(y[:, par], psY[par][:, 0:D], b2b[:, bass.ds(e, 1), :].rearrange("p o n -> p (o n)"), op=ALU.add).then_inc(y_done, 1)

            steps(dve, step)

        @block.tensor
        def _(pe):
            for s in (xtr, h_mm, htr, y_mm):
                pe.sem_inc(s, 2)
            for w in weights[0:2]:
                pe.wait_ge(w, 16)

            def expert(t):
                return pe.value_load(tile_expert[0:1, t:t + 1] if isinstance(t, int) else tile_expert[0:1, bass.ds(t, 1)], min_val=0, max_val=E - 1)

            def step(cur, nxt, prev):
                if nxt:
                    q, par = nxt
                    t = 2 * q + par
                    pe.wait_ge(x_loaded[par], 16 * q + 16)
                    pe.wait_ge(xT_done, t + 1)
                    for c in range(DC):
                        last = nc.tensor.transpose(psX[par][:, c * P:(c + 1) * P], xt[:, par, c * P:(c + 1) * P], ident[:, :])
                    last.then_inc(xtr, 1)
                if prev:
                    q, par = prev
                    t = 2 * q + par
                    pe.wait_ge(h_done, t + 3)
                    pe.wait_ge(hT_done, t + 1)
                    for c in range(HC):
                        last = nc.tensor.transpose(psHT[par][:, c * P:(c + 1) * P], h[:, par, c * P:(c + 1) * P], ident[:, :])
                    last.then_inc(htr, 1)
                if cur:
                    q, par = cur
                    t = 2 * q + par
                    e = expert(t)
                    pe.wait_ge(xT_done, t + 3)
                    pe.wait_ge(h_done, t + 1)
                    for c in range(DC):
                        last = nc.tensor.matmul(psH[par][:, :], xT[:, par, c], w1[:, bass.ds(e, 1), c].rearrange("p o n -> p (o n)"),
                                                start=(c == 0), stop=(c == DC - 1))
                    last.then_inc(h_mm, 1)
                if prev:
                    q, par = prev
                    t = 2 * q + par
                    e = expert(t)
                    pe.wait_ge(hT_done, t + 3)
                    pe.wait_ge(y_done, t + 1)
                    for c in range(HC):
                        last = nc.tensor.matmul(psY[par][:, 0:D], hT[:, par, c], w2[:, bass.ds(e, 1), c].rearrange("p o n -> p (o n)"),
                                                start=(c == 0), stop=(c == HC - 1))
                    last.then_inc(y_mm, 1)

            steps(pe, step)


CREDIT = 4


def attention(nc, keep, dims, xf, Wq, Wk, Wv, cq, ck, cv, Wg, norm_w, Wo, xnT_d, yg_d, of):
    B, T, N, NT, NG, MT = dims
    ident, tri_le, tri_gt, ones = keep["ident"], keep["tri_le"], keep["tri_gt"], keep["ones"]
    U = GROUP * H
    NB = P // 32
    PAIRS = QKV // 2
    QKP = 2 * H // 2
    HV = H * DV
    PER_BATCH = T // GT
    assert U == 32
    with ExitStack() as ctx:
        def sb(name, shape, dt=F32):
            return ctx.enter_context(nc.sbuf_tensor("att_" + name, shape, dt))

        wqkv = sb("wqkv", [P, DC, QKV * P]); wg = sb("wg", [P, DC, HV]); wo = sb("wo", [P, VC, D])
        cw = sb("cw", [P, QKV, TAPS]); nw = sb("nw", [P, DV])
        identb = sb("identb", [P, P], BF16); negb = sb("negb", [P, GROUP, P], BF16)
        half = sb("half", [P, GROUP, H]); mhalf = sb("mhalf", [P, GROUP, H]); goes_on = sb("goes_on", [P, NG])
        xt = sb("xt", [P, DC, GT])
        qk = sb("qk", [P, H, 2, GT]); vc = sb("vc", [P, VC, GT]); sq = sb("sq", [P, 2, 2, GT])
        tails = sb("tails", [P, QKV, 3]); tk = sb("tk", [P, QKV, 3]); corr = sb("corr", [P, QKV, 3]); ctmp = sb("ctmp", [P, QKV, 3])
        gate = sb("gate", [P, GROUP, HV])
        mst = sb("mst", [P, GROUP, NSTAT, H]); bg = sb("beta_g", [P, GROUP, 2, H]); wt = sb("wt", [P, GROUP, 2]); sidx = sb("sidx", [P, GROUP, 2], I32)
        nkq = sb("nkq", [P, GROUP, 2, H]); rn = sb("rn", [P, GROUP, H]); eps = sb("eps", [P, GROUP, H])
        knorm = sb("knorm", [P, GROUP, H]); qscale = sb("qscale", [P, GROUP, H])
        qg = sb("qg", [P, H, P])
        Y = sb("Y", [P, U, P]); AT = sb("AT", [P, U, P]); X = sb("X", [P, U, 64])
        vr = sb("vr", [P, GROUP, HV]); ktok = sb("ktok", [P, 2, H, P])
        Pb = sb("Pb", [P, H, 64])
        S = sb("S", [P, HV]); Sd = sb("Sd", [P, HV])
        ks = sb("ks", [P, HV]); R = sb("R", [P, HV]); W1s = sb("Wp", [P, HV])
        t2 = sb("t2", [P, HV]); O = sb("O", [P, HV]); osq = sb("osq", [P, HV]); O3 = sb("O3", [P, HV])
        ss = sb("ss", [P, H]); f1 = sb("f1", [P, H]); f2 = sb("f2", [P, H]); f3 = sb("f3", [P, H]); f4 = sb("f4", [P, H]); fo = sb("fo", [P, H])
        oT = sb("oT", [P, VC, P]); yb = sb("yb", [P, GROUP, 2, D]); xr = sb("xr", [P, GROUP, D])
        ob = sb("ob", [P, 2, D])
        lane_n, lane_x = (vr[:, 2 * i:2 * i + 2].rearrange("p a (i j) -> p (a i) j", j=32) for i in range(2))
        lane_t = R[:, 0:256]

        pA = ctx.enter_context(nc.psum_tensor("att_psA", [P, 2, 512], F32))
        pB = ctx.enter_context(nc.psum_tensor("att_psB", [P, 2, 512], F32))
        pC = ctx.enter_context(nc.psum_tensor("att_psC", [P, 2, 512], F32))
        pD = ctx.enter_context(nc.psum_tensor("att_psD", [P, 512], F32))
        pE = ctx.enter_context(nc.psum_tensor("att_psE", [P, 512], F32))
        pair_bank = (pA, pC)

        names = {
            "tensor": "proj_ready gate_ready norms_mm dexp_ready kk_ready qk_ready vtr_ready ktok_ready p32_ready y32_ready "
                      "p64_ready y64_ready ks_ready s_read w_ready aw_ready sup_ready otr_ready wo_ready",
            "scalar": "tap3_done silu_done sq_ready gate_done dec_done ktok_done p32_done y32_done p64_done y64_done t2_done oT_done",
            "vector": "tap taps_done tails_done nk_done nq_done rn_done eps_done kk_used qk_used vr_done elim inv_done p32_done_v "
                      "y32_done_v ks_scaled r_done w1_done o_sum s_kept s_done ss_done o2_done o3_done "
                      "acc1_done acc2_done fin_done",
            "gpsimd": "bg_done mst_done wt_done sidx_done tk_done corr_step corr_done qg_ready gatew_done knorm_done "
                      "qscale_done sd_done osq_done f_step f5_done f_done",
        }
        s = {n: ctx.enter_context(nc.semaphore("att_" + n)) for group in names.values() for n in group.split()}
        params, consts = ctx.enter_context(nc.semaphore("att_params")), ctx.enter_context(nc.semaphore("att_consts"))
        xt_loaded, xr_loaded, y_loaded = (ctx.enter_context(nc.semaphore("att_" + n)) for n in ("xt_loaded", "xr_loaded", "y_loaded"))
        out_stored = [ctx.enter_context(nc.semaphore(f"att_out_stored{i}")) for i in range(2)]
        block = ctx.enter_context(nc.Block())
        passed = ctx.enter_context(nc.semaphore("att_passed"))
        NPARAM, NCONST = 9, 10

        def credits(eng, which):
            for n in names[which].split():
                eng.sem_inc(s[n], CREDIT)

        def wait(eng, name, count):
            eng.wait_ge(s[name], count + CREDIT)

        def apart(eng):
            eng.sem_inc(passed, 1)

        ORDER = list(range(H // 2, H)) + list(range(H // 2)) + list(range(H, PAIRS))

        def conv_dst(j):
            k = ORDER[j]
            if k < H // 2:
                return qk[:, 2 * k:2 * k + 2, 0, :]
            if k < H:
                return qk[:, 2 * k - H:2 * k - H + 2, 1, :]
            return vc[:, 2 * (k - H):2 * (k - H) + 2, :]

        def heads(ap):
            return ap.rearrange("p (h v) -> p h v", h=H)

        xt_v = xnT_d
        xr_v = xf.rearrange("(g a p) d -> g p a d", a=GROUP, p=P)
        of_v = of.rearrange("(t p) d -> t p d", p=P)

        @block.sync
        def _(sp):
            hq = H * DK
            sp.dma_start(wqkv[:, :, 0:hq], Wq.rearrange("(c p) n -> p c n", p=P)).then_inc(params, 16)
            sp.dma_start(wqkv[:, :, hq:2 * hq], Wk.rearrange("(c p) n -> p c n", p=P)).then_inc(params, 16)
            sp.dma_start(wqkv[:, :, 2 * hq:], Wv.rearrange("(c p) n -> p c n", p=P)).then_inc(params, 16)
            sp.dma_start(cw[:, 0:H, :], cq.rearrange("(c p) k -> p c k", p=P)).then_inc(params, 16)
            sp.dma_start(cw[:, H:2 * H, :], ck.rearrange("(c p) k -> p c k", p=P)).then_inc(params, 16)
            sp.dma_start(cw[:, 2 * H:QKV, :], cv.rearrange("(c p) k -> p c k", p=P)).then_inc(params, 16)
            sp.dma_start(wg[:, :, :], Wg.rearrange("(c p) n -> p c n", p=P)).then_inc(params, 16)
            sp.dma_start(wo[:, :, :], Wo.rearrange("(c p) n -> p c n", p=P)).then_inc(params, 16)
            sp.dma_start(nw[:, :], norm_w.rearrange("(a n) -> a n", a=1).to_broadcast([P, DV])).then_inc(params, 16)

            def load_columns(m):
                wait(sp, "proj_ready", PAIRS * m)
                wait(sp, "gate_ready", GROUP * m)
                sp.dma_start(xt[:, :, :], xt_v[:, :, bass.ds(m * GT, GT)]).then_inc(xt_loaded, 16)

            def load_rows(m):
                wait(sp, "fin_done", GROUP * m)
                sp.dma_start(xr[:, :, :], xr_v[bass.ds(m, 1)].rearrange("o p a d -> (o p) a d")).then_inc(xr_loaded, 16)

            def store(m, c):
                wait(sp, "fin_done", GROUP * m + c + 1)
                sp.dma_start(of_v[bass.ds(GROUP * m + c, 1)].rearrange("o p d -> (o p) d"), ob[:, c % 2]).then_inc(out_stored[c % 2], 16)

            load_columns(0)
            with sp.Fori(0, NG - 1) as m:
                load_rows(m)
                load_columns(m + 1)
                for c in range(GROUP):
                    store(m, c)
            load_rows(NG - 1)
            for c in range(GROUP):
                store(NG - 1, c)
            for q in out_stored:
                sp.wait_ge(q, 16 * 2 * NG + 16)

        @block.tensor
        def _(pe):
            credits(pe, "tensor")
            pe.wait_ge(params, 16 * NPARAM)
            pe.wait_ge(consts, NCONST)
            MM, TR = nc.tensor.matmul, nc.tensor.transpose

            def project(m, j):
                wait(pe, "taps_done", PAIRS * m + j - 1)
                if j == 0:
                    pe.wait_ge(xt_loaded, 16 * m + 16)
                    wait(pe, "ktok_done", 2 * GROUP * m)
                if j == 1:
                    wait(pe, "w1_done", GROUP * m)
                    wait(pe, "oT_done", GROUP * m)
                k = ORDER[j]
                for h in range(2):
                    for c in range(DC):
                        last = MM(pair_bank[j % 2][:, h, :], wqkv[:, c, (2 * k + h) * P:(2 * k + h + 1) * P], xt[:, c, :], start=(c == 0), stop=(c == DC - 1))
                last.then_inc(s["proj_ready"], 1)

            def project_gate(m, c):
                wait(pe, "o_sum", GROUP * m)
                wait(pe, "gate_done", GROUP * m + c)
                for d in range(DC):
                    last = MM(pD[:, :], xt[:, d, c * P:(c + 1) * P], wg[:, d, :], start=(d == 0), stop=(d == DC - 1))
                last.then_inc(s["gate_ready"], 1)

            def norms(m, j):
                wait(pe, "sq_ready", QKP * m + j + 1)
                wait(pe, "fin_done", GROUP * m)
                for h in range(2):
                    for c in range(GROUP):
                        at = c * 2 * H + 2 * ORDER[j] + h
                        last = MM(pE[:, at:at + 1], sq[:, j % 2, h, c * P:(c + 1) * P], ones[:, 0:1], start=True, stop=True)
                last.then_inc(s["norms_mm"], 1)

            def decays(m, c):
                n = GROUP * m + c
                for g in range(2):
                    wait(pe, "qg_ready", n + 1)
                    wait(pe, "dec_done", 2 * n + g - 1)
                    wait(pe, "y64_done", GROUP * m)
                    MM(pB[:, g, :], tri_gt[:, :], qg[:, 4 * g:4 * g + 4, :], start=True, stop=False)
                    MM(pB[:, g, :], identb[:, :], negb[:, :, :], start=False, stop=True).then_inc(s["dexp_ready"], 1)

            def keys(m, c):
                n = GROUP * m + c
                for g in range(2):
                    wait(pe, "silu_done", PAIRS * m + H // 2)
                    wait(pe, "dec_done", 2 * GROUP * (m + 1))
                    wait(pe, "kk_used", 2 * n + g - 1)
                    for h in range(4):
                        kc = qk[:, 4 * g + h, 1, c * P:(c + 1) * P]
                        last = MM(pB[:, g, h * P:(h + 1) * P], kc, kc, start=True, stop=True)
                    last.then_inc(s["kk_ready"], 1)

            def queries(m, c):
                n = GROUP * m + c
                wait(pe, "silu_done", PAIRS * m + H)
                wait(pe, "taps_done", PAIRS * m + PAIRS)
                wait(pe, "qk_used", n - 1)
                for h in range(H):
                    last = MM(pair_bank[c % 2][:, h // 4, (h % 4) * P:(h % 4 + 1) * P], qk[:, h, 1, c * P:(c + 1) * P], qk[:, h, 0, c * P:(c + 1) * P],
                              start=True, stop=True)
                last.then_inc(s["qk_ready"], 1)

            def values(m, c):
                n = GROUP * m + c
                wait(pe, "silu_done", PAIRS * m + PAIRS)
                wait(pe, "gate_done", GROUP * m + GROUP)
                wait(pe, "nq_done", m + 1)
                wait(pe, "vr_done", n - 1)
                for j in range(VC):
                    last = TR((pD, pE)[c % 2][:, j * P:(j + 1) * P], vc[:, j, c * P:(c + 1) * P], ident[:, :])
                last.then_inc(s["vtr_ready"], 1)

            def tokens(m, c):
                n = GROUP * m + c
                wait(pe, "ktok_done", 2 * n)
                wait(pe, "qk_used", GROUP * (m + 1))
                for g in range(2):
                    for h in range(4):
                        last = TR(pA[:, g, h * P:(h + 1) * P], qk[:, 4 * g + h, 1, c * P:(c + 1) * P], ident[:, :])
                    last.then_inc(s["ktok_ready"], 1)

            def p32(m, c):
                n = GROUP * m + c
                wait(pe, "inv_done", m + 1)
                wait(pe, "y64_done", n)
                apart(pe)
                for q in range(2):
                    a, b = 64 * q, 64 * q + 32
                    for h in range(H):
                        u = c * H + h
                        last = MM(pB[b:b + 32, q, 32 * h:32 * h + 32], Y[a:a + 32, u, b:b + 32], X[a:a + 32, u, 0:32], start=True, stop=True)
                last.then_inc(s["p32_ready"], 1)

            def y32(m, c):
                n = GROUP * m + c
                wait(pe, "p32_done", n + 1)
                wait(pe, "p32_done_v", n + 1)
                apart(pe)
                for q in range(2):
                    a, b = 64 * q, 64 * q + 32
                    for h in range(H):
                        u = c * H + h
                        last = MM(pB[a:a + 32, q, 256 + 32 * h:288 + 32 * h], Pb[b:b + 32, h, 0:32], Y[b:b + 32, u, b:b + 32], start=True, stop=True)
                for h in range(H):
                    last = MM(pB[32:64, 0, 256 + 32 * h:288 + 32 * h], Y[32:64, c * H + h, 32:64], Pb[32:64, h, 0:32], start=True, stop=True)
                last.then_inc(s["y32_ready"], 1)

            def p64(m, c):
                n = GROUP * m + c
                wait(pe, "y32_done", n + 1)
                wait(pe, "y32_done_v", n + 1)
                apart(pe)
                for h in range(H):
                    last = MM(pB[64:128, 0, 64 * h:64 * h + 64], Y[0:64, c * H + h, 64:128], X[0:64, c * H + h, :], start=True, stop=True)
                last.then_inc(s["p64_ready"], 1)

            def y64(m, c):
                n = GROUP * m + c
                wait(pe, "p64_done", n + 1)
                apart(pe)
                for h in range(H):
                    last = MM(pB[0:64, 1, 64 * h:64 * h + 64], Pb[64:128, h, :], Y[64:128, c * H + h, 64:128], start=True, stop=True)
                last.then_inc(s["y64_ready"], 1)

            def read(m, c):
                n = GROUP * m + c
                if c == 0:
                    wait(pe, "qk_used", GROUP * (m + 1))
                    wait(pe, "s_kept", m + 1)
                wait(pe, "s_done", n)
                wait(pe, "w1_done", n)
                for h in range(H):
                    last = MM(pC[:, 0, DV * h:DV * h + DV], qk[:, h, 1, c * P:(c + 1) * P], S[:, DV * h:DV * h + DV], start=True, stop=True)
                last.then_inc(s["ks_ready"], 1)
                wait(pe, "oT_done", n - 1)
                for h in range(H):
                    last = MM(pC[:, 1, DV * h:DV * h + DV], qk[:, h, 0, c * P:(c + 1) * P], S[:, DV * h:DV * h + DV], start=True, stop=True)
                last.then_inc(s["s_read"], 1)

            def solve(m, c):
                n = GROUP * m + c
                wait(pe, "r_done", n + 1)
                wait(pe, "y64_done", n + 1)
                for h in range(H):
                    last = MM(pC[:, 0, DV * h:DV * h + DV], Y[:, c * H + h, :], R[:, DV * h:DV * h + DV], start=True, stop=True)
                last.then_inc(s["w_ready"], 1)

            def apply(m, c):
                n = GROUP * m + c
                wait(pe, "w1_done", n + 1)
                wait(pe, "ktok_done", 2 * n + 2)
                wait(pe, "fin_done", n - 1 if c else n)
                wait(pe, "vr_done", GROUP * (m + 1))
                for h in range(H):
                    last = MM(pE[:, DV * h:DV * h + DV], ktok[:, c % 2, h, :], W1s[:, DV * h:DV * h + DV], start=True, stop=True)
                last.then_inc(s["sup_ready"], 1)
                wait(pe, "o_sum", n)
                for h in range(H):
                    last = MM(pD[:, DV * h:DV * h + DV], AT[:, c * H + h, :], W1s[:, DV * h:DV * h + DV], start=True, stop=True)
                last.then_inc(s["aw_ready"], 1)

            def turn(m, c):
                n = GROUP * m + c
                wait(pe, "o3_done", n + 1)
                wait(pe, "t2_done", n + (2 if c + 1 < GROUP else 1))
                for j in range(VC):
                    last = TR(pC[:, 1, j * P:(j + 1) * P], O3[:, j * P:(j + 1) * P], ident[:, :])
                last.then_inc(s["otr_ready"], 1)

            def out(m, c):
                n = GROUP * m + c
                wait(pe, "oT_done", n + 1)
                wait(pe, "s_done", n + (2 if c + 1 < GROUP else 1))
                wait(pe, "fin_done", n)
                for j in range(VC):
                    last = MM(pE[:, 0:D], oT[:, j, :], wo[:, j, :], start=(j == 0), stop=(j == VC - 1))
                last.then_inc(s["wo_ready"], 1)

            with pe.Fori(0, NG) as m:
                project(m, 0)
                decays(m, 0)
                project(m, 1)
                decays(m, 1)
                project(m, 2)
                decays(m, 2)
                decays(m, 3)
                project(m, 3)
                norms(m, 0)
                project(m, 4)
                norms(m, 1)
                norms(m, 2)
                project(m, 5)
                norms(m, 3)
                keys(m, 0)
                project(m, 6)
                keys(m, 1)
                keys(m, 2)
                keys(m, 3)
                project_gate(m, 0)
                norms(m, 4)
                project(m, 7)
                project_gate(m, 1)
                norms(m, 5)
                project(m, 8)
                project_gate(m, 2)
                norms(m, 6)
                project(m, 9)
                project_gate(m, 3)
                norms(m, 7)
                queries(m, 0)
                queries(m, 1)
                values(m, 0)
                values(m, 1)
                p32(m, 0)
                queries(m, 2)
                y32(m, 0)
                queries(m, 3)
                p64(m, 0)
                tokens(m, 0)
                y64(m, 0)
                values(m, 2)
                values(m, 3)
                for c in range(GROUP):
                    more = c + 1 < GROUP
                    read(m, c)
                    if more:
                        p32(m, c + 1)
                    solve(m, c)
                    if more:
                        y32(m, c + 1)
                    apply(m, c)
                    if more:
                        p64(m, c + 1)
                    if c:
                        turn(m, c - 1)
                    if more:
                        tokens(m, c + 1)
                        y64(m, c + 1)
                    if c:
                        out(m, c - 1)
                turn(m, GROUP - 1)
                out(m, GROUP - 1)

        @block.scalar
        def _(act):
            credits(act, "scalar")
            for q in out_stored:
                act.sem_inc(q, 16)
            act.wait_ge(params, 16 * NPARAM)
            A = nc.scalar.activation

            def tap3(m, j):
                wait(act, "proj_ready", PAIRS * m + j + 1)
                if j == 0:
                    wait(act, "s_read", GROUP * m)
                    wait(act, "ktok_ready", 2 * GROUP * m)
                    wait(act, "vtr_ready", GROUP * m)
                dst = conv_dst(j)
                for h in range(2):
                    last = A(dst[:, h, :], pair_bank[j % 2][:, h, :], ACT.Copy, scale=cw[:, 2 * ORDER[j] + h, TAPS - 1:TAPS])
                last.then_inc(s["tap3_done"], 1)

            def silu(m, j):
                wait(act, "taps_done", PAIRS * m + j + 1)
                A(conv_dst(j), conv_dst(j), ACT.Silu).then_inc(s["silu_done"], 1)

            def squares(m, j):
                wait(act, "silu_done", PAIRS * m + j + 1)
                wait(act, "norms_mm", QKP * m + j - 1)
                A(sq[:, j % 2], conv_dst(j), ACT.Square).then_inc(s["sq_ready"], 1)

            def silu_gate(m, c):
                wait(act, "gate_ready", GROUP * m + c + 1)
                wait(act, "o3_done", GROUP * m)
                A(gate[:, c, :], pD[:, :], ACT.Silu).then_inc(s["gate_done"], 1)

            def decays(m, c):
                n = GROUP * m + c
                for g in range(2):
                    wait(act, "dexp_ready", 2 * n + g + 1)
                    wait(act, "aw_ready", GROUP * m)
                    A(AT[:, c * H + 4 * g:c * H + 4 * g + 4, :], pB[:, g, :].rearrange("p (h n) -> p h n", h=4), ACT.Exp).then_inc(s["dec_done"], 1)

            def tokens(m, c):
                n = GROUP * m + c
                wait(act, "sup_ready", n - 1)
                wait(act, "mst_done", m + 1)
                for g in range(2):
                    wait(act, "ktok_ready", 2 * n + g + 1)
                    for h in range(4 * g, 4 * g + 4):
                        last = A(ktok[:, c % 2, h, :], pA[:, g, (h % 4) * P:(h % 4 + 1) * P], ACT.Copy, scale=mst[:, c, 3, h:h + 1])
                    last.then_inc(s["ktok_done"], 1)

            def p32(m, c):
                n = GROUP * m + c
                wait(act, "p32_ready", n + 1)
                wait(act, "y64_ready", n)
                A(Pb[32:64, :, 0:32], pB[32:64, 0, 0:256].rearrange("p (h n) -> p h n", h=H), ACT.Copy).then_inc(s["p32_done"], 1)

            def y32(m, c):
                n = GROUP * m + c
                wait(act, "y32_ready", n + 1)
                A(Y[0:32, c * H:(c + 1) * H, 32:64], pB[0:32, 0, 256:512].rearrange("p (h n) -> p h n", h=H), ACT.Copy, scale=-1.0)
                A(X[32:64, c * H:(c + 1) * H, 0:32], pB[32:64, 0, 256:512].rearrange("p (h n) -> p h n", h=H), ACT.Copy, scale=-1.0).then_inc(s["y32_done"], 1)

            def p64(m, c):
                n = GROUP * m + c
                wait(act, "p64_ready", n + 1)
                A(Pb[64:128, :, :], pB[64:128, 0, :].rearrange("p (h n) -> p h n", h=H), ACT.Copy).then_inc(s["p64_done"], 1)

            def y64(m, c):
                n = GROUP * m + c
                wait(act, "y64_ready", n + 1)
                A(Y[0:64, c * H:(c + 1) * H, 64:128], pB[0:64, 1, :].rearrange("p (h n) -> p h n", h=H), ACT.Copy, scale=-1.0).then_inc(s["y64_done"], 1)

            def read(m, c):
                n = GROUP * m + c
                wait(act, "s_read", n + 1)
                wait(act, "o_sum", n)
                for h in range(H):
                    last = A(t2[:, DV * h:DV * h + DV], pC[:, 1, DV * h:DV * h + DV], ACT.Copy, scale=mst[:, c, 2, h:h + 1])
                last.then_inc(s["t2_done"], 1)

            def turn(m, c):
                n = GROUP * m + c
                wait(act, "otr_ready", n + 1)
                wait(act, "wo_ready", n)
                A(oT[:, :, :], pC[:, 1, :].rearrange("p (j n) -> p j n", j=VC), ACT.Copy).then_inc(s["oT_done"], 1)

            with act.Fori(0, NG) as m:
                tap3(m, 0)
                decays(m, 0)
                tap3(m, 1)
                decays(m, 1)
                tap3(m, 2)
                decays(m, 2)
                decays(m, 3)
                silu(m, 0)
                squares(m, 0)
                tap3(m, 3)
                silu(m, 1)
                squares(m, 1)
                silu(m, 2)
                squares(m, 2)
                for j in range(4, PAIRS):
                    tap3(m, j)
                    silu(m, j - 1)
                    if j - 1 < QKP:
                        squares(m, j - 1)
                    if j >= 6:
                        silu_gate(m, j - 6)
                silu(m, PAIRS - 1)
                p32(m, 0)
                y32(m, 0)
                p64(m, 0)
                tokens(m, 0)
                y64(m, 0)
                for c in range(GROUP):
                    more = c + 1 < GROUP
                    read(m, c)
                    if more:
                        p32(m, c + 1)
                        y32(m, c + 1)
                        p64(m, c + 1)
                    if c:
                        turn(m, c - 1)
                    if more:
                        tokens(m, c + 1)
                        y64(m, c + 1)
                turn(m, GROUP - 1)

        @block.vector
        def _(dve):
            credits(dve, "vector")
            dve.wait_ge(params, 16 * NPARAM)
            dve.wait_ge(consts, NCONST)
            V = nc.vector

            def taps(m, j):
                i = PAIRS * m + j
                k = ORDER[j]
                wait(dve, "tap3_done", i + 1)
                dst, src = conv_dst(j), pair_bank[j % 2]
                for d in range(1, TAPS):
                    for h in range(2):
                        if d > 1:
                            wait(dve, "tap", 6 * i + 2 * (d - 2) + h + 1)
                        V.scalar_tensor_tensor(out=dst[:, h, d:GT], in0=src[:, h, 0:GT - d], scalar=cw[:, 2 * k + h, TAPS - 1 - d:TAPS - d],
                                               in1=dst[:, h, d:GT], op0=ALU.mult, op1=ALU.add).then_inc(s["tap"], 1)
                        yield
                wait(dve, "corr_done", m + 1)
                V.tensor_copy(tails[:, 2 * k:2 * k + 2, :], src[:, :, GT - 3:GT]).then_inc(s["tails_done"], 1)
                wait(dve, "tap", 6 * i + 6)
                V.tensor_tensor(dst[:, :, 0:3], dst[:, :, 0:3], corr[:, 2 * k:2 * k + 2, :], op=ALU.add).then_inc(s["taps_done"], 1)
                yield

            def key_stats(m):
                wait(dve, "norms_mm", QKP * m + H // 2)
                wait(dve, "knorm_done", m)
                V.tensor_scalar(nkq[:, :, 1, :], pE[:, 0:GROUP * 2 * H].rearrange("p (c a h) -> p c a h", c=GROUP, a=2)[:, :, 1], L2_EPS, None, ALU.add).then_inc(s["nk_done"], 1)
                wait(dve, "nk_done", m + 1)
                V.reciprocal(rn[:, :, :], nkq[:, :, 1, :]).then_inc(s["rn_done"], 1)
                wait(dve, "s_done", GROUP * m)
                V.tensor_scalar(S[:, :], S[:, :], goes_on[:, bass.ds(m, 1)], None, ALU.mult).then_inc(s["s_kept"], 1)
                wait(dve, "rn_done", m + 1)
                wait(dve, "bg_done", m + 1)
                wait(dve, "w1_done", GROUP * m)
                V.tensor_tensor(eps[:, :, :], rn[:, :, :], bg[:, :, 0, :], op=ALU.mult).then_inc(s["eps_done"], 1)

            def query_stats(m):
                wait(dve, "norms_mm", QKP * m + QKP)
                wait(dve, "qscale_done", m)
                V.tensor_scalar(nkq[:, :, 0, :], pE[:, 0:GROUP * 2 * H].rearrange("p (c a h) -> p c a h", c=GROUP, a=2)[:, :, 0], L2_EPS, None, ALU.add).then_inc(s["nq_done"], 1)

            def keys(m, c):
                n = GROUP * m + c
                wait(dve, "eps_done", m + 1)
                wait(dve, "w_ready", GROUP * m)
                for g in range(2):
                    wait(dve, "kk_ready", 2 * n + g + 1)
                    for h in range(4 * g, 4 * g + 4):
                        u = c * H + h
                        last = V.scalar_tensor_tensor(out=Y[:, u, :], in0=pB[:, g, (h % 4) * P:(h % 4 + 1) * P], scalar=eps[:, c, h:h + 1],
                                                      in1=AT[:, u, :], op0=ALU.mult, op1=ALU.mult)
                    last.then_inc(s["kk_used"], 1)

            def queries(m, c):
                n = GROUP * m + c
                wait(dve, "qk_ready", n + 1)
                wait(dve, "kk_used", 2 * GROUP * (m + 1))
                at = AT[:, c * H:(c + 1) * H, :]
                V.tensor_tensor(at, pair_bank[c % 2][:, :, :].rearrange("p g (h n) -> p (g h) n", n=P), at, op=ALU.mult).then_inc(s["qk_used"], 1)

            def values(m, c):
                n = GROUP * m + c
                wait(dve, "vtr_ready", n + 1)
                wait(dve, "knorm_done", m + 1)
                V.tensor_tensor(heads(vr[:, c, :]), heads((pD, pE)[c % 2][:, :]), bc(knorm[:, c, :], 2, DV), op=ALU.mult).then_inc(s["vr_done"], 1)

            def invert(m, others):
                step = [0]
                per = 7 + 2 * 30

                def link(ins, hold=True):
                    step[0] += 1
                    ins.then_inc(s["elim"], 1)
                    if hold:
                        if step[0] % 2:
                            next(others, None)
                        wait(dve, "elim", per * m + step[0])

                wait(dve, "kk_used", 2 * GROUP * (m + 1))
                wait(dve, "r_done", GROUP * m)
                for a in range(NB):
                    r = slice(32 * a, 32 * a + 32)
                    link(V.transpose(lane_n[r, :, :], Y[r, :, r].rearrange("p u i -> p i u")), hold=(a == NB - 1))
                link(V.tensor_scalar(lane_x[:, :, :], lane_n[:, :, :], -1.0, None, ALU.mult))
                link(V.memset(lane_x[:, :, :].rearrange("p i j -> p (i j)")[:, 0:1024:33], 1.0))
                for j in range(1, 31):
                    tmp = lane_t[:, 0:(31 - j) * j].rearrange("p (i j) -> p i j", j=j)
                    link(V.tensor_tensor(tmp, lane_n[:, j + 1:32, j:j + 1].to_broadcast([P, 31 - j, j]),
                                         lane_x[:, j:j + 1, 0:j].to_broadcast([P, 31 - j, j]), op=ALU.mult))
                    link(V.tensor_tensor(lane_x[:, j + 1:32, 0:j], lane_x[:, j + 1:32, 0:j], tmp, op=ALU.subtract))
                for a in range(NB):
                    r = slice(32 * a, 32 * a + 32)
                    V.transpose(Y[r, :, r].rearrange("p u i -> p i u"), lane_x[r, :, :])
                for a in range(3):
                    r = slice(32 * a, 32 * a + 32)
                    k = 32 if a == 1 else 0
                    last = V.transpose(X[r, :, k:k + 32].rearrange("p u j -> p j u"), lane_x[r, :, :].rearrange("p i j -> p j i"))
                last.then_inc(s["elim"], 1)
                wait(dve, "elim", per * m + per)
                assert step[0] + 1 == per
                V.memset(X[0:32, :, 32:64], 0.0).then_inc(s["inv_done"], 1)
                for _ in others:
                    pass

            def p32(m, c):
                n = GROUP * m + c
                wait(dve, "p32_ready", n + 1)
                V.tensor_copy(Pb[96:128, :, 0:32], pB[96:128, 1, 0:256].rearrange("p (h n) -> p h n", h=H)).then_inc(s["p32_done_v"], 1)

            def y32(m, c):
                n = GROUP * m + c
                wait(dve, "y32_ready", n + 1)
                V.tensor_scalar(Y[64:96, c * H:(c + 1) * H, 96:128], pB[64:96, 1, 256:512].rearrange("p (h n) -> p h n", h=H), -1.0, None, ALU.mult).then_inc(s["y32_done_v"], 1)

            def read(m, c):
                n = GROUP * m + c
                wait(dve, "ks_ready", n + 1)
                wait(dve, "mst_done", m + 1)
                wait(dve, "r_done", n)
                V.tensor_tensor(heads(ks[:, :]), heads(pC[:, 0, :]), bc(mst[:, c, 2, :], 2, DV), op=ALU.mult).then_inc(s["ks_scaled"], 1)
                wait(dve, "ks_scaled", n + 1)
                wait(dve, "vr_done", n + 1)
                wait(dve, "w_ready", n)
                V.tensor_tensor(R[:, :], vr[:, c, :], ks[:, :], op=ALU.subtract).then_inc(s["r_done"], 1)

            def solve(m, c):
                n = GROUP * m + c
                wait(dve, "w_ready", n + 1)
                wait(dve, "aw_ready", n)
                V.tensor_tensor(heads(W1s[:, :]), heads(pC[:, 0, :]), bc(eps[:, c, :], 2, DV), op=ALU.mult).then_inc(s["w1_done"], 1)

            def apply(m, c):
                n = GROUP * m + c
                wait(dve, "sup_ready", n + 1)
                wait(dve, "sd_done", n + 1)
                wait(dve, "s_read", n + 1)
                V.tensor_tensor(S[:, :], pE[:, :], Sd[:, :], op=ALU.add).then_inc(s["s_done"], 1)
                wait(dve, "aw_ready", n + 1)
                wait(dve, "t2_done", n + 1)
                wait(dve, "o3_done", n)
                V.tensor_tensor(O[:, :], pD[:, :], t2[:, :], op=ALU.add).then_inc(s["o_sum"], 1)

            def expert_rows(m, c):
                n = GROUP * m + c
                if c == 0:
                    dve.wait_ge(y_loaded, 2 * GROUP * 16 * (m + 1))
                    dve.wait_ge(xr_loaded, 16 * (m + 1))
                    wait(dve, "wt_done", m + 1)
                V.scalar_tensor_tensor(out=xr[:, c, :], in0=yb[:, c, 0, :], scalar=wt[:, c, 0:1], in1=xr[:, c, :], op0=ALU.mult, op1=ALU.add).then_inc(s["acc1_done"], 1)

            def expert_rows_2(m, c):
                n = GROUP * m + c
                wait(dve, "acc1_done", n + 1)
                V.scalar_tensor_tensor(out=xr[:, c, :], in0=yb[:, c, 1, :], scalar=wt[:, c, 1:2], in1=xr[:, c, :], op0=ALU.mult, op1=ALU.add).then_inc(s["acc2_done"], 1)

            def squares_sum(m, c):
                n = GROUP * m + c
                wait(dve, "osq_done", n + 1)
                wait(dve, "f_done", n)
                V.tensor_reduce(ss[:, :], heads(osq[:, :]), op=ALU.add, axis=AX_X).then_inc(s["ss_done"], 1)

            def scale_out(m, c):
                n = GROUP * m + c
                wait(dve, "f_done", n + 1)
                V.tensor_tensor(heads(O[:, :]), heads(O[:, :]), bc(fo[:, :], 2, DV), op=ALU.mult).then_inc(s["o2_done"], 1)
                wait(dve, "o2_done", n + 1)
                wait(dve, "gatew_done", n + 1)
                wait(dve, "otr_ready", n)
                V.tensor_tensor(O3[:, :], O[:, :], gate[:, c, :], op=ALU.mult).then_inc(s["o3_done"], 1)

            def out(m, c):
                n = GROUP * m + c
                wait(dve, "acc2_done", n + 1)
                wait(dve, "wo_ready", n + 1)
                dve.wait_ge(out_stored[c % 2], 16 * (2 * m + c // 2) + 16)
                V.tensor_tensor(ob[:, c % 2], pE[:, 0:D], xr[:, c, :], op=ALU.add).then_inc(s["fin_done"], 1)

            def late(m):
                for j in range(6, PAIRS):
                    yield from taps(m, j)
                query_stats(m)
                yield
                for c in range(2):
                    queries(m, c)
                    yield

            with dve.Fori(0, NG) as m:
                for j in range(5):
                    for _ in taps(m, j):
                        pass
                key_stats(m)
                keys(m, 0)
                for _ in taps(m, 5):
                    pass
                for c in range(1, GROUP):
                    keys(m, c)
                invert(m, late(m))
                values(m, 0)
                values(m, 1)
                p32(m, 0)
                queries(m, 2)
                y32(m, 0)
                queries(m, 3)
                values(m, 2)
                values(m, 3)
                for c in range(GROUP):
                    more = c + 1 < GROUP
                    read(m, c)
                    if c >= 2:
                        out(m, c - 2)
                    if more:
                        p32(m, c + 1)
                    solve(m, c)
                    expert_rows(m, c)
                    if more:
                        y32(m, c + 1)
                    expert_rows_2(m, c)
                    if c:
                        scale_out(m, c - 1)
                    apply(m, c)
                    squares_sum(m, c)
                out(m, GROUP - 2)
                scale_out(m, GROUP - 1)
                out(m, GROUP - 1)

        @block.gpsimd
        def _(pool):
            credits(pool, "gpsimd")
            G = pool
            G.memset(identb[:, :], 0.0).then_inc(consts, 1)
            G.memset(negb[:, :, :], 0.0).then_inc(consts, 1)
            G.memset(half[:, :, :], 0.5).then_inc(consts, 1)
            G.memset(mhalf[:, :, :], -0.5).then_inc(consts, 1)
            G.memset(goes_on[:, :], 1.0).then_inc(consts, 1)
            G.memset(tails[:, :, :], 0.0).then_inc(consts, 1)
            G.memset(S[:, :], 0.0).then_inc(consts, 1)
            G.wait_ge(consts, 7)
            G.memset(goes_on[:, 0:NG:PER_BATCH], 0.0).then_inc(consts, 1)
            G.affine_select(out=identb[:, :], in_=identb[:, :], compare_op=ALU.not_equal, fill=1.0, base=0,
                            pattern=[[-1, P]], channel_multiplier=1).then_inc(consts, 1)
            G.affine_select(out=negb[:, :, :], in_=negb[:, :, :], compare_op=ALU.is_ge, fill=NEG, base=0,
                            pattern=[[0, GROUP], [1, P]], channel_multiplier=-1).then_inc(consts, 1)
            G.wait_ge(consts, NCONST)
            G.wait_ge(params, 16 * NPARAM)

            def early_stats(m):
                wait(G, "eps_done", m)
                wait(G, "qg_ready", GROUP * m)
                apart(G)
                G.tensor_copy(bg[:, :, :, :], keep["stat"][:, bass.ds(GROUP * m, GROUP), 0:2, :]).then_inc(s["bg_done"], 1)

            def scan_stats(m):
                wait(G, "ktok_done", 2 * GROUP * m)
                wait(G, "t2_done", GROUP * m)
                wait(G, "ks_scaled", GROUP * m)
                wait(G, "sd_done", GROUP * m)
                apart(G)
                G.tensor_copy(mst[:, :, :, :], keep["stat"][:, bass.ds(GROUP * m, GROUP), :, :]).then_inc(s["mst_done"], 1)

            def halo(m):
                wait(G, "tails_done", PAIRS * m)
                wait(G, "taps_done", PAIRS * m)
                G.tensor_tensor(tk[:, :, :], tails[:, :, :], bc(goes_on[:, bass.ds(m, 1)], 1, QKV).to_broadcast([P, QKV, 3]), op=ALU.mult).then_inc(s["tk_done"], 1)
                wait(G, "tk_done", m + 1)
                G.tensor_tensor(corr[:, :, 0:3], tk[:, :, 0:3], cw[:, :, 0:1].to_broadcast([P, QKV, 3]), op=ALU.mult).then_inc(s["corr_step"], 1)
                for d in (1, 2):
                    w = 3 - d
                    G.tensor_tensor(ctmp[:, :, 0:w], tk[:, :, d:3], cw[:, :, d:d + 1].to_broadcast([P, QKV, w]), op=ALU.mult).then_inc(s["corr_step"], 1)
                    wait(G, "corr_step", 4 * m + 2 * d)
                    last = G.tensor_tensor(corr[:, :, 0:w], corr[:, :, 0:w], ctmp[:, :, 0:w], op=ALU.add)
                    if d == 1:
                        last.then_inc(s["corr_step"], 1)
                        wait(G, "corr_step", 4 * m + 3)
                last.then_inc(s["corr_done"], 1)

            def gather(m):
                wait(G, "acc2_done", GROUP * m)
                apart(G)
                G.tensor_copy(wt[:, :, :], keep["wtop"][:, bass.ds(GROUP * m, GROUP), :]).then_inc(s["wt_done"], 1)
                G.tensor_copy(sidx[:, :, :], keep["slot"][:, bass.ds(GROUP * m, GROUP), :]).then_inc(s["sidx_done"], 1)
                wait(G, "sidx_done", m + 1)
                apart(G)
                for c in range(GROUP):
                    for k in range(2):
                        G.indirect_dma_start(yb[:, c, k, :], None, yg_d[:, :], bass.IndirectOffsetOnAxis(ap=sidx[:, c, k:k + 1], axis=0)).then_inc(y_loaded, 16)

            def weigh_gate(m, c):
                wait(G, "gate_done", GROUP * m + c + 1)
                G.tensor_tensor(heads(gate[:, c, :]), heads(gate[:, c, :]), bc(nw[:, :], 1, H), op=ALU.mult).then_inc(s["gatew_done"], 1)

            def decay_sums(m, c):
                n = GROUP * m + c
                wait(G, "bg_done", m + 1)
                wait(G, "dexp_ready", 2 * n)
                G.tensor_tensor(qg[:, :, :], bc(tri_le[:, :], 1, H), bc(bg[:, c, 1, :], 2, P), op=ALU.mult).then_inc(s["qg_ready"], 1)

            def key_powers(m):
                wait(G, "nk_done", m + 1)
                wait(G, "vr_done", GROUP * m)
                G.tensor_tensor(knorm[:, :, :], nkq[:, :, 1, :], half[:, :, :], op=ALU.pow).then_inc(s["knorm_done"], 1)

            def query_powers(m):
                wait(G, "nq_done", m + 1)
                G.tensor_tensor(qscale[:, :, :], nkq[:, :, 0, :], mhalf[:, :, :], op=ALU.pow).then_inc(s["qscale_done"], 1)

            def read(m, c):
                n = GROUP * m + c
                if c == 0:
                    wait(G, "s_kept", m + 1)
                wait(G, "s_done", n)
                wait(G, "mst_done", m + 1)
                G.tensor_tensor(heads(Sd[:, :]), heads(S[:, :]), bc(mst[:, c, 4, :], 2, DV), op=ALU.mult).then_inc(s["sd_done"], 1)

            def squares(m, c):
                n = GROUP * m + c
                wait(G, "o_sum", n + 1)
                wait(G, "ss_done", n)
                G.tensor_tensor(osq[:, :], O[:, :], O[:, :], op=ALU.mult).then_inc(s["osq_done"], 1)

            def factor(m, c):
                n = GROUP * m + c
                wait(G, "ss_done", n + 1)
                wait(G, "qscale_done", m + 1)
                G.tensor_tensor(f1[:, :], ss[:, :], qscale[:, c, :], op=ALU.mult).then_inc(s["f_step"], 1)
                wait(G, "f_step", 4 * n + 1)
                G.tensor_tensor(f2[:, :], f1[:, :], qscale[:, c, :], op=ALU.mult).then_inc(s["f_step"], 1)
                wait(G, "f_step", 4 * n + 2)
                apart(G)
                G.tensor_scalar(f3[:, :], f2[:, :], 1.0 / (DK * DV), RMS_EPS, ALU.mult, ALU.add).then_inc(s["f_step"], 1)
                wait(G, "f_step", 4 * n + 3)
                G.tensor_tensor(f4[:, :], f3[:, :], mhalf[:, 0, :], op=ALU.pow).then_inc(s["f_step"], 1)
                wait(G, "f_step", 4 * n + 4)
                wait(G, "o2_done", n)
                apart(G)
                G.tensor_tensor(f1[:, :], f4[:, :], qscale[:, c, :], op=ALU.mult).then_inc(s["f5_done"], 1)
                wait(G, "f5_done", n + 1)
                apart(G)
                G.tensor_scalar(fo[:, :], f1[:, :], DK ** -0.5, None, ALU.mult).then_inc(s["f_done"], 1)

            with G.Fori(0, NG) as m:
                early_stats(m)
                decay_sums(m, 0)
                halo(m)
                for c in range(1, GROUP):
                    decay_sums(m, c)
                scan_stats(m)
                gather(m)
                key_powers(m)
                for c in range(GROUP):
                    weigh_gate(m, c)
                query_powers(m)
                read(m, 0)
                for c in range(GROUP):
                    squares(m, c)
                    if c + 1 < GROUP:
                        read(m, c + 1)
                    factor(m, c)


_INS = ["L0_attn_x", "L0_attn_Wq", "L0_attn_Wk", "L0_attn_Wv", "L0_attn_conv_q", "L0_attn_conv_k", "L0_attn_conv_v",
        "L0_attn_Wb", "L0_attn_Wa", "L0_attn_A_log", "L0_attn_dt_bias", "L0_attn_Wg", "L0_attn_norm_w", "L0_attn_Wo",
        "L0_ffn_Wg", "L0_ffn_W1", "L0_ffn_b1", "L0_ffn_W2", "L0_ffn_b2"]


def kernel(**inputs):
    import numpy as _np
    import concourse.bacc as _bacc
    from concourse import mybir as _mybir
    from concourse.bass_utils import run_bass_kernel_spmd as _run

    nc = _bacc.Bacc("TRN2", target_bir_lowering=False, num_devices=1)
    arrays, args = {}, []
    for name in _INS:
        a = _np.ascontiguousarray(inputs[name])
        arrays[f"in_{name}_dram"] = a
        args.append(nc.dram_tensor(f"in_{name}_dram", a.shape, _mybir.dt.from_np(a.dtype), kind="ExternalInput").ap())
    out = nc.dram_tensor("out_dram", inputs["L0_attn_x"].shape, _mybir.dt.float32, kind="ExternalOutput").ap()
    build(nc, *args, out)
    r = _run(nc, [arrays], core_ids=[0])
    return r.results[0]["out_dram"]
```

```python
from contextlib import ExitStack

import concourse.bass as bass
from concourse import mybir

ALU = mybir.AluOpType
ACT = mybir.ActivationFunctionType
F32 = mybir.dt.float32
BF16 = mybir.dt.bfloat16
I32 = mybir.dt.int32
AX_X = mybir.AxisListType.X

P = 128
GROUP = 4
GT = GROUP * P
D = 256
DC = D // P
E = 8
HID = 512
HC = HID // P
H = 8
DK = 128
DV = 64
TAPS = 4
QKV = 2 * H + H * DV // P
VC = H * DV // P
SMALL = E + 2 * H
NEG = -30000.0
LN_EPS = 1e-5
L2_EPS = 1e-6
RMS_EPS = 1e-5
NSTAT = 5


def bc(ap, axis, n):
    ap = ap.unsqueeze(axis)
    shape = list(ap.shape)
    shape[axis] = n
    return ap.to_broadcast(shape)


def col(t, i):
    return t[:, bass.ds(i, 1)]


def build(nc, x, Wq, Wk, Wv, cq, ck, cv, Wb, Wa, A_log, dt_bias, Wg, norm_w, Wo, Wr, W1, b1, W2, b2, out):
    B, T, _ = x.shape
    N = B * T
    NT = N // P
    NG = N // GT
    MT = 2 * NT + E
    xf = x.rearrange("b t d -> (b t) d")
    of = out.rearrange("b t d -> (b t) d")
    xn_d = nc.dram_tensor("xn_rows", [N, D], F32, kind="Internal").ap()
    xnT_d = nc.dram_tensor("xn_cols", [P, DC, N], F32, kind="Internal").ap()
    xg_d = nc.dram_tensor("expert_in", [MT * P, D], F32, kind="Internal").ap()
    yg_d = nc.dram_tensor("expert_out", [MT * P, D], F32, kind="Internal").ap()
    dims = (B, T, N, NT, NG, MT)
    with ExitStack() as ctx:
        def sb(name, shape, dt=F32):
            return ctx.enter_context(nc.sbuf_tensor(name, shape, dt))

        keep = {
            "ident": sb("ident", [P, P]), "tri_le": sb("tri_le", [P, P]), "tri_gt": sb("tri_gt", [P, P]),
            "ones": sb("ones", [P, P]),
            "stat": sb("stat", [P, NT, NSTAT, H]),
            "slot": sb("slot", [P, NT, 2], I32),
            "wtop": sb("wtop", [P, NT, 2]),
            "tile_expert": sb("tile_expert", [1, MT], I32),
        }
        attention_params = {
            "wqkv": sb("att_wqkv", [P, DC, QKV * P]), "wg": sb("att_wg", [P, DC, H * DV]), "wo": sb("att_wo", [P, VC, D]),
            "cw": sb("att_cw", [P, QKV, TAPS]), "nw": sb("att_nw", [P, DV]),
            "loaded": ctx.enter_context(nc.semaphore("att_params")),
        }
        attention_sources = (
            [(attention_params["wqkv"][:, :, a * P:b * P], w.rearrange("(c p) n -> p c n", p=P)) for a, b, w in
             ((0, H, Wq), (H, 2 * H, Wk), (2 * H, QKV, Wv))]
            + [(attention_params["cw"][:, a:b, :], w.rearrange("(c p) k -> p c k", p=P)) for a, b, w in
               ((0, H, cq), (H, 2 * H, ck), (2 * H, QKV, cv))]
            + [(attention_params["wg"][:, :, :], Wg.rearrange("(c p) n -> p c n", p=P)),
               (attention_params["wo"][:, :, :], Wo.rearrange("(c p) n -> p c n", p=P)),
               (attention_params["nw"][:, :], norm_w.rearrange("(a n) -> a n", a=1).to_broadcast([P, DV]))])
        with ExitStack() as expert_ctx:
            def load(name, shape, source):
                return (expert_ctx.enter_context(nc.sbuf_tensor("moe_" + name, shape, F32)), source,
                        expert_ctx.enter_context(nc.semaphore("moe_loaded_" + name)))

            expert_params = (
                load("w1", [P, E, DC, HID], W1.rearrange("e (c p) n -> p e c n", p=P)),
                load("w2", [P, E, HC, D], W2.rearrange("e (c p) n -> p e c n", p=P)),
                load("b1b", [P, E, HID], b1.rearrange("(o e) n -> o e n", o=1).to_broadcast([P, E, HID])),
                load("b2b", [P, E, D], b2.rearrange("(o e) n -> o e n", o=1).to_broadcast([P, E, D])),
            )
            norm_and_route(nc, keep, dims, xf, Wr, Wb, Wa, A_log, dt_bias, xn_d, xnT_d, xg_d, expert_params)
            experts(nc, keep, dims, expert_params, xn_d, xg_d, yg_d, attention_sources, attention_params["loaded"])
        attention(nc, keep, dims, attention_params, len(attention_sources), xf, xnT_d, yg_d, of)


def norm_and_route(nc, keep, dims, xf, Wr, Wb, Wa, A_log, dt_bias, xn_d, xnT_d, xg_d, expert_params):
    B, T, N, NT, NG, MT = dims
    ident, tri_le, tri_gt, ones = keep["ident"], keep["tri_le"], keep["tri_gt"], keep["ones"]
    stat, slot, wtop, tile_expert = keep["stat"], keep["slot"], keep["wtop"], keep["tile_expert"]
    ZR = 8
    with ExitStack() as ctx:
        def sb(name, shape, dt=F32):
            return ctx.enter_context(nc.sbuf_tensor("route_" + name, shape, dt))

        def sem(name):
            return ctx.enter_context(nc.semaphore("route_" + name))

        zero = sb("zero", [P, ZR * D])
        w_small = sb("w_small", [P, DC, SMALL])
        alog = sb("alog", [P, H]); dtb = sb("dtb", [P, H]); expa = sb("expa", [P, H])
        tri_lt = sb("tri_lt", [P, P])
        x_in = sb("x_in", [P, 2, GROUP, D])
        xn = sb("xn", [P, 2, GROUP, D])
        xnT = sb("xnT", [P, 2, DC, GT])
        bnst = sb("bnst", [P, 2, GROUP, 6]); mv = sb("mv", [P, 2, GROUP, 2])
        var_eps = sb("var_eps", [P, 2, GROUP]); rstd = sb("rstd", [P, 2, GROUP])
        minus_half = sb("minus_half", [P, GROUP])
        lg = sb("lg", [P, NT, SMALL])
        psT = ctx.enter_context(nc.psum_tensor("route_psT", [P, 2, DC, GT], F32))
        psL = ctx.enter_context(nc.psum_tensor("route_psL", [P, 2, 512], F32))
        psR = ctx.enter_context(nc.psum_tensor("route_psR", [P, 2, 512], F32))
        big = [sb(f"route{i}", [P, NT, E]) for i in range(8)]
        r1 = [sb(f"row{i}", [P, NT]) for i in range(6)]
        e8 = [sb(f"per_expert{i}", [P, E]) for i in range(6)]
        e8i = sb("per_expert_int", [P, E], I32)
        rank_w = sb("rank_w", [P, E])
        jt = sb("jt", [1, MT]); jcmp = sb("jcmp", [1, MT, E]); jsum = sb("jsum", [1, MT])

        consts, params, xn_made = sem("consts"), sem("params"), sem("xn_made")
        x_loaded = [sem(f"x_loaded{par}") for par in range(2)]
        bn_done, aggr_done, ve_done, rstd_done = (sem(n) for n in ("bn_done", "aggr_done", "ve_done", "rstd_done"))
        tr_done, xnT_done, lg_mm, lg_done = sem("tr_done"), sem("xnT_done"), sem("lg_mm"), sem("lg_done")
        rows_stored = [sem(f"rows_stored{par}") for par in range(2)]
        cols_stored = [sem(f"cols_stored{par}") for par in range(2)]
        zeroed, passed = sem("zeroed"), sem("passed")
        step, a_step, mm_step, p_step = sem("route_step"), sem("route_exp"), sem("route_mm"), sem("route_iota")
        block = ctx.enter_context(nc.Block())
        xt_v = xf.rearrange("(g a p) d -> g p a d", a=GROUP, p=P)
        xn_v = xn_d.rearrange("(g a p) d -> g p a d", a=GROUP, p=P)
        NCONST = 12
        counts = {}

        @block.sync
        def _(sp):
            sp.dma_start(w_small[:, :, 0:E], Wr.rearrange("(c p) e -> p c e", p=P)).then_inc(params, 16)
            sp.dma_start(w_small[:, :, E:E + H], Wb.rearrange("(c p) e -> p c e", p=P)).then_inc(params, 16)
            sp.dma_start(w_small[:, :, E + H:SMALL], Wa.rearrange("(c p) e -> p c e", p=P)).then_inc(params, 16)
            sp.dma_start(alog[:, :], A_log.rearrange("(a h) -> a h", a=1).to_broadcast([P, H])).then_inc(params, 16)
            sp.dma_start(dtb[:, :], dt_bias.rearrange("(a h) -> a h", a=1).to_broadcast([P, H])).then_inc(params, 16)
            with sp.Fori(0, NG // 2) as i:
                for par in range(2):
                    g = 2 * i + par
                    sp.wait_ge(xn_made, 4 * g + 4)
                    sp.dma_start(x_in[:, par], xt_v[bass.ds(g, 1)].rearrange("o p a d -> (o p) a d")).then_inc(x_loaded[par], 16)

        @block.gpsimd
        def _(pool):
            pool.memset(zero[:, :], 0.0).then_inc(consts, 1)
            pool.memset(ident[:, :], 0.0).then_inc(consts, 1)
            pool.memset(ones[:, :], 1.0).then_inc(consts, 1)
            pool.memset(minus_half[:, :], -0.5).then_inc(consts, 1)
            pool.wait_ge(consts, 4)
            pool.affine_select(out=ident[:, :], in_=ident[:, :], compare_op=ALU.not_equal, fill=1.0, base=0,
                               pattern=[[-1, P]], channel_multiplier=1).then_inc(consts, 1)
            pool.affine_select(out=tri_le[:, :], in_=ones[:, :], compare_op=ALU.is_ge, fill=0.0, base=0,
                               pattern=[[1, P]], channel_multiplier=-1).then_inc(consts, 1)
            pool.affine_select(out=tri_lt[:, :], in_=ones[:, :], compare_op=ALU.is_gt, fill=0.0, base=0,
                               pattern=[[1, P]], channel_multiplier=-1).then_inc(consts, 1)
            pool.affine_select(out=tri_gt[:, :], in_=ones[:, :], compare_op=ALU.is_gt, fill=0.0, base=0,
                               pattern=[[-1, P]], channel_multiplier=1).then_inc(consts, 1)
            pool.iota(e8i[:, :], pattern=[[-1, E]], base=E, channel_multiplier=0).then_inc(consts, 1)
            pool.wait_ge(consts, 9)
            pool.tensor_copy(rank_w[:, :], e8i[:, :]).then_inc(consts, 1)
            pool.iota(jcmp[0:1, :, 0].bitcast(I32), pattern=[[1, MT]], base=0, channel_multiplier=0).then_inc(consts, 1)
            pool.wait_ge(consts, 11)
            pool.tensor_copy(jt[0:1, :], jcmp[0:1, :, 0].bitcast(I32)).then_inc(consts, 1)
            for r in range(MT // ZR):
                pool.dma_start(xg_d[r * ZR * P:(r + 1) * ZR * P, :].rearrange("(p r) d -> p (r d)", p=P), zero[:, :]).then_inc(zeroed, 16)
            with pool.Fori(0, NG // 2) as i:
                for par in range(2):
                    pool.wait_ge(ve_done, 2 * i + par + 1)
                    pool.tensor_tensor(rstd[:, par], var_eps[:, par], minus_half[:, :], op=ALU.pow).then_inc(rstd_done, 1)
            pool.wait_ge(zeroed, 16 * (MT // ZR))

        @block.vector
        def _(dve):
            dve.sem_inc(xn_made, 2 * GROUP)
            dve.sem_inc(lg_done, 2)
            dve.sem_inc(xnT_done, 4)

            def normalise(i, par):
                g = 2 * i + par
                dve.wait_ge(x_loaded[par], 16 * i + 16)
                for a in range(GROUP):
                    nc.vector.bn_stats(bnst[:, par, a], x_in[:, par, a]).then_inc(bn_done, 1)
                for a in range(GROUP):
                    dve.wait_ge(bn_done, 4 * g + a + 1)
                    dve.sem_inc(passed, 1)
                    nc.vector.bn_aggr(mv[:, par, a], bnst[:, par, a]).then_inc(aggr_done, 1)
                dve.wait_ge(aggr_done, 4 * g + 4)
                nc.vector.tensor_scalar(var_eps[:, par], mv[:, par, :, 1], LN_EPS, None, ALU.add).then_inc(ve_done, 1)

            def scale(i, par):
                g = 2 * i + par
                dve.wait_ge(rstd_done, g + 1)
                dve.wait_ge(rows_stored[par], 16 * i + 16)
                dve.wait_ge(tr_done, g + 1)
                for a in range(GROUP):
                    nc.vector.tensor_scalar(xn[:, par, a], x_in[:, par, a], mv[:, par, a, 0:1], rstd[:, par, a:a + 1],
                                            ALU.subtract, ALU.mult).then_inc(xn_made, 1)

            def columns(i, par):
                g = 2 * i + par
                dve.wait_ge(tr_done, g + 3)
                dve.wait_ge(cols_stored[par], 16 * i + 16)
                nc.vector.tensor_copy(xnT[:, par, 1], psT[:, par, 1]).then_inc(xnT_done, 1)

            def logits(i, par):
                g = 2 * i + par
                dve.wait_ge(lg_mm, g + 1)
                nc.vector.tensor_scalar(lg[:, bass.ds(4 * g, GROUP), :], psL[:, par, 0:GROUP * SMALL].rearrange("p (a s) -> p a s", a=GROUP),
                                        1.0, None, ALU.mult).then_inc(lg_done, 1)

            normalise(0, 0)
            scale(0, 0)
            normalise(0, 1)
            columns(0, 0)
            scale(0, 1)
            with dve.Fori(1, NG // 2) as i:
                normalise(i, 0)
                columns(i - 1, 1)
                logits(i - 1, 0)
                scale(i, 0)
                normalise(i, 1)
                columns(i, 0)
                logits(i - 1, 1)
                scale(i, 1)
            columns(NG // 2 - 1, 1)
            logits(NG // 2 - 1, 0)
            logits(NG // 2 - 1, 1)
            n = [0]

            def link(ins):
                n[0] += 1
                ins.then_inc(step, 1)
                dve.wait_ge(step, n[0])

            V = nc.vector
            dve.wait_ge(lg_done, NG + 2)
            L = lg[:, :, 0:E]
            oh1, cand, oh2, l2, mask, ex, cnt, pos = big
            m1, m2, pick, esum, w1s, dd = r1
            rw = bc(rank_w[:, :], 1, NT)

            def onehot(dst, src, top):
                link(V.tensor_reduce(top[:, :], src, op=ALU.max, axis=AX_X))
                link(V.tensor_tensor(cand[:, :, :], src, bc(top[:, :], 2, E), op=ALU.is_equal))
                link(V.tensor_tensor(cand[:, :, :], cand[:, :, :], rw, op=ALU.mult))
                link(V.tensor_reduce(pick[:, :], cand[:, :, :], op=ALU.max, axis=AX_X))
                link(V.tensor_tensor(dst[:, :, :], cand[:, :, :], bc(pick[:, :], 2, E), op=ALU.is_equal))

            onehot(oh1, L, m1)
            link(V.scalar_tensor_tensor(out=l2[:, :, :], in0=oh1[:, :, :], scalar=-3.0e38, in1=L, op0=ALU.mult, op1=ALU.add))
            onehot(oh2, l2[:, :, :], m2)
            link(V.tensor_tensor(dd[:, :], m2[:, :], m1[:, :], op=ALU.subtract))
            link(V.tensor_tensor(mask[:, :, :], oh1[:, :, :], oh2[:, :, :], op=ALU.add))
            mask_at = n[0]
            dve.wait_ge(a_step, 1)
            link(V.tensor_scalar(esum[:, :], w1s[:, :], 1.0, None, ALU.add))
            link(V.reciprocal(pick[:, :], esum[:, :]))
            link(V.tensor_copy(wtop[:, :, 0], pick[:, :]))
            link(V.tensor_tensor(wtop[:, :, 1], pick[:, :], w1s[:, :], op=ALU.mult))
            dve.wait_ge(mm_step, 1)
            link(V.tensor_copy(cnt[:, :, :], psR[:, 1, 0:NT * E].rearrange("p (t e) -> p t e", e=E)))
            link(V.memset(l2[:, :, :], 0.0))
            for e in range(E):
                link(V.tensor_tensor_scan(out=ex[:, :, e], data0=cnt[:, :, e], data1=l2[:, :, e], initial=0.0,
                                          op0=ALU.add, op1=ALU.add))
            tot, tiles_f, end, base, zer8, tmp8 = e8
            link(V.tensor_scalar(tot[:, :], ex[:, NT - 1, :], float(P - 1), None, ALU.add))
            link(V.tensor_copy(e8i[:, :], tot[:, :]))
            link(V.tensor_scalar(e8i[:, :], e8i[:, :], 7, None, ALU.arith_shift_right))
            link(V.tensor_copy(tiles_f[:, :], e8i[:, :]))
            link(V.memset(zer8[:, :], 0.0))
            link(V.tensor_tensor_scan(out=end[:, :], data0=tiles_f[:, :], data1=zer8[:, :], initial=0.0, op0=ALU.add, op1=ALU.add))
            link(V.tensor_tensor(base[:, :], end[:, :], tiles_f[:, :], op=ALU.subtract))
            link(V.tensor_scalar(base[:, :], base[:, :], float(P), None, ALU.mult))
            link(V.tensor_tensor(ex[:, :, :], ex[:, :, :], cnt[:, :, :], op=ALU.subtract))
            link(V.tensor_tensor(pos[:, :, :], ex[:, :, :], psR[:, 0, 0:NT * E].rearrange("p (t e) -> p t e", e=E), op=ALU.add))
            link(V.tensor_tensor(pos[:, :, :], pos[:, :, :], bc(base[:, :], 1, NT), op=ALU.add))
            for k, oh in enumerate((oh1, oh2)):
                link(V.tensor_tensor(cand[:, :, :], pos[:, :, :], oh[:, :, :], op=ALU.mult))
                link(V.tensor_reduce(m1[:, :], cand[:, :, :], op=ALU.add, axis=AX_X))
                link(V.tensor_copy(slot[:, :, k], m1[:, :]))
            link(V.tensor_tensor(jcmp[0:1, :, :], bc(jt[0:1, :], 2, E), bc(end[0:1, :], 1, MT), op=ALU.is_ge))
            link(V.tensor_reduce(jsum[0:1, :], jcmp[0:1, :, :], op=ALU.add, axis=AX_X))
            link(V.tensor_scalar(jsum[0:1, :], jsum[0:1, :], float(E - 1), None, ALU.min))
            link(V.tensor_copy(tile_expert[0:1, :], jsum[0:1, :]))
            a_in, u, s, s2, acc, ab = (t for t in (oh1, cand, oh2, l2, mask, ex))
            link(V.tensor_tensor(a_in[:, :, :], lg[:, :, E + H:SMALL], bc(dtb[:, :], 1, NT), op=ALU.add))
            link(V.tensor_scalar(ab[:, :, :], a_in[:, :, :], -1.0, None, ALU.mult))
            link(V.tensor_tensor(ab[:, :, :], a_in[:, :, :], ab[:, :, :], op=ALU.min))
            ab_at = n[0]
            dve.wait_ge(a_step, 4)
            link(V.tensor_scalar(s[:, :, :], u[:, :, :], 2.0, None, ALU.add))
            link(V.reciprocal(s[:, :, :], s[:, :, :]))
            link(V.tensor_tensor(s[:, :, :], s[:, :, :], u[:, :, :], op=ALU.mult))
            link(V.tensor_tensor(s2[:, :, :], s[:, :, :], s[:, :, :], op=ALU.mult))
            link(V.tensor_scalar(acc[:, :, :], s2[:, :, :], 1.0 / 17, 1.0 / 15, ALU.mult, ALU.add))
            for k in (13, 11, 9, 7, 5, 3, 1):
                link(V.tensor_tensor(acc[:, :, :], acc[:, :, :], s2[:, :, :], op=ALU.mult))
                link(V.tensor_scalar(acc[:, :, :], acc[:, :, :], 1.0 / k, None, ALU.add))
            link(V.tensor_tensor(acc[:, :, :], acc[:, :, :], s[:, :, :], op=ALU.mult))
            link(V.tensor_scalar(a_in[:, :, :], a_in[:, :, :], 0.0, None, ALU.max))
            link(V.scalar_tensor_tensor(out=acc[:, :, :], in0=acc[:, :, :], scalar=2.0, in1=a_in[:, :, :], op0=ALU.mult, op1=ALU.add))
            link(V.scalar_tensor_tensor(out=stat[:, :, 1, :], in0=acc[:, :, :], scalar=-1.0, in1=bc(expa[:, :], 1, NT), op0=ALU.mult, op1=ALU.mult))
            g_at = n[0]
            link(V.tensor_scalar(pos[:, :, :], pos[:, :, :], 1.0, None, ALU.add))
            link(V.reciprocal(pos[:, :, :], pos[:, :, :]))
            link(V.tensor_copy(stat[:, :, 0, :], pos[:, :, :]))
            counts["mask"], counts["ab"], counts["g"] = mask_at, ab_at, g_at
            counts["end"] = n[0]

        @block.scalar
        def _(act):
            act.wait_ge(params, 80)
            with act.Fori(0, NG // 2) as i:
                for par in range(2):
                    g = 2 * i + par
                    act.wait_ge(xn_made, 4 * g + 12)
                    act.dma_start(xn_v[bass.ds(g, 1)].rearrange("o p a d -> (o p) a d"), xn[:, par]).then_inc(rows_stored[par], 16)
                    act.wait_ge(tr_done, g + 3)
                    act.wait_ge(cols_stored[par], 16 * i + 16)
                    nc.scalar.activation(xnT[:, par, 0], psT[:, par, 0], ACT.Copy).then_inc(xnT_done, 1)
                    act.wait_ge(xnT_done, 2 * g + 6)
                    act.dma_start(xnT_d[:, :, bass.ds(g * GT, GT)], xnT[:, par]).then_inc(cols_stored[par], 16)
            for tile, source, loaded in expert_params:
                act.dma_start(tile[tuple(slice(None) for _ in tile.shape)], source).then_inc(loaded, 16)
            m2_m1, w1s = r1[5], r1[4]
            act.wait_ge(step, counts["mask"])
            nc.scalar.activation(w1s[:, :], m2_m1[:, :], ACT.Exp).then_inc(a_step, 1)
            nc.scalar.activation(expa[:, :], alog[:, :], ACT.Exp).then_inc(a_step, 1)
            act.wait_ge(step, counts["ab"])
            nc.scalar.activation(big[1][:, :, :], big[5][:, :, :], ACT.Exp).then_inc(a_step, 1)
            nc.scalar.activation(big[7][:, :, :], lg[:, :, E:E + H], ACT.Exp, scale=-1.0).then_inc(a_step, 1)
            for k in range(3):
                act.wait_ge(mm_step, 2 + k)
                src = (psR[:, 0], psR[:, 1], psL[:, 0])[k]
                nc.scalar.activation(stat[:, :, 2 + k, :], src[:, 0:NT * H].rearrange("p (t h) -> p t h", h=H), ACT.Exp).then_inc(a_step, 1)
            for par in range(2):
                act.wait_ge(rows_stored[par], 8 * NG + 16)
            for par in range(2):
                act.wait_ge(cols_stored[par], 8 * NG + 16)

        @block.tensor
        def _(pe):
            pe.sem_inc(tr_done, 2)
            for par in range(2):
                pe.sem_inc(rows_stored[par], 16)
            for par in range(2):
                pe.sem_inc(cols_stored[par], 16)
            pe.wait_ge(params, 80)
            pe.wait_ge(consts, NCONST)
            with pe.Fori(0, NG // 2) as i:
                for par in range(2):
                    g = 2 * i + par
                    pe.wait_ge(xn_made, 4 * g + 12)
                    pe.wait_ge(xnT_done, 2 * g + 2)
                    for c in range(DC):
                        for a in range(GROUP):
                            last = nc.tensor.transpose(psT[:, par, c, a * P:(a + 1) * P], xn[:, par, a, c * P:(c + 1) * P], ident[:, :])
                    last.then_inc(tr_done, 1)
                    pe.wait_ge(xnT_done, 2 * g + 6)
                    pe.wait_ge(lg_done, g + 1)
                    for a in range(GROUP):
                        for c in range(DC):
                            last = nc.tensor.matmul(psL[:, par, a * SMALL:(a + 1) * SMALL], xnT[:, par, c, a * P:(a + 1) * P],
                                                    w_small[:, c, :], start=(c == 0), stop=(c == DC - 1))
                    last.then_inc(lg_mm, 1)
            pe.wait_ge(step, counts["mask"])
            mk = big[4][:, :, :].rearrange("p t e -> p (t e)")
            nc.tensor.matmul(psR[:, 0, 0:NT * E], tri_lt[:, :], mk, start=True, stop=True)
            nc.tensor.matmul(psR[:, 1, 0:NT * E], ones[:, :], mk, start=True, stop=True).then_inc(mm_step, 1)
            pe.wait_ge(step, counts["g"])
            for k, (dst, tri) in enumerate(((psR[:, 0], tri_le), (psR[:, 1], tri_gt), (psL[:, 0], ones))):
                nc.tensor.matmul(dst[:, 0:NT * H], tri[:, :], stat[:, :, 1, :], start=True, stop=True).then_inc(mm_step, 1)


def experts(nc, keep, dims, expert_params, xn_d, xg_d, yg_d, attention_sources, attention_loaded):
    B, T, N, NT, NG, MT = dims
    ident, slot, tile_expert = keep["ident"], keep["slot"], keep["tile_expert"]
    with ExitStack() as ctx:
        def sb(name, shape, dt=F32):
            return ctx.enter_context(nc.sbuf_tensor("moe_" + name, shape, dt))

        def pair(name):
            return [ctx.enter_context(nc.psum_tensor(f"moe_{name}{i}", [P, 512], F32)) for i in range(2)]

        def sem(name):
            return ctx.enter_context(nc.semaphore("moe_" + name))

        (w1, _, w1_loaded), (w2, _, w2_loaded), (b1b, _, b1_loaded), (b2b, _, b2_loaded) = expert_params
        rows = sb("rows", [P, 2, GROUP, D]); idx = sb("idx", [P, 2, GROUP, 2], I32)
        xt = sb("xt", [P, 2, D]); xT = sb("xT", [P, 2, DC, P])
        h = sb("h", [P, 2, HID]); hT = sb("hT", [P, 2, HC, P]); y = sb("y", [P, 2, D])
        psX, psH, psHT, psY = pair("psX"), pair("psH"), pair("psHT"), pair("psY")

        rows_loaded = [sem(f"rows_loaded{i}") for i in range(2)]
        scattered = [sem(f"scattered{i}") for i in range(2)]
        idx_copied, passed = sem("idx_copied"), sem("passed")
        x_loaded = [sem(f"tile_loaded{i}") for i in range(2)]
        y_stored = [sem(f"y_stored{i}") for i in range(2)]
        xtr, xT_done, h_mm, h_done, htr, hT_done, y_mm, y_done = (
            sem(n) for n in ("xtr", "xT_done", "h_mm", "h_done", "htr", "hT_done", "y_mm", "y_done"))
        block = ctx.enter_context(nc.Block())
        rows_v = xn_d.rearrange("(g a p) d -> g p a d", a=GROUP, p=P)
        xg_v = xg_d.rearrange("(t p) d -> t p d", p=P)
        yg_v = yg_d.rearrange("(t p) d -> t p d", p=P)

        def before(q, par):
            return (q, 0) if par else (q - 1, 1)

        def after(q, par):
            return (q + 1, 0) if par else (q, 1)

        def steps(eng, step):
            step(None, (0, 0), None)
            step((0, 0), (0, 1), None)
            step((0, 1), (1, 0), (0, 0))
            step((1, 0), (1, 1), (0, 1))
            with eng.Fori(1, MT // 2 - 1) as i:
                for tile in ((i, 1), (i + 1, 0)):
                    step(tile, after(*tile), before(*tile))
            last = (MT // 2 - 1, 1)
            step(last, None, before(*last))
            step(None, None, last)

        @block.sync
        def _(sp):
            for par in range(2):
                sp.dma_start(rows[:, par], rows_v[par]).then_inc(rows_loaded[par], 16)
            with sp.Fori(1, NG // 2) as i:
                for par in range(2):
                    sp.wait_ge(scattered[par], 2 * GROUP * 16 * i)
                    sp.dma_start(rows[:, par], rows_v[bass.ds(2 * i + par, 1)].rearrange("o p a d -> (o p) a d")).then_inc(rows_loaded[par], 16)
            for par in range(2):
                sp.wait_ge(scattered[par], 2 * GROUP * 16 * (NG // 2))
            for par in range(2):
                sp.wait_ge(xtr, par + 1)
                sp.dma_start(xt[:, par], xg_v[par]).then_inc(x_loaded[par], 16)
            for tile, source in attention_sources:
                sp.dma_start(tile, source).then_inc(attention_loaded, 16)
            with sp.Fori(1, MT // 2) as i:
                for par in range(2):
                    sp.wait_ge(xtr, 2 * i + par + 1)
                    sp.dma_start(xt[:, par], xg_v[bass.ds(2 * i + par, 1)].rearrange("o p d -> (o p) d")).then_inc(x_loaded[par], 16)

        @block.gpsimd
        def _(pool):
            pool.sem_inc(idx_copied, 1)

            def scatter(i):
                for par in range(2):
                    g = 2 * i + par
                    if not (isinstance(i, int) and i == 0):
                        pool.wait_ge(scattered[par], 2 * GROUP * 16 * i)
                    pool.tensor_copy(idx[:, par], slot[:, bass.ds(GROUP * g, GROUP), :]).then_inc(idx_copied, 1)
                    pool.wait_ge(rows_loaded[par], 16 * i + 16)
                    pool.wait_ge(idx_copied, g + 2)
                    pool.sem_inc(passed, 1)
                    for a in range(GROUP):
                        for k in range(2):
                            pool.indirect_dma_start(xg_d[:, :], bass.IndirectOffsetOnAxis(ap=idx[:, par, a, k:k + 1], axis=0),
                                                    rows[:, par, a], None).then_inc(scattered[par], 16)

            scatter(0)
            with pool.Fori(1, NG // 2) as i:
                scatter(i)
            with pool.Fori(0, MT // 2) as i:
                for par in range(2):
                    t = 2 * i + par
                    pool.wait_ge(y_done, t + 3)
                    pool.sem_inc(passed, 1)
                    pool.dma_start(yg_v[bass.ds(t, 1)].rearrange("o p d -> (o p) d"), y[:, par]).then_inc(y_stored[par], 16)
            for par in range(2):
                pool.wait_ge(y_stored[par], 8 * MT)

        @block.scalar
        def _(act):
            act.sem_inc(xT_done, 2)
            act.sem_inc(hT_done, 2)

            def step(cur, nxt, prev):
                if prev:
                    q, par = prev
                    t = 2 * q + par
                    act.wait_ge(htr, t + 3)
                    act.wait_ge(y_mm, t + 1)
                    nc.scalar.activation(hT[:, par], psHT[par][:, :].rearrange("p (c n) -> p c n", c=HC), ACT.Relu).then_inc(hT_done, 1)
                if nxt:
                    q, par = nxt
                    t = 2 * q + par
                    act.wait_ge(xtr, t + 3)
                    act.wait_ge(h_mm, t + 1)
                    nc.scalar.activation(xT[:, par], psX[par][:, 0:D].rearrange("p (c n) -> p c n", c=DC), ACT.Copy).then_inc(xT_done, 1)

            steps(act, step)

        @block.vector
        def _(dve):
            dve.sem_inc(h_done, 2)
            dve.sem_inc(y_done, 2)
            for w in (b1_loaded, b2_loaded):
                dve.wait_ge(w, 16)

            def step(cur, nxt, prev):
                if cur:
                    q, par = cur
                    t = 2 * q + par
                    e = dve.value_load(tile_expert[0:1, t:t + 1] if isinstance(t, int) else tile_expert[0:1, bass.ds(t, 1)], min_val=0, max_val=E - 1)
                    dve.wait_ge(h_mm, t + 3)
                    dve.wait_ge(htr, t + 1)
                    nc.vector.tensor_tensor(h[:, par], psH[par][:, :], b1b[:, bass.ds(e, 1), :].rearrange("p o n -> p (o n)"), op=ALU.add).then_inc(h_done, 1)
                if prev:
                    q, par = prev
                    t = 2 * q + par
                    e = dve.value_load(tile_expert[0:1, t:t + 1] if isinstance(t, int) else tile_expert[0:1, bass.ds(t, 1)], min_val=0, max_val=E - 1)
                    dve.wait_ge(y_mm, t + 3)
                    if not isinstance(q, int) or q > 0:
                        dve.wait_ge(y_stored[par], 16 * q)
                    nc.vector.tensor_tensor(y[:, par], psY[par][:, 0:D], b2b[:, bass.ds(e, 1), :].rearrange("p o n -> p (o n)"), op=ALU.add).then_inc(y_done, 1)

            steps(dve, step)

        @block.tensor
        def _(pe):
            for s in (xtr, h_mm, htr, y_mm):
                pe.sem_inc(s, 2)
            for w in (w1_loaded, w2_loaded):
                pe.wait_ge(w, 16)

            def expert(t):
                return pe.value_load(tile_expert[0:1, t:t + 1] if isinstance(t, int) else tile_expert[0:1, bass.ds(t, 1)], min_val=0, max_val=E - 1)

            def step(cur, nxt, prev):
                if nxt:
                    q, par = nxt
                    t = 2 * q + par
                    pe.wait_ge(x_loaded[par], 16 * q + 16)
                    pe.wait_ge(xT_done, t + 1)
                    for c in range(DC):
                        last = nc.tensor.transpose(psX[par][:, c * P:(c + 1) * P], xt[:, par, c * P:(c + 1) * P], ident[:, :])
                    last.then_inc(xtr, 1)
                if prev:
                    q, par = prev
                    t = 2 * q + par
                    pe.wait_ge(h_done, t + 3)
                    pe.wait_ge(hT_done, t + 1)
                    for c in range(HC):
                        last = nc.tensor.transpose(psHT[par][:, c * P:(c + 1) * P], h[:, par, c * P:(c + 1) * P], ident[:, :])
                    last.then_inc(htr, 1)
                if cur:
                    q, par = cur
                    t = 2 * q + par
                    e = expert(t)
                    pe.wait_ge(xT_done, t + 3)
                    pe.wait_ge(h_done, t + 1)
                    for c in range(DC):
                        last = nc.tensor.matmul(psH[par][:, :], xT[:, par, c], w1[:, bass.ds(e, 1), c].rearrange("p o n -> p (o n)"),
                                                start=(c == 0), stop=(c == DC - 1))
                    last.then_inc(h_mm, 1)
                if prev:
                    q, par = prev
                    t = 2 * q + par
                    e = expert(t)
                    pe.wait_ge(hT_done, t + 3)
                    pe.wait_ge(y_done, t + 1)
                    for c in range(HC):
                        last = nc.tensor.matmul(psY[par][:, 0:D], hT[:, par, c], w2[:, bass.ds(e, 1), c].rearrange("p o n -> p (o n)"),
                                                start=(c == 0), stop=(c == HC - 1))
                    last.then_inc(y_mm, 1)

            steps(pe, step)


CREDIT = 4


def attention(nc, keep, dims, loaded_params, NPARAM, xf, xnT_d, yg_d, of):
    B, T, N, NT, NG, MT = dims
    ident, tri_le, tri_gt, ones = keep["ident"], keep["tri_le"], keep["tri_gt"], keep["ones"]
    U = GROUP * H
    NB = P // 32
    PAIRS = QKV // 2
    QKP = 2 * H // 2
    HV = H * DV
    PER_BATCH = T // GT
    assert U == 32
    with ExitStack() as ctx:
        def sb(name, shape, dt=F32):
            return ctx.enter_context(nc.sbuf_tensor("att_" + name, shape, dt))

        wqkv, wg, wo, cw, nw, params = (loaded_params[n] for n in ("wqkv", "wg", "wo", "cw", "nw", "loaded"))
        identb = sb("identb", [P, P], BF16); negb = sb("negb", [P, GROUP, P], BF16)
        half = sb("half", [P, GROUP, H]); mhalf = sb("mhalf", [P, GROUP, H]); goes_on = sb("goes_on", [P, NG])
        xt = sb("xt", [P, DC, GT])
        qk = sb("qk", [P, H, 2, GT]); vc = sb("vc", [P, VC, GT]); sq = sb("sq", [P, 2, 2, GT])
        tails = sb("tails", [P, QKV, 3]); tk = sb("tk", [P, QKV, 3]); corr = sb("corr", [P, QKV, 3]); ctmp = sb("ctmp", [P, QKV, 3])
        gate = sb("gate", [P, GROUP, HV])
        mst = sb("mst", [P, GROUP, NSTAT, H]); bg = sb("beta_g", [P, GROUP, 2, H]); wt = sb("wt", [P, GROUP, 2]); sidx = sb("sidx", [P, GROUP, 2], I32)
        nkq = sb("nkq", [P, GROUP, 2, H]); rn = sb("rn", [P, GROUP, H]); eps = sb("eps", [P, GROUP, H])
        knorm = sb("knorm", [P, GROUP, H]); qscale = sb("qscale", [P, GROUP, H])
        qg = sb("qg", [P, 2, H, P])
        Y = sb("Y", [P, U, P]); AT = sb("AT", [P, U, P]); X = sb("X", [P, U, 64])
        vr = sb("vr", [P, GROUP, HV]); ktok = sb("ktok", [P, 2, H, P])
        Pb = sb("Pb", [P, H, 64])
        S = sb("S", [P, HV]); Sd = sb("Sd", [P, HV])
        passing = sb("passing", [P, 2, HV]); ks, osq = passing[:, 0], passing[:, 1]
        R = sb("R", [P, HV]); W1s = sb("Wp", [P, HV])
        t2 = sb("t2", [P, HV]); O = sb("O", [P, HV]); O3 = sb("O3", [P, HV])
        ss = sb("ss", [P, H]); f1 = sb("f1", [P, H]); f2 = sb("f2", [P, H]); f3 = sb("f3", [P, H]); f4 = sb("f4", [P, H]); fo = sb("fo", [P, H])
        oT = sb("oT", [P, VC, P]); yb = sb("yb", [P, GROUP, 2, D]); xr = sb("xr", [P, GROUP, D])
        lane_n, lane_x = (vr[:, 2 * i:2 * i + 2].rearrange("p a (i j) -> p (a i) j", j=32) for i in range(2))
        lane_t = R[:, 0:256]
        blocks = sq[:, 0].rearrange("p h (a j) -> p (h a) j", j=32)
        oldest = passing

        pA = ctx.enter_context(nc.psum_tensor("att_psA", [P, 2, 512], F32))
        pB = ctx.enter_context(nc.psum_tensor("att_psB", [P, 2, 512], F32))
        pC = ctx.enter_context(nc.psum_tensor("att_psC", [P, 2, 512], F32))
        pD = ctx.enter_context(nc.psum_tensor("att_psD", [P, 512], F32))
        pE = ctx.enter_context(nc.psum_tensor("att_psE", [P, 512], F32))
        pair_bank = (pA, pC)

        names = {
            "tensor": "proj_ready gate_ready norms_mm dexp_ready kk_ready qk_ready vtr_ready ktok_ready p32_ready y32_ready "
                      "p64_ready y64_ready ks_ready s_read w_ready aw_ready sup_ready otr_ready wo_ready",
            "scalar": "tap3_done silu_done sq_ready old_ready placed gate_done dec_done ktok_done p32_done y32_done p64_done y64_done t2_done oT_done",
            "vector": "tap taps_done tails_done nk_done nq_done rn_done eps_done kk_used qk_used vr_done elim inv_done p32_done_v "
                      "y32_done_v ks_scaled r_done w1_done o_sum s_kept s_done ss_done o2_done o3_done "
                      "acc1_done acc2_done fin_done",
            "gpsimd": "bg_done mst_done wt_done sidx_done tk_done corr_step corr_done qg_ready old_added gatew_done knorm_done "
                      "qscale_done sd_done osq_done f_step f5_done f_done",
        }
        s = {n: ctx.enter_context(nc.semaphore("att_" + n)) for group in names.values() for n in group.split()}
        consts = ctx.enter_context(nc.semaphore("att_consts"))
        xt_loaded, xr_loaded, y_loaded = (ctx.enter_context(nc.semaphore("att_" + n)) for n in ("xt_loaded", "xr_loaded", "y_loaded"))
        out_stored = [ctx.enter_context(nc.semaphore(f"att_out_stored{i}")) for i in range(2)]
        block = ctx.enter_context(nc.Block())
        passed = ctx.enter_context(nc.semaphore("att_passed"))
        NCONST = 10

        def credits(eng, which):
            for n in names[which].split():
                eng.sem_inc(s[n], CREDIT)

        def wait(eng, name, count):
            eng.wait_ge(s[name], count + CREDIT)

        def apart(eng):
            eng.sem_inc(passed, 1)

        ORDER = list(range(H // 2, H)) + list(range(H // 2)) + list(range(H, PAIRS))
        SHARED = list(range(7, PAIRS))
        NS = len(SHARED)
        tap_ops = [2 * (TAPS - 2) if j in SHARED else 2 * (TAPS - 1) for j in range(PAIRS)]

        def conv_dst(j):
            k = ORDER[j]
            if k < H // 2:
                return qk[:, 2 * k:2 * k + 2, 0, :]
            if k < H:
                return qk[:, 2 * k - H:2 * k - H + 2, 1, :]
            return vc[:, 2 * (k - H):2 * (k - H) + 2, :]

        def heads(ap):
            return ap.rearrange("p (h v) -> p h v", h=H)

        def turned(c):
            return pC[:, 1, :] if c + 1 < GROUP else pD[:, :]

        xt_v = xnT_d
        xr_v = xf.rearrange("(g a p) d -> g p a d", a=GROUP, p=P)
        of_v = of.rearrange("(t p) d -> t p d", p=P)

        @block.sync
        def _(sp):
            def load_columns(m):
                wait(sp, "proj_ready", PAIRS * m)
                wait(sp, "gate_ready", GROUP * m)
                sp.dma_start(xt[:, :, :], xt_v[:, :, bass.ds(m * GT, GT)]).then_inc(xt_loaded, 16)

            def load_rows(m):
                wait(sp, "fin_done", GROUP * m)
                for q in out_stored:
                    sp.wait_ge(q, 16 * 2 * m + 16)
                sp.dma_start(xr[:, :, :], xr_v[bass.ds(m, 1)].rearrange("o p a d -> (o p) a d")).then_inc(xr_loaded, 16)

            def store(m, c):
                wait(sp, "fin_done", GROUP * m + c + 1)
                sp.dma_start(of_v[bass.ds(GROUP * m + c, 1)].rearrange("o p d -> (o p) d"), xr[:, c, :]).then_inc(out_stored[c % 2], 16)

            load_columns(0)
            with sp.Fori(0, NG - 1) as m:
                load_rows(m)
                load_columns(m + 1)
                for c in range(GROUP):
                    store(m, c)
            load_rows(NG - 1)
            for c in range(GROUP):
                store(NG - 1, c)
            for q in out_stored:
                sp.wait_ge(q, 16 * 2 * NG + 16)

        @block.tensor
        def _(pe):
            credits(pe, "tensor")
            pe.wait_ge(params, 16 * NPARAM)
            pe.wait_ge(consts, NCONST)
            MM, TR = nc.tensor.matmul, nc.tensor.transpose

            def project(m, j):
                wait(pe, "taps_done", PAIRS * m + j - 1)
                if j == 0:
                    pe.wait_ge(xt_loaded, 16 * m + 16)
                    wait(pe, "ktok_done", 2 * GROUP * m)
                if j == 1:
                    wait(pe, "w1_done", GROUP * m)
                    wait(pe, "t2_done", GROUP * m)
                    wait(pe, "oT_done", GROUP * m - 1)
                k = ORDER[j]
                for h in range(2):
                    for c in range(DC):
                        last = MM(pair_bank[j % 2][:, h, :], wqkv[:, c, (2 * k + h) * P:(2 * k + h + 1) * P], xt[:, c, :], start=(c == 0), stop=(c == DC - 1))
                last.then_inc(s["proj_ready"], 1)

            def project_gate(m, c):
                wait(pe, "oT_done", GROUP * m)
                wait(pe, "gate_done", GROUP * m + c)
                for d in range(DC):
                    last = MM(pD[:, :], xt[:, d, c * P:(c + 1) * P], wg[:, d, :], start=(d == 0), stop=(d == DC - 1))
                last.then_inc(s["gate_ready"], 1)

            def norms(m, j):
                wait(pe, "sq_ready", QKP * m + j + 1)
                wait(pe, "fin_done", GROUP * m)
                for h in range(2):
                    for c in range(GROUP):
                        at = c * 2 * H + 2 * ORDER[j] + h
                        last = MM(pE[:, at:at + 1], sq[:, j % 2, h, c * P:(c + 1) * P], ones[:, 0:1], start=True, stop=True)
                last.then_inc(s["norms_mm"], 1)

            def decays(m, c):
                n = GROUP * m + c
                for g in range(2):
                    wait(pe, "qg_ready", n + 1)
                    wait(pe, "dec_done", 2 * n + g - 1)
                    wait(pe, "y64_done", GROUP * m)
                    MM(pB[:, g, :], tri_gt[:, :], qg[:, c % 2, 4 * g:4 * g + 4, :], start=True, stop=False)
                    MM(pB[:, g, :], identb[:, :], negb[:, :, :], start=False, stop=True).then_inc(s["dexp_ready"], 1)

            def keys(m, c):
                n = GROUP * m + c
                for g in range(2):
                    wait(pe, "silu_done", PAIRS * m + H // 2)
                    wait(pe, "y64_done", GROUP * m)
                    wait(pe, "dec_done", 2 * GROUP * (m + 1))
                    wait(pe, "kk_used", 2 * n + g - 1)
                    for h in range(4):
                        kc = qk[:, 4 * g + h, 1, c * P:(c + 1) * P]
                        last = MM(pB[:, g, h * P:(h + 1) * P], kc, kc, start=True, stop=True)
                    last.then_inc(s["kk_ready"], 1)

            def queries(m, c):
                n = GROUP * m + c
                wait(pe, "silu_done", PAIRS * m + H)
                wait(pe, "taps_done", PAIRS * m + PAIRS - (1 if c == 0 else 0))
                wait(pe, "qk_used", n - 1)
                for h in range(H):
                    last = MM(pair_bank[c % 2][:, h // 4, (h % 4) * P:(h % 4 + 1) * P], qk[:, h, 1, c * P:(c + 1) * P], qk[:, h, 0, c * P:(c + 1) * P],
                              start=True, stop=True)
                last.then_inc(s["qk_ready"], 1)

            def values(m, c):
                n = GROUP * m + c
                wait(pe, "silu_done", PAIRS * m + PAIRS)
                wait(pe, "gate_done", GROUP * m + GROUP)
                wait(pe, "nq_done", m + 1)
                wait(pe, "vr_done", n - 1)
                for j in range(VC):
                    last = TR((pD, pE)[c % 2][:, j * P:(j + 1) * P], vc[:, j, c * P:(c + 1) * P], ident[:, :])
                last.then_inc(s["vtr_ready"], 1)

            def tokens(m, c):
                n = GROUP * m + c
                wait(pe, "ktok_done", 2 * n)
                wait(pe, "qk_used", GROUP * (m + 1))
                for g in range(2):
                    for h in range(4):
                        last = TR(pA[:, g, h * P:(h + 1) * P], qk[:, 4 * g + h, 1, c * P:(c + 1) * P], ident[:, :])
                    last.then_inc(s["ktok_ready"], 1)

            def p32(m, c):
                n = GROUP * m + c
                wait(pe, "inv_done", m + 1)
                wait(pe, "y64_done", n)
                apart(pe)
                for q in range(2):
                    a, b = 64 * q, 64 * q + 32
                    for h in range(H):
                        u = c * H + h
                        last = MM(pB[b:b + 32, q, 32 * h:32 * h + 32], Y[a:a + 32, u, b:b + 32], X[a:a + 32, u, 0:32], start=True, stop=True)
                last.then_inc(s["p32_ready"], 1)

            def y32(m, c):
                n = GROUP * m + c
                wait(pe, "p32_done", n + 1)
                wait(pe, "p32_done_v", n + 1)
                apart(pe)
                for q in range(2):
                    a, b = 64 * q, 64 * q + 32
                    for h in range(H):
                        u = c * H + h
                        last = MM(pB[a:a + 32, q, 256 + 32 * h:288 + 32 * h], Pb[b:b + 32, h, 0:32], blocks[b:b + 32, u, :], start=True, stop=True)
                for h in range(H):
                    last = MM(pB[32:64, 0, 256 + 32 * h:288 + 32 * h], blocks[32:64, c * H + h, :], Pb[32:64, h, 0:32], start=True, stop=True)
                last.then_inc(s["y32_ready"], 1)

            def p64(m, c):
                n = GROUP * m + c
                wait(pe, "y32_done", n + 1)
                wait(pe, "y32_done_v", n + 1)
                apart(pe)
                for h in range(H):
                    last = MM(pB[64:128, 0, 64 * h:64 * h + 64], Y[0:64, c * H + h, 64:128], X[0:64, c * H + h, :], start=True, stop=True)
                last.then_inc(s["p64_ready"], 1)

            def y64(m, c):
                n = GROUP * m + c
                wait(pe, "p64_done", n + 1)
                apart(pe)
                for h in range(H):
                    last = MM(pB[0:64, 1, 64 * h:64 * h + 64], Pb[64:128, h, :], Y[64:128, c * H + h, 64:128], start=True, stop=True)
                last.then_inc(s["y64_ready"], 1)

            def read(m, c):
                n = GROUP * m + c
                if c == 0:
                    wait(pe, "qk_used", GROUP * (m + 1))
                    wait(pe, "s_kept", m + 1)
                wait(pe, "s_done", n)
                wait(pe, "w1_done", n)
                for h in range(H):
                    last = MM(pC[:, 0, DV * h:DV * h + DV], qk[:, h, 1, c * P:(c + 1) * P], S[:, DV * h:DV * h + DV], start=True, stop=True)
                last.then_inc(s["ks_ready"], 1)
                wait(pe, "oT_done", n - 1)
                for h in range(H):
                    last = MM(pC[:, 1, DV * h:DV * h + DV], qk[:, h, 0, c * P:(c + 1) * P], S[:, DV * h:DV * h + DV], start=True, stop=True)
                last.then_inc(s["s_read"], 1)

            def solve(m, c):
                n = GROUP * m + c
                wait(pe, "r_done", n + 1)
                wait(pe, "y64_done", n + 1)
                for h in range(H):
                    last = MM(pC[:, 0, DV * h:DV * h + DV], Y[:, c * H + h, :], R[:, DV * h:DV * h + DV], start=True, stop=True)
                last.then_inc(s["w_ready"], 1)

            def apply(m, c):
                n = GROUP * m + c
                wait(pe, "w1_done", n + 1)
                wait(pe, "ktok_done", 2 * n + 2)
                wait(pe, "fin_done", n - 1 if c else n)
                wait(pe, "vr_done", GROUP * (m + 1))
                for h in range(H):
                    last = MM(pE[:, DV * h:DV * h + DV], ktok[:, c % 2, h, :], W1s[:, DV * h:DV * h + DV], start=True, stop=True)
                last.then_inc(s["sup_ready"], 1)
                wait(pe, "o_sum", n)
                for h in range(H):
                    last = MM(pD[:, DV * h:DV * h + DV], AT[:, c * H + h, :], W1s[:, DV * h:DV * h + DV], start=True, stop=True)
                last.then_inc(s["aw_ready"], 1)

            def turn(m, c):
                n = GROUP * m + c
                wait(pe, "o3_done", n + 1)
                if c + 1 < GROUP:
                    wait(pe, "t2_done", n + 2)
                else:
                    wait(pe, "o_sum", n + 1)
                for j in range(VC):
                    last = TR(turned(c)[:, j * P:(j + 1) * P], O3[:, j * P:(j + 1) * P], ident[:, :])
                last.then_inc(s["otr_ready"], 1)

            def out(m, c):
                n = GROUP * m + c
                wait(pe, "oT_done", n + 1)
                wait(pe, "s_done", n + (2 if c + 1 < GROUP else 1))
                wait(pe, "fin_done", n)
                for j in range(VC):
                    last = MM(pE[:, 0:D], oT[:, j, :], wo[:, j, :], start=(j == 0), stop=(j == VC - 1))
                last.then_inc(s["wo_ready"], 1)

            def start(m):
                project(m, 0)
                project(m, 1)
                decays(m, 2)

            def macro_tile(m, following):
                decays(m, 3)
                project(m, 3)
                project(m, 4)
                project(m, 5)
                norms(m, 0)
                norms(m, 1)
                norms(m, 2)
                norms(m, 3)
                keys(m, 0)
                project(m, 6)
                keys(m, 1)
                keys(m, 2)
                keys(m, 3)
                project_gate(m, 0)
                norms(m, 4)
                project(m, 7)
                project_gate(m, 1)
                norms(m, 5)
                project(m, 8)
                project_gate(m, 2)
                norms(m, 6)
                project(m, 9)
                project_gate(m, 3)
                norms(m, 7)
                queries(m, 0)
                queries(m, 1)
                values(m, 0)
                values(m, 1)
                p32(m, 0)
                queries(m, 2)
                y32(m, 0)
                queries(m, 3)
                p64(m, 0)
                tokens(m, 0)
                y64(m, 0)
                values(m, 2)
                values(m, 3)
                for c in range(GROUP):
                    more = c + 1 < GROUP
                    read(m, c)
                    if more:
                        p32(m, c + 1)
                    elif following is not None:
                        decays(following, 0)
                    solve(m, c)
                    if more:
                        y32(m, c + 1)
                    elif following is not None:
                        decays(following, 1)
                    apply(m, c)
                    if more:
                        p64(m, c + 1)
                    if c:
                        turn(m, c - 1)
                    if more:
                        tokens(m, c + 1)
                        y64(m, c + 1)
                    if c:
                        out(m, c - 1)
                if following is not None:
                    start(following)
                turn(m, GROUP - 1)
                if following is not None:
                    project(following, 2)
                out(m, GROUP - 1)

            decays(0, 0)
            decays(0, 1)
            start(0)
            project(0, 2)
            with pe.Fori(0, NG - 1) as m:
                macro_tile(m, m + 1)
            macro_tile(NG - 1, None)

        @block.scalar
        def _(act):
            credits(act, "scalar")
            for q in out_stored:
                act.sem_inc(q, 16)
            act.wait_ge(params, 16 * NPARAM)
            A = nc.scalar.activation

            def tap3(m, j):
                wait(act, "proj_ready", PAIRS * m + j + 1)
                if j == 0:
                    wait(act, "s_read", GROUP * m)
                    wait(act, "ktok_ready", 2 * GROUP * m)
                    wait(act, "vtr_ready", GROUP * m)
                dst = conv_dst(j)
                for h in range(2):
                    last = A(dst[:, h, :], pair_bank[j % 2][:, h, :], ACT.Copy, scale=cw[:, 2 * ORDER[j] + h, TAPS - 1:TAPS])
                last.then_inc(s["tap3_done"], 1)

            def oldest_tap(m, j):
                wait(act, "old_added", NS * m + SHARED.index(j))
                wait(act, "r_done", GROUP * m)
                wait(act, "ss_done", GROUP * m)
                for h in range(2):
                    last = A(oldest[:, h, 0:GT - 3], pair_bank[j % 2][:, h, 0:GT - 3], ACT.Copy, scale=cw[:, 2 * ORDER[j] + h, 0:1])
                last.then_inc(s["old_ready"], 1)

            def place(m, c):
                wait(act, "inv_done", m + 1)
                u = slice(c * H, (c + 1) * H)
                for a in range(NB):
                    r = slice(32 * a, 32 * a + 32)
                    A(Y[r, u, r], blocks[r, u, :], ACT.Copy)
                A(X[32:64, u, 32:64], X[32:64, u, 0:32], ACT.Copy).then_inc(s["placed"], 1)

            def silu(m, j):
                wait(act, "taps_done", PAIRS * m + j + 1)
                if j in SHARED:
                    wait(act, "old_added", NS * m + SHARED.index(j) + 1)
                A(conv_dst(j), conv_dst(j), ACT.Silu).then_inc(s["silu_done"], 1)

            def squares(m, j):
                wait(act, "silu_done", PAIRS * m + j + 1)
                wait(act, "norms_mm", QKP * m + j - 1)
                wait(act, "y32_ready", GROUP * m)
                wait(act, "placed", GROUP * m)
                A(sq[:, j % 2], conv_dst(j), ACT.Square).then_inc(s["sq_ready"], 1)

            def silu_gate(m, c):
                wait(act, "gate_ready", GROUP * m + c + 1)
                wait(act, "o3_done", GROUP * m)
                A(gate[:, c, :], pD[:, :], ACT.Silu).then_inc(s["gate_done"], 1)

            def decays(m, c):
                n = GROUP * m + c
                for g in range(2):
                    wait(act, "dexp_ready", 2 * n + g + 1)
                    wait(act, "aw_ready", GROUP * (m - 1) + c + 1)
                    A(AT[:, c * H + 4 * g:c * H + 4 * g + 4, :], pB[:, g, :].rearrange("p (h n) -> p h n", h=4), ACT.Exp).then_inc(s["dec_done"], 1)

            def tokens(m, c):
                n = GROUP * m + c
                wait(act, "sup_ready", n - 1)
                wait(act, "mst_done", m + 1)
                for g in range(2):
                    wait(act, "ktok_ready", 2 * n + g + 1)
                    for h in range(4 * g, 4 * g + 4):
                        last = A(ktok[:, c % 2, h, :], pA[:, g, (h % 4) * P:(h % 4 + 1) * P], ACT.Copy, scale=mst[:, c, 3, h:h + 1])
                    last.then_inc(s["ktok_done"], 1)

            def p32(m, c):
                n = GROUP * m + c
                wait(act, "p32_ready", n + 1)
                wait(act, "y64_ready", n)
                A(Pb[32:64, :, 0:32], pB[32:64, 0, 0:256].rearrange("p (h n) -> p h n", h=H), ACT.Copy).then_inc(s["p32_done"], 1)

            def y32(m, c):
                n = GROUP * m + c
                wait(act, "y32_ready", n + 1)
                wait(act, "placed", n + 1)
                A(Y[0:32, c * H:(c + 1) * H, 32:64], pB[0:32, 0, 256:512].rearrange("p (h n) -> p h n", h=H), ACT.Copy, scale=-1.0)
                A(X[32:64, c * H:(c + 1) * H, 0:32], pB[32:64, 0, 256:512].rearrange("p (h n) -> p h n", h=H), ACT.Copy, scale=-1.0).then_inc(s["y32_done"], 1)

            def p64(m, c):
                n = GROUP * m + c
                wait(act, "p64_ready", n + 1)
                A(Pb[64:128, :, :], pB[64:128, 0, :].rearrange("p (h n) -> p h n", h=H), ACT.Copy).then_inc(s["p64_done"], 1)

            def y64(m, c):
                n = GROUP * m + c
                wait(act, "y64_ready", n + 1)
                A(Y[0:64, c * H:(c + 1) * H, 64:128], pB[0:64, 1, :].rearrange("p (h n) -> p h n", h=H), ACT.Copy, scale=-1.0).then_inc(s["y64_done"], 1)

            def read(m, c):
                n = GROUP * m + c
                wait(act, "s_read", n + 1)
                wait(act, "o_sum", n)
                for h in range(H):
                    last = A(t2[:, DV * h:DV * h + DV], pC[:, 1, DV * h:DV * h + DV], ACT.Copy, scale=mst[:, c, 2, h:h + 1])
                last.then_inc(s["t2_done"], 1)

            def turn(m, c):
                n = GROUP * m + c
                wait(act, "otr_ready", n + 1)
                wait(act, "wo_ready", n)
                A(oT[:, :, :], turned(c).rearrange("p (j n) -> p j n", j=VC), ACT.Copy).then_inc(s["oT_done"], 1)

            def start(m):
                tap3(m, 0)
                tap3(m, 1)
                decays(m, 2)

            def macro_tile(m, following):
                tap3(m, 2)
                decays(m, 3)
                tap3(m, 3)
                silu(m, 0)
                squares(m, 0)
                tap3(m, 4)
                silu(m, 1)
                squares(m, 1)
                tap3(m, 5)
                silu(m, 2)
                squares(m, 2)
                silu(m, 3)
                squares(m, 3)
                tap3(m, 6)
                silu(m, 4)
                squares(m, 4)
                silu(m, 5)
                squares(m, 5)
                silu_gate(m, 0)
                for j in range(7, PAIRS):
                    tap3(m, j)
                    if j in SHARED:
                        oldest_tap(m, j)
                    silu(m, j - 1)
                    if j - 1 < QKP:
                        squares(m, j - 1)
                    silu_gate(m, j - 6)
                silu(m, PAIRS - 1)
                place(m, 0)
                p32(m, 0)
                y32(m, 0)
                p64(m, 0)
                tokens(m, 0)
                y64(m, 0)
                for c in range(GROUP):
                    more = c + 1 < GROUP
                    read(m, c)
                    if more:
                        place(m, c + 1)
                        p32(m, c + 1)
                        y32(m, c + 1)
                        p64(m, c + 1)
                    elif following is not None:
                        decays(following, 0)
                        decays(following, 1)
                    if c:
                        turn(m, c - 1)
                    if more:
                        tokens(m, c + 1)
                        y64(m, c + 1)
                if following is not None:
                    start(following)
                turn(m, GROUP - 1)

            decays(0, 0)
            decays(0, 1)
            start(0)
            with act.Fori(0, NG - 1) as m:
                macro_tile(m, m + 1)
            macro_tile(NG - 1, None)

        @block.vector
        def _(dve):
            credits(dve, "vector")
            dve.wait_ge(params, 16 * NPARAM)
            dve.wait_ge(consts, NCONST)
            V = nc.vector

            def taps(m, j):
                i = sum(tap_ops) * m + sum(tap_ops[:j])
                k = ORDER[j]
                wait(dve, "tap3_done", PAIRS * m + j + 1)
                if j in SHARED:
                    wait(dve, "old_ready", NS * m + SHARED.index(j) + 1)
                dst, src = conv_dst(j), pair_bank[j % 2]
                for d in range(1, 1 + tap_ops[j] // 2):
                    for h in range(2):
                        if d > 1:
                            wait(dve, "tap", i + 2 * (d - 2) + h + 1)
                        V.scalar_tensor_tensor(out=dst[:, h, d:GT], in0=src[:, h, 0:GT - d], scalar=cw[:, 2 * k + h, TAPS - 1 - d:TAPS - d],
                                               in1=dst[:, h, d:GT], op0=ALU.mult, op1=ALU.add).then_inc(s["tap"], 1)
                        yield
                wait(dve, "corr_done", m + 1)
                V.tensor_copy(tails[:, 2 * k:2 * k + 2, :], src[:, :, GT - 3:GT]).then_inc(s["tails_done"], 1)
                wait(dve, "tap", i + tap_ops[j])
                V.tensor_tensor(dst[:, :, 0:3], dst[:, :, 0:3], corr[:, 2 * k:2 * k + 2, :], op=ALU.add).then_inc(s["taps_done"], 1)
                yield

            def key_stats(m):
                wait(dve, "norms_mm", QKP * m + H // 2)
                wait(dve, "knorm_done", m)
                V.tensor_scalar(nkq[:, :, 1, :], pE[:, 0:GROUP * 2 * H].rearrange("p (c a h) -> p c a h", c=GROUP, a=2)[:, :, 1], L2_EPS, None, ALU.add).then_inc(s["nk_done"], 1)
                wait(dve, "nk_done", m + 1)
                V.reciprocal(rn[:, :, :], nkq[:, :, 1, :]).then_inc(s["rn_done"], 1)
                wait(dve, "s_done", GROUP * m)
                V.tensor_scalar(S[:, :], S[:, :], goes_on[:, bass.ds(m, 1)], None, ALU.mult).then_inc(s["s_kept"], 1)
                wait(dve, "rn_done", m + 1)
                wait(dve, "bg_done", m + 1)
                wait(dve, "w1_done", GROUP * m)
                V.tensor_tensor(eps[:, :, :], rn[:, :, :], bg[:, :, 0, :], op=ALU.mult).then_inc(s["eps_done"], 1)

            def query_stats(m):
                wait(dve, "norms_mm", QKP * m + QKP)
                wait(dve, "qscale_done", m)
                V.tensor_scalar(nkq[:, :, 0, :], pE[:, 0:GROUP * 2 * H].rearrange("p (c a h) -> p c a h", c=GROUP, a=2)[:, :, 0], L2_EPS, None, ALU.add).then_inc(s["nq_done"], 1)

            def queries(m, c):
                n = GROUP * m + c
                wait(dve, "qk_ready", n + 1)
                wait(dve, "kk_used", 2 * GROUP * (m + 1))
                at = AT[:, c * H:(c + 1) * H, :]
                V.tensor_tensor(at, pair_bank[c % 2][:, :, :].rearrange("p g (h n) -> p (g h) n", n=P), at, op=ALU.mult).then_inc(s["qk_used"], 1)

            def values(m, c):
                n = GROUP * m + c
                wait(dve, "vtr_ready", n + 1)
                wait(dve, "knorm_done", m + 1)
                wait(dve, "elim", (8 + 2 * 30) * (m + 1))
                V.tensor_tensor(heads(vr[:, c, :]), heads((pD, pE)[c % 2][:, :]), bc(knorm[:, c, :], 2, DV), op=ALU.mult).then_inc(s["vr_done"], 1)

            def keys(m, c):
                n = GROUP * m + c
                wait(dve, "eps_done", m + 1)
                wait(dve, "w_ready", GROUP * m)
                for g in range(2):
                    wait(dve, "kk_ready", 2 * n + g + 1)
                    for h in range(4 * g, 4 * g + 4):
                        u = c * H + h
                        last = V.scalar_tensor_tensor(out=Y[:, u, :], in0=pB[:, g, (h % 4) * P:(h % 4 + 1) * P], scalar=eps[:, c, h:h + 1],
                                                      in1=AT[:, u, :], op0=ALU.mult, op1=ALU.mult)
                    last.then_inc(s["kk_used"], 1)

            def invert(m, others):
                step = [0]
                per = 8 + 2 * 30

                def link(ins, hold=True):
                    step[0] += 1
                    ins.then_inc(s["elim"], 1)
                    if hold:
                        if step[0] % 2:
                            next(others, None)
                        wait(dve, "elim", per * m + step[0])

                wait(dve, "kk_used", 2 * GROUP * (m + 1))
                wait(dve, "r_done", GROUP * m)
                for a in range(NB):
                    r = slice(32 * a, 32 * a + 32)
                    link(V.transpose(lane_n[r, :, :], Y[r, :, r].rearrange("p u i -> p i u")), hold=(a == NB - 1))
                link(V.tensor_scalar(lane_x[:, :, :], lane_n[:, :, :], -1.0, None, ALU.mult))
                link(V.memset(lane_x[:, :, :].rearrange("p i j -> p (i j)")[:, 0:1024:33], 1.0))
                for j in range(1, 31):
                    tmp = lane_t[:, 0:(31 - j) * j].rearrange("p (i j) -> p i j", j=j)
                    link(V.tensor_tensor(tmp, lane_n[:, j + 1:32, j:j + 1].to_broadcast([P, 31 - j, j]),
                                         lane_x[:, j:j + 1, 0:j].to_broadcast([P, 31 - j, j]), op=ALU.mult))
                    link(V.tensor_tensor(lane_x[:, j + 1:32, 0:j], lane_x[:, j + 1:32, 0:j], tmp, op=ALU.subtract))
                for _ in others:
                    pass
                link(V.transpose(X[:, :, 0:32].rearrange("p u j -> p j u"), lane_x[:, :, :].rearrange("p i j -> p j i")), hold=False)
                V.transpose(blocks[:, :, :].rearrange("p u i -> p i u"), lane_x[:, :, :]).then_inc(s["elim"], 1)
                assert step[0] + 1 == per
                wait(dve, "p64_ready", GROUP * m)
                V.memset(X[0:32, :, 32:64], 0.0).then_inc(s["inv_done"], 1)

            def p32(m, c):
                n = GROUP * m + c
                wait(dve, "p32_ready", n + 1)
                V.tensor_copy(Pb[96:128, :, 0:32], pB[96:128, 1, 0:256].rearrange("p (h n) -> p h n", h=H)).then_inc(s["p32_done_v"], 1)

            def y32(m, c):
                n = GROUP * m + c
                wait(dve, "y32_ready", n + 1)
                V.tensor_scalar(Y[64:96, c * H:(c + 1) * H, 96:128], pB[64:96, 1, 256:512].rearrange("p (h n) -> p h n", h=H), -1.0, None, ALU.mult).then_inc(s["y32_done_v"], 1)

            def read(m, c):
                n = GROUP * m + c
                wait(dve, "ks_ready", n + 1)
                wait(dve, "old_added", NS * (m + 1))
                wait(dve, "mst_done", m + 1)
                wait(dve, "r_done", n)
                V.tensor_tensor(heads(ks), heads(pC[:, 0, :]), bc(mst[:, c, 2, :], 2, DV), op=ALU.mult).then_inc(s["ks_scaled"], 1)
                wait(dve, "ks_scaled", n + 1)
                wait(dve, "vr_done", n + 1)
                wait(dve, "w_ready", n)
                V.tensor_tensor(R[:, :], vr[:, c, :], ks, op=ALU.subtract).then_inc(s["r_done"], 1)

            def solve(m, c):
                n = GROUP * m + c
                wait(dve, "w_ready", n + 1)
                wait(dve, "aw_ready", n)
                V.tensor_tensor(heads(W1s[:, :]), heads(pC[:, 0, :]), bc(eps[:, c, :], 2, DV), op=ALU.mult).then_inc(s["w1_done"], 1)

            def apply(m, c):
                n = GROUP * m + c
                wait(dve, "sup_ready", n + 1)
                wait(dve, "sd_done", n + 1)
                wait(dve, "s_read", n + 1)
                V.tensor_tensor(S[:, :], pE[:, :], Sd[:, :], op=ALU.add).then_inc(s["s_done"], 1)
                wait(dve, "aw_ready", n + 1)
                wait(dve, "t2_done", n + 1)
                wait(dve, "o3_done", n)
                V.tensor_tensor(O[:, :], pD[:, :], t2[:, :], op=ALU.add).then_inc(s["o_sum"], 1)

            def expert_rows(m, c):
                n = GROUP * m + c
                if c == 0:
                    dve.wait_ge(y_loaded, 2 * GROUP * 16 * (m + 1))
                    dve.wait_ge(xr_loaded, 16 * (m + 1))
                    wait(dve, "wt_done", m + 1)
                V.scalar_tensor_tensor(out=xr[:, c, :], in0=yb[:, c, 0, :], scalar=wt[:, c, 0:1], in1=xr[:, c, :], op0=ALU.mult, op1=ALU.add).then_inc(s["acc1_done"], 1)

            def expert_rows_2(m, c):
                n = GROUP * m + c
                wait(dve, "acc1_done", n + 1)
                V.scalar_tensor_tensor(out=xr[:, c, :], in0=yb[:, c, 1, :], scalar=wt[:, c, 1:2], in1=xr[:, c, :], op0=ALU.mult, op1=ALU.add).then_inc(s["acc2_done"], 1)

            def squares_sum(m, c):
                n = GROUP * m + c
                wait(dve, "osq_done", n + 1)
                wait(dve, "f_done", n)
                V.tensor_reduce(ss[:, :], heads(osq), op=ALU.add, axis=AX_X).then_inc(s["ss_done"], 1)

            def scale_out(m, c):
                n = GROUP * m + c
                wait(dve, "f_done", n + 1)
                V.tensor_tensor(heads(O[:, :]), heads(O[:, :]), bc(fo[:, :], 2, DV), op=ALU.mult).then_inc(s["o2_done"], 1)
                wait(dve, "o2_done", n + 1)
                wait(dve, "gatew_done", n + 1)
                wait(dve, "otr_ready", n)
                V.tensor_tensor(O3[:, :], O[:, :], gate[:, c, :], op=ALU.mult).then_inc(s["o3_done"], 1)

            def out(m, c):
                n = GROUP * m + c
                wait(dve, "acc2_done", n + 1)
                wait(dve, "wo_ready", n + 1)
                V.tensor_tensor(xr[:, c, :], pE[:, 0:D], xr[:, c, :], op=ALU.add).then_inc(s["fin_done"], 1)

            def late(m):
                for j in range(6, PAIRS):
                    yield from taps(m, j)
                    if j in SHARED:
                        yield
                        yield
                query_stats(m)
                yield
                for c in range(2):
                    queries(m, c)
                    yield

            def start(m):
                for _ in taps(m, 0):
                    pass

            def start_2(m):
                for _ in taps(m, 1):
                    pass

            def macro_tile(m, following):
                for j in range(2, 6):
                    for _ in taps(m, j):
                        pass
                key_stats(m)
                for c in range(GROUP):
                    keys(m, c)
                invert(m, late(m))
                values(m, 0)
                values(m, 1)
                p32(m, 0)
                queries(m, 2)
                y32(m, 0)
                queries(m, 3)
                values(m, 2)
                values(m, 3)
                for c in range(GROUP):
                    more = c + 1 < GROUP
                    read(m, c)
                    if c >= 2:
                        out(m, c - 2)
                    if more:
                        p32(m, c + 1)
                    solve(m, c)
                    expert_rows(m, c)
                    if more:
                        y32(m, c + 1)
                    expert_rows_2(m, c)
                    if c:
                        scale_out(m, c - 1)
                    apply(m, c)
                    squares_sum(m, c)
                out(m, GROUP - 2)
                if following is not None:
                    start(following)
                scale_out(m, GROUP - 1)
                if following is not None:
                    start_2(following)
                out(m, GROUP - 1)

            start(0)
            start_2(0)
            with dve.Fori(0, NG - 1) as m:
                macro_tile(m, m + 1)
            macro_tile(NG - 1, None)

        @block.gpsimd
        def _(pool):
            credits(pool, "gpsimd")
            G = pool
            G.memset(identb[:, :], 0.0).then_inc(consts, 1)
            G.memset(negb[:, :, :], 0.0).then_inc(consts, 1)
            G.memset(half[:, :, :], 0.5).then_inc(consts, 1)
            G.memset(mhalf[:, :, :], -0.5).then_inc(consts, 1)
            G.memset(goes_on[:, :], 1.0).then_inc(consts, 1)
            G.memset(tails[:, :, :], 0.0).then_inc(consts, 1)
            G.memset(S[:, :], 0.0).then_inc(consts, 1)
            G.wait_ge(consts, 7)
            G.memset(goes_on[:, 0:NG:PER_BATCH], 0.0).then_inc(consts, 1)
            G.affine_select(out=identb[:, :], in_=identb[:, :], compare_op=ALU.not_equal, fill=1.0, base=0,
                            pattern=[[-1, P]], channel_multiplier=1).then_inc(consts, 1)
            G.affine_select(out=negb[:, :, :], in_=negb[:, :, :], compare_op=ALU.is_ge, fill=NEG, base=0,
                            pattern=[[0, GROUP], [1, P]], channel_multiplier=-1).then_inc(consts, 1)
            G.wait_ge(consts, NCONST)
            G.wait_ge(params, 16 * NPARAM)

            def early_stats(m):
                wait(G, "eps_done", m)
                wait(G, "qg_ready", GROUP * m)
                apart(G)
                G.tensor_copy(bg[:, :, :, :], keep["stat"][:, bass.ds(GROUP * m, GROUP), 0:2, :]).then_inc(s["bg_done"], 1)

            def scan_stats(m):
                wait(G, "ktok_done", 2 * GROUP * m)
                wait(G, "t2_done", GROUP * m)
                wait(G, "ks_scaled", GROUP * m)
                wait(G, "sd_done", GROUP * m)
                apart(G)
                G.tensor_copy(mst[:, :, :, :], keep["stat"][:, bass.ds(GROUP * m, GROUP), :, :]).then_inc(s["mst_done"], 1)

            def halo(m):
                wait(G, "tails_done", PAIRS * m)
                wait(G, "taps_done", PAIRS * m)
                G.tensor_tensor(tk[:, :, :], tails[:, :, :], bc(goes_on[:, bass.ds(m, 1)], 1, QKV).to_broadcast([P, QKV, 3]), op=ALU.mult).then_inc(s["tk_done"], 1)
                wait(G, "tk_done", m + 1)
                G.tensor_tensor(corr[:, :, 0:3], tk[:, :, 0:3], cw[:, :, 0:1].to_broadcast([P, QKV, 3]), op=ALU.mult).then_inc(s["corr_step"], 1)
                for d in (1, 2):
                    w = 3 - d
                    G.tensor_tensor(ctmp[:, :, 0:w], tk[:, :, d:3], cw[:, :, d:d + 1].to_broadcast([P, QKV, w]), op=ALU.mult).then_inc(s["corr_step"], 1)
                    wait(G, "corr_step", 4 * m + 2 * d)
                    last = G.tensor_tensor(corr[:, :, 0:w], corr[:, :, 0:w], ctmp[:, :, 0:w], op=ALU.add)
                    if d == 1:
                        last.then_inc(s["corr_step"], 1)
                        wait(G, "corr_step", 4 * m + 3)
                last.then_inc(s["corr_done"], 1)

            def gather(m):
                wait(G, "acc2_done", GROUP * m)
                apart(G)
                G.tensor_copy(wt[:, :, :], keep["wtop"][:, bass.ds(GROUP * m, GROUP), :]).then_inc(s["wt_done"], 1)
                G.tensor_copy(sidx[:, :, :], keep["slot"][:, bass.ds(GROUP * m, GROUP), :]).then_inc(s["sidx_done"], 1)
                wait(G, "sidx_done", m + 1)
                apart(G)
                for c in range(GROUP):
                    for k in range(2):
                        G.indirect_dma_start(yb[:, c, k, :], None, yg_d[:, :], bass.IndirectOffsetOnAxis(ap=sidx[:, c, k:k + 1], axis=0)).then_inc(y_loaded, 16)

            def weigh_gate(m, c):
                wait(G, "gate_done", GROUP * m + c + 1)
                G.tensor_tensor(heads(gate[:, c, :]), heads(gate[:, c, :]), bc(nw[:, :], 1, H), op=ALU.mult).then_inc(s["gatew_done"], 1)

            def decay_sums(m, c):
                n = GROUP * m + c
                wait(G, "bg_done", m + 1)
                wait(G, "dexp_ready", 2 * n - 2)
                G.tensor_tensor(qg[:, c % 2], bc(tri_le[:, :], 1, H), bc(bg[:, c, 1, :], 2, P), op=ALU.mult).then_inc(s["qg_ready"], 1)

            def add_oldest(m, j):
                wait(G, "old_ready", NS * m + SHARED.index(j) + 1)
                wait(G, "taps_done", PAIRS * m + j + 1)
                dst = conv_dst(j)[:, :, 3:GT]
                G.tensor_tensor(dst, dst, oldest[:, :, 0:GT - 3], op=ALU.add).then_inc(s["old_added"], 1)

            def key_powers(m):
                wait(G, "nk_done", m + 1)
                wait(G, "vr_done", GROUP * m)
                G.tensor_tensor(knorm[:, :, :], nkq[:, :, 1, :], half[:, :, :], op=ALU.pow).then_inc(s["knorm_done"], 1)

            def query_powers(m):
                wait(G, "nq_done", m + 1)
                G.tensor_tensor(qscale[:, :, :], nkq[:, :, 0, :], mhalf[:, :, :], op=ALU.pow).then_inc(s["qscale_done"], 1)

            def read(m, c):
                n = GROUP * m + c
                if c == 0:
                    wait(G, "s_kept", m + 1)
                wait(G, "s_done", n)
                wait(G, "mst_done", m + 1)
                G.tensor_tensor(heads(Sd[:, :]), heads(S[:, :]), bc(mst[:, c, 4, :], 2, DV), op=ALU.mult).then_inc(s["sd_done"], 1)

            def squares(m, c):
                n = GROUP * m + c
                wait(G, "o_sum", n + 1)
                wait(G, "old_added", NS * (m + 1))
                wait(G, "ss_done", n)
                G.tensor_tensor(osq, O[:, :], O[:, :], op=ALU.mult).then_inc(s["osq_done"], 1)

            def factor(m, c):
                n = GROUP * m + c
                wait(G, "ss_done", n + 1)
                wait(G, "qscale_done", m + 1)
                G.tensor_tensor(f1[:, :], ss[:, :], qscale[:, c, :], op=ALU.mult).then_inc(s["f_step"], 1)
                wait(G, "f_step", 4 * n + 1)
                G.tensor_tensor(f2[:, :], f1[:, :], qscale[:, c, :], op=ALU.mult).then_inc(s["f_step"], 1)
                wait(G, "f_step", 4 * n + 2)
                apart(G)
                G.tensor_scalar(f3[:, :], f2[:, :], 1.0 / (DK * DV), RMS_EPS, ALU.mult, ALU.add).then_inc(s["f_step"], 1)
                wait(G, "f_step", 4 * n + 3)
                G.tensor_tensor(f4[:, :], f3[:, :], mhalf[:, 0, :], op=ALU.pow).then_inc(s["f_step"], 1)
                wait(G, "f_step", 4 * n + 4)
                wait(G, "o2_done", n)
                apart(G)
                G.tensor_tensor(f1[:, :], f4[:, :], qscale[:, c, :], op=ALU.mult).then_inc(s["f5_done"], 1)
                wait(G, "f5_done", n + 1)
                apart(G)
                G.tensor_scalar(fo[:, :], f1[:, :], DK ** -0.5, None, ALU.mult).then_inc(s["f_done"], 1)

            def start(m):
                early_stats(m)
                decay_sums(m, 0)
                decay_sums(m, 1)
                halo(m)

            def macro_tile(m, following):
                decay_sums(m, 3)
                scan_stats(m)
                key_powers(m)
                gather(m)
                weigh_gate(m, 0)
                add_oldest(m, 7)
                weigh_gate(m, 1)
                add_oldest(m, 8)
                weigh_gate(m, 2)
                add_oldest(m, 9)
                weigh_gate(m, 3)
                query_powers(m)
                read(m, 0)
                for c in range(GROUP):
                    if c + 1 == GROUP and following is not None:
                        decay_sums(following, 2)
                    squares(m, c)
                    if c + 1 < GROUP:
                        read(m, c + 1)
                    factor(m, c)
                    if c == 1 and following is not None:
                        start(following)

            start(0)
            decay_sums(0, 2)
            with G.Fori(0, NG - 1) as m:
                macro_tile(m, m + 1)
            macro_tile(NG - 1, None)


_INS = ["L0_attn_x", "L0_attn_Wq", "L0_attn_Wk", "L0_attn_Wv", "L0_attn_conv_q", "L0_attn_conv_k", "L0_attn_conv_v",
        "L0_attn_Wb", "L0_attn_Wa", "L0_attn_A_log", "L0_attn_dt_bias", "L0_attn_Wg", "L0_attn_norm_w", "L0_attn_Wo",
        "L0_ffn_Wg", "L0_ffn_W1", "L0_ffn_b1", "L0_ffn_W2", "L0_ffn_b2"]


def kernel(**inputs):
    import numpy as _np
    import concourse.bacc as _bacc
    from concourse import mybir as _mybir
    from concourse.bass_utils import run_bass_kernel_spmd as _run

    nc = _bacc.Bacc("TRN2", target_bir_lowering=False, num_devices=1)
    arrays, args = {}, []
    for name in _INS:
        a = _np.ascontiguousarray(inputs[name])
        arrays[f"in_{name}_dram"] = a
        args.append(nc.dram_tensor(f"in_{name}_dram", a.shape, _mybir.dt.from_np(a.dtype), kind="ExternalInput").ap())
    out = nc.dram_tensor("out_dram", inputs["L0_attn_x"].shape, _mybir.dt.float32, kind="ExternalOutput").ap()
    build(nc, *args, out)
    r = _run(nc, [arrays], core_ids=[0])
    return r.results[0]["out_dram"]
```
